# Optimizing a Trainium2 kernel written in Bass

```python
import numpy as np
import jax
import jax.numpy as jnp

def _softmax(x, axis=-1):
    return jax.nn.softmax(x, axis=axis)

def _gelu(x):
    return jax.nn.gelu(x, approximate=True)

def _silu(x):
    return jax.nn.silu(x)

def _sigmoid(x):
    return jax.nn.sigmoid(x)

def _layernorm(x, axis=-1, eps=1e-05):
    m = jnp.mean(x, axis=axis, keepdims=True)
    v = jnp.var(x, axis=axis, keepdims=True)
    return (x - m) / jnp.sqrt(v + eps)

def _scatter_add(tgt, idx, src, axis=0):
    return tgt.at[idx].add(src)

def _segment_sum(src, seg, n):
    return jax.ops.segment_sum(src, seg, n)
kernel_name = 'mk_decoder_postln_d2_seqx_r4_175461'

def setup_inputs(seed: int=0):
    np.random.seed(seed)
    _w = jnp.asarray

    def _rec_inputs():
        import jax
        import jax.numpy as jnp
        _rk = jax.random.key(seed)
        x = 7.22e-05 + 1 * jax.random.normal(jax.random.fold_in(_rk, 1), (4, 512, 512), jnp.float32)
        _lenS = 512 - jax.random.randint(jax.random.fold_in(_rk, 7), (4,), 0, max(1, 512 // 4) + 1, jnp.int32)
        _lenS2 = 512 - jax.random.randint(jax.random.fold_in(_rk, 8), (4,), 0, max(1, 512 // 4) + 1, jnp.int32)
        _ctx_1024P = jax.random.normal(jax.random.fold_in(_rk, 11), (4, 16, 256), jnp.float32)
        _ctx_1024c = jax.random.dirichlet(jax.random.fold_in(_rk, 511), 0.3 * jnp.ones((16,), jnp.float32), (4, 512))
        _ctx_1024t = jnp.einsum('bsk,bkd->bsd', _ctx_1024c, _ctx_1024P)
        _ctx_1024t = _ctx_1024t * jax.lax.rsqrt(jnp.mean(jnp.square(_ctx_1024t)) + 1e-12) * 0.953939
        ctx_1024 = 2.81802e-05 + 1.00001 * (_ctx_1024t + 0.3 * jax.random.normal(jax.random.fold_in(_rk, 611), (4, 512, 256), jnp.float32))
        return (x, ctx_1024)
    x, ctx_1024 = _rec_inputs()

    def _L0_attn_setup():
        import jax, jax.numpy as jnp
        import numpy as np
        B, S, D = (2, 512, 512)
        N_HEADS, N_KV_HEADS = (16, 4)
        HEAD_DIM = D // N_HEADS

        def _apply_rope(xh, positions):
            Dh = xh.shape[-1]
            half = Dh // 2
            freqs = 1.0 / 10000.0 ** (jnp.arange(half, dtype=jnp.float32) / half)
            angles = positions[:, None].astype(jnp.float32) * freqs[None, :]
            cos, sin = (jnp.cos(angles), jnp.sin(angles))
            xp = xh.reshape(*xh.shape[:-1], half, 2)
            x0, x1 = (xp[..., 0], xp[..., 1])
            r0 = x0 * cos - x1 * sin
            r1 = x0 * sin + x1 * cos
            return jnp.stack([r0, r1], axis=-1).reshape(xh.shape)
        key = jax.random.key(seed)
        ks = jax.random.split(key, 5)
        x = jax.random.normal(ks[0], (B, S, D), dtype=jnp.float32)
        W_q = jax.random.normal(ks[1], (D, D), dtype=jnp.float32) * 0.02
        W_k = jax.random.normal(ks[2], (D, N_KV_HEADS * HEAD_DIM), dtype=jnp.float32) * 0.02
        W_v = jax.random.normal(ks[3], (D, N_KV_HEADS * HEAD_DIM), dtype=jnp.float32) * 0.02
        W_o = jax.random.normal(ks[4], (D, D), dtype=jnp.float32) * 0.02
        return {'x': x, 'W_q': W_q, 'W_k': W_k, 'W_v': W_v, 'W_o': W_o}
    _L0_attn_all = _L0_attn_setup()
    _L0_attn_in = {k: v for k, v in _L0_attn_all.items() if k in ('W_q', 'W_k', 'W_v', 'W_o')}
    del _L0_attn_all

    def _L0_xattn_setup():
        import jax, jax.numpy as jnp
        import numpy as np
        key = jax.random.key(seed)
        ks = jax.random.split(key, 6)
        B, L, N, C, D = (8, 128, 512, 256, 128)
        return {'teacher_logits': jax.random.normal(ks[0], (B, L, N), dtype=jnp.float32), 'teacher_features': jax.random.normal(ks[1], (B, N, C), dtype=jnp.float32), 'Wq': jax.random.normal(ks[2], (D, C), dtype=jnp.float32) * (1.0 / np.sqrt(C)), 'bq': jnp.zeros((D,), dtype=jnp.float32), 'Wk': jax.random.normal(ks[3], (D, C), dtype=jnp.float32) * (1.0 / np.sqrt(C)), 'bk': jnp.zeros((D,), dtype=jnp.float32)}
    _L0_xattn_all = _L0_xattn_setup()
    _L0_xattn_in = {k: v for k, v in _L0_xattn_all.items() if k in ('Wq', 'bq', 'Wk', 'bk')}
    del _L0_xattn_all

    def _L0_ffn_setup():
        import jax, jax.numpy as jnp
        import numpy as np
        LORA_ALPHA = 16.0
        TOP_K = 2
        key = jax.random.key(seed)
        k_x, k_w, k_g, k_a, k_b = jax.random.split(key, 5)
        B, S, H, O, E, R = (2, 512, 512, 512, 8, 16)
        x = jax.random.normal(k_x, (B, S, H), dtype=jnp.float32)
        weight = jax.random.normal(k_w, (O, H), dtype=jnp.float32)
        gate_w = jax.random.normal(k_g, (E, H), dtype=jnp.float32) * 0.02
        A_w = jax.random.normal(k_a, (E, R, H), dtype=jnp.float32) * (1.0 / np.sqrt(H))
        B_w = jax.random.normal(k_b, (E, O, R), dtype=jnp.float32) * 0.01
        return {'x': x, 'weight': weight, 'gate_w': gate_w, 'A_w': A_w, 'B_w': B_w}
    _L0_ffn_all = _L0_ffn_setup()
    _L0_ffn_in = {k: v for k, v in _L0_ffn_all.items() if k in ('weight', 'gate_w', 'A_w', 'B_w')}
    del _L0_ffn_all

    def _L1_attn_setup():
        import jax, jax.numpy as jnp
        import numpy as np
        D_MODEL = 512
        N_HEADS = 16
        N_KV_HEADS = 4
        D_K = D_MODEL // N_HEADS
        N_REP = N_HEADS // N_KV_HEADS
        WINDOW = 128
        RMS_EPS = 1e-08
        ROPE_BASE = 10000.0
        MASK_FILL = -10000.0

        def _rmsnorm(x, w):
            rms = jnp.sqrt(jnp.mean(x * x, axis=-1, keepdims=True) + RMS_EPS)
            return x / rms * w

        def _rope(x, cos, sin):
            B, S, H, dk = x.shape
            xr = x.reshape(B, S, H, dk // 2, 2)
            x1, x2 = (xr[..., 0], xr[..., 1])
            c = cos[None, :, None, :]
            s = sin[None, :, None, :]
            o1 = x1 * c - x2 * s
            o2 = x1 * s + x2 * c
            return jnp.stack([o1, o2], axis=-1).reshape(B, S, H, dk)
        key = jax.random.key(seed)
        ks = jax.random.split(key, 10)
        B, S = (2, 512)
        std = 1.0 / np.sqrt(D_MODEL)
        inp = {'x': jax.random.normal(ks[0], (B, S, D_MODEL), dtype=jnp.float32), 'Wq': jax.random.normal(ks[1], (D_MODEL, D_MODEL), dtype=jnp.float32) * std, 'bq': jnp.zeros((D_MODEL,), dtype=jnp.float32), 'Wk': jax.random.normal(ks[2], (N_KV_HEADS * D_K, D_MODEL), dtype=jnp.float32) * std, 'bk': jnp.zeros((N_KV_HEADS * D_K,), dtype=jnp.float32), 'Wv': jax.random.normal(ks[3], (N_KV_HEADS * D_K, D_MODEL), dtype=jnp.float32) * std, 'bv': jnp.zeros((N_KV_HEADS * D_K,), dtype=jnp.float32), 'Wo': jax.random.normal(ks[4], (D_MODEL, D_MODEL), dtype=jnp.float32) * std, 'bo': jnp.zeros((D_MODEL,), dtype=jnp.float32), 'qn_w': jnp.ones((D_K,), dtype=jnp.float32), 'kn_w': jnp.ones((D_K,), dtype=jnp.float32), 'scale': jnp.asarray(1.0 / np.sqrt(D_K), dtype=jnp.float32)}
        return inp
    _L1_attn_all = _L1_attn_setup()
    _L1_attn_in = {k: v for k, v in _L1_attn_all.items() if k in ('Wq', 'bq', 'Wk', 'bk', 'Wv', 'bv', 'Wo', 'bo', 'qn_w', 'kn_w', 'scale')}
    del _L1_attn_all

    def _L1_xattn_setup():
        import jax, jax.numpy as jnp
        import numpy as np
        EPS = 1e-05

        def rmsnorm(x, g, eps=EPS):
            var = jnp.mean(jnp.square(x), axis=-1, keepdims=True)
            return x * jax.lax.rsqrt(var + eps) * g
        key = jax.random.key(seed)
        ks = jax.random.split(key, 8)
        B, Sq, Skv = (2, 1024, 128)
        dim, cdim, H, D = (512, 256, 16, 128)
        inner = H * D
        s = lambda f: 1.0 / np.sqrt(f)
        return {'hidden_states': jax.random.normal(ks[0], (B, Sq, dim), jnp.float32), 'encoder_hidden_states': jax.random.normal(ks[1], (B, Skv, cdim), jnp.float32), 'Wq': jax.random.normal(ks[2], (dim, inner), jnp.float32) * s(dim), 'Wk': jax.random.normal(ks[3], (cdim, inner), jnp.float32) * s(cdim), 'Wv': jax.random.normal(ks[4], (cdim, inner), jnp.float32) * s(cdim), 'Wo': jax.random.normal(ks[5], (inner, dim), jnp.float32) * s(inner), 'gq': jnp.ones((D,), jnp.float32), 'gk': jnp.ones((D,), jnp.float32)}
    _L1_xattn_all = _L1_xattn_setup()
    _L1_xattn_in = {k: v for k, v in _L1_xattn_all.items() if k in ('Wq', 'Wk', 'Wv', 'Wo', 'gq', 'gk')}
    del _L1_xattn_all

    def _L1_ffn_setup():
        import jax, jax.numpy as jnp
        import numpy as np
        B, L, D = (4, 512, 512)
        S, K, NB = (16, 4, 2)
        H = D // 64
        EPS = 1e-06

        def _rms(x, w):
            return x * jax.lax.rsqrt(jnp.mean(x * x, axis=-1, keepdims=True) + EPS) * w
        key = jax.random.key(seed)
        ks = jax.random.split(key, 8)
        g = lambda k, shape, s: jax.random.normal(k, shape, dtype=jnp.float32) * s
        return {'x': g(ks[0], (B, L, D), 1.0), 'workspace': g(ks[1], (S, D), 0.02), 'compete_w': g(ks[2], (S, D), 0.02), 'compete_b': jnp.zeros((S,), jnp.float32), 'write_w': g(ks[3], (D, D), 0.02), 'write_b': jnp.zeros((D,), jnp.float32), 'in_proj_w': g(ks[4], (3 * D, D), 0.02), 'in_proj_b': jnp.zeros((3 * D,), jnp.float32), 'out_proj_w': g(ks[5], (D, D), 0.02), 'out_proj_b': jnp.zeros((D,), jnp.float32), 'ig_w': g(ks[6], (1, D), 0.02), 'ig_b': jnp.zeros((1,), jnp.float32), 'norm_pre_w': jnp.ones((D,), jnp.float32), 'norm_post_w': jnp.ones((D,), jnp.float32)}
    _L1_ffn_all = _L1_ffn_setup()
    _L1_ffn_in = {k: v for k, v in _L1_ffn_all.items() if k in ('workspace', 'compete_w', 'compete_b', 'write_w', 'write_b', 'in_proj_w', 'in_proj_b', 'out_proj_w', 'out_proj_b', 'ig_w', 'ig_b', 'norm_pre_w', 'norm_post_w')}
    del _L1_ffn_all
    return {'x': x, 'ctx_1024': ctx_1024, 'L0_attn_W_q': _L0_attn_in['W_q'], 'L0_attn_W_k': _L0_attn_in['W_k'], 'L0_attn_W_v': _L0_attn_in['W_v'], 'L0_attn_W_o': _L0_attn_in['W_o'], 'L0_xattn_Wq': _L0_xattn_in['Wq'], 'L0_xattn_bq': _L0_xattn_in['bq'], 'L0_xattn_Wk': _L0_xattn_in['Wk'], 'L0_xattn_bk': _L0_xattn_in['bk'], 'L0_ffn_weight': _L0_ffn_in['weight'], 'L0_ffn_gate_w': _L0_ffn_in['gate_w'], 'L0_ffn_A_w': _L0_ffn_in['A_w'], 'L0_ffn_B_w': _L0_ffn_in['B_w'], 'L1_attn_Wq': _L1_attn_in['Wq'], 'L1_attn_bq': _L1_attn_in['bq'], 'L1_attn_Wk': _L1_attn_in['Wk'], 'L1_attn_bk': _L1_attn_in['bk'], 'L1_attn_Wv': _L1_attn_in['Wv'], 'L1_attn_bv': _L1_attn_in['bv'], 'L1_attn_Wo': _L1_attn_in['Wo'], 'L1_attn_bo': _L1_attn_in['bo'], 'L1_attn_qn_w': _L1_attn_in['qn_w'], 'L1_attn_kn_w': _L1_attn_in['kn_w'], 'L1_attn_scale': _L1_attn_in['scale'], 'L1_xattn_Wq': _L1_xattn_in['Wq'], 'L1_xattn_Wk': _L1_xattn_in['Wk'], 'L1_xattn_Wv': _L1_xattn_in['Wv'], 'L1_xattn_Wo': _L1_xattn_in['Wo'], 'L1_xattn_gq': _L1_xattn_in['gq'], 'L1_xattn_gk': _L1_xattn_in['gk'], 'L1_ffn_workspace': _L1_ffn_in['workspace'], 'L1_ffn_compete_w': _L1_ffn_in['compete_w'], 'L1_ffn_compete_b': _L1_ffn_in['compete_b'], 'L1_ffn_write_w': _L1_ffn_in['write_w'], 'L1_ffn_write_b': _L1_ffn_in['write_b'], 'L1_ffn_in_proj_w': _L1_ffn_in['in_proj_w'], 'L1_ffn_in_proj_b': _L1_ffn_in['in_proj_b'], 'L1_ffn_out_proj_w': _L1_ffn_in['out_proj_w'], 'L1_ffn_out_proj_b': _L1_ffn_in['out_proj_b'], 'L1_ffn_ig_w': _L1_ffn_in['ig_w'], 'L1_ffn_ig_b': _L1_ffn_in['ig_b'], 'L1_ffn_norm_pre_w': _L1_ffn_in['norm_pre_w'], 'L1_ffn_norm_post_w': _L1_ffn_in['norm_post_w']}

def reference(x, ctx_1024, L0_attn_W_q, L0_attn_W_k, L0_attn_W_v, L0_attn_W_o, L0_xattn_Wq, L0_xattn_bq, L0_xattn_Wk, L0_xattn_bk, L0_ffn_weight, L0_ffn_gate_w, L0_ffn_A_w, L0_ffn_B_w, L1_attn_Wq, L1_attn_bq, L1_attn_Wk, L1_attn_bk, L1_attn_Wv, L1_attn_bv, L1_attn_Wo, L1_attn_bo, L1_attn_qn_w, L1_attn_kn_w, L1_attn_scale, L1_xattn_Wq, L1_xattn_Wk, L1_xattn_Wv, L1_xattn_Wo, L1_xattn_gq, L1_xattn_gk, L1_ffn_workspace, L1_ffn_compete_w, L1_ffn_compete_b, L1_ffn_write_w, L1_ffn_write_b, L1_ffn_in_proj_w, L1_ffn_in_proj_b, L1_ffn_out_proj_w, L1_ffn_out_proj_b, L1_ffn_ig_w, L1_ffn_ig_b, L1_ffn_norm_pre_w, L1_ffn_norm_post_w):
    import jax
    import jax.numpy as jnp

    def _L0_attn_ref(x, W_q, W_k, W_v, W_o):
        import jax, jax.numpy as jnp
        import numpy as np
        B, S, D = (2, 512, 512)
        N_HEADS, N_KV_HEADS = (16, 4)
        HEAD_DIM = D // N_HEADS

        def _apply_rope(xh, positions):
            Dh = xh.shape[-1]
            half = Dh // 2
            freqs = 1.0 / 10000.0 ** (jnp.arange(half, dtype=jnp.float32) / half)
            angles = positions[:, None].astype(jnp.float32) * freqs[None, :]
            cos, sin = (jnp.cos(angles), jnp.sin(angles))
            xp = xh.reshape(*xh.shape[:-1], half, 2)
            x0, x1 = (xp[..., 0], xp[..., 1])
            r0 = x0 * cos - x1 * sin
            r1 = x0 * sin + x1 * cos
            return jnp.stack([r0, r1], axis=-1).reshape(xh.shape)
        b, s, d = x.shape
        positions = jnp.arange(s)
        rep = N_HEADS // N_KV_HEADS
        Q = (x @ W_q).reshape(b, s, N_HEADS, HEAD_DIM).transpose(0, 2, 1, 3)
        K = (x @ W_k).reshape(b, s, N_KV_HEADS, HEAD_DIM).transpose(0, 2, 1, 3)
        V = (x @ W_v).reshape(b, s, N_KV_HEADS, HEAD_DIM).transpose(0, 2, 1, 3)
        Qr = _apply_rope(Q, positions)
        K_rep = jnp.tile(K, (1, rep, 1, 1))
        V_rep = jnp.tile(V, (1, rep, 1, 1))
        Kr = _apply_rope(K_rep, positions)
        scores = jnp.einsum('bhqd,bhkd->bhqk', Qr, Kr) / HEAD_DIM ** 0.5
        weights = jax.nn.softmax(scores, axis=-1)
        out = jnp.einsum('bhqk,bhkd->bhqd', weights, V_rep)
        out = out.transpose(0, 2, 1, 3).reshape(b, s, d)
        return out @ W_o

    def _L0_xattn_ref(teacher_logits, teacher_features, Wq, bq, Wk, bk):
        import jax, jax.numpy as jnp
        import numpy as np
        query = jnp.einsum('bnc,dc->bnd', teacher_features, Wq) + bq
        key = jnp.einsum('bnc,dc->bnd', teacher_features, Wk) + bk
        energy = jnp.einsum('bnd,bmd->bnm', query, key)
        attention = jax.nn.softmax(energy, axis=-1)
        x_m = jnp.einsum('bln,bmn->blm', teacher_logits, attention)
        return x_m

    def _L0_ffn_ref(x, weight, gate_w, A_w, B_w):
        import jax, jax.numpy as jnp
        import numpy as np
        LORA_ALPHA = 16.0
        TOP_K = 2
        E = gate_w.shape[0]
        out = jnp.einsum('bsh,oh->bso', x, weight)
        logits = jnp.einsum('bsh,eh->bse', x, gate_w)
        probs = jax.nn.softmax(logits, axis=-1)
        topk_w, topk_idx = jax.lax.top_k(probs, TOP_K)
        topk_w = topk_w / jnp.sum(topk_w, axis=-1, keepdims=True)
        onehot = jax.nn.one_hot(topk_idx, E, dtype=x.dtype)
        cw = jnp.einsum('bsk,bske->bse', topk_w, onehot)
        t = jnp.einsum('bsh,erh->bser', x, A_w)
        t = t * cw[..., None]
        lora = jnp.einsum('bser,eor->bso', t, B_w)
        return out + LORA_ALPHA * lora

    def _L1_attn_ref(x, Wq, bq, Wk, bk, Wv, bv, Wo, bo, qn_w, kn_w, scale):
        import jax, jax.numpy as jnp
        import numpy as np
        D_MODEL = 512
        N_HEADS = 16
        N_KV_HEADS = 4
        D_K = D_MODEL // N_HEADS
        N_REP = N_HEADS // N_KV_HEADS
        WINDOW = 128
        RMS_EPS = 1e-08
        ROPE_BASE = 10000.0
        MASK_FILL = -10000.0

        def _rmsnorm(x, w):
            rms = jnp.sqrt(jnp.mean(x * x, axis=-1, keepdims=True) + RMS_EPS)
            return x / rms * w

        def _rope(x, cos, sin):
            B, S, H, dk = x.shape
            xr = x.reshape(B, S, H, dk // 2, 2)
            x1, x2 = (xr[..., 0], xr[..., 1])
            c = cos[None, :, None, :]
            s = sin[None, :, None, :]
            o1 = x1 * c - x2 * s
            o2 = x1 * s + x2 * c
            return jnp.stack([o1, o2], axis=-1).reshape(B, S, H, dk)
        B, S, D = x.shape
        q = (x @ Wq.T + bq).reshape(B, S, N_HEADS, D_K)
        k = (x @ Wk.T + bk).reshape(B, S, N_KV_HEADS, D_K)
        v = (x @ Wv.T + bv).reshape(B, S, N_KV_HEADS, D_K)
        q = _rmsnorm(q, qn_w)
        k = _rmsnorm(k, kn_w)
        inv_freq = 1.0 / ROPE_BASE ** (jnp.arange(0, D_K, 2, dtype=jnp.float32) / D_K)
        t = jnp.arange(S, dtype=jnp.float32)
        freqs = t[:, None] * inv_freq[None, :]
        cos, sin = (jnp.cos(freqs), jnp.sin(freqs))
        q = _rope(q, cos, sin)
        k = _rope(k, cos, sin)
        q = q.transpose(0, 2, 1, 3)
        k = k.transpose(0, 2, 1, 3)
        v = v.transpose(0, 2, 1, 3)
        k = jnp.repeat(k, N_REP, axis=1)
        v = jnp.repeat(v, N_REP, axis=1)
        scores = jnp.einsum('bhqd,bhkd->bhqk', q, k) * scale
        idx = jnp.arange(S)
        causal = idx[:, None] < idx[None, :]
        local = jnp.abs(idx[:, None] - idx[None, :]) > WINDOW // 2
        mask = causal | local
        scores = jnp.where(mask[None, None, :, :], MASK_FILL, scores)
        attn = jax.nn.softmax(scores, axis=-1)
        out = jnp.einsum('bhqk,bhkd->bhqd', attn, v)
        out = out.transpose(0, 2, 1, 3).reshape(B, S, D)
        return out @ Wo.T + bo

    def _L1_xattn_ref(hidden_states, encoder_hidden_states, Wq, Wk, Wv, Wo, gq, gk):
        import jax, jax.numpy as jnp
        import numpy as np
        EPS = 1e-05

        def rmsnorm(x, g, eps=EPS):
            var = jnp.mean(jnp.square(x), axis=-1, keepdims=True)
            return x * jax.lax.rsqrt(var + eps) * g
        B, Sq, _ = hidden_states.shape
        Skv = encoder_hidden_states.shape[1]
        D = gq.shape[0]
        H = Wq.shape[1] // D
        scale = 1.0 / np.sqrt(D)
        q = (hidden_states @ Wq).reshape(B, Sq, H, D)
        k = (encoder_hidden_states @ Wk).reshape(B, Skv, H, D)
        v = (encoder_hidden_states @ Wv).reshape(B, Skv, H, D)
        q = rmsnorm(q, gq)
        k = rmsnorm(k, gk)
        scores = jnp.einsum('bqhd,bkhd->bhqk', q, k) * scale
        attn = jax.nn.softmax(scores, axis=-1)
        out = jnp.einsum('bhqk,bkhd->bqhd', attn, v)
        out = out.reshape(B, Sq, H * D)
        return out @ Wo

    def _L1_ffn_ref(x, workspace, compete_w, compete_b, write_w, write_b, in_proj_w, in_proj_b, out_proj_w, out_proj_b, ig_w, ig_b, norm_pre_w, norm_post_w):
        import jax, jax.numpy as jnp
        import numpy as np
        B, L, D = (4, 512, 512)
        S, K, NB = (16, 4, 2)
        H = D // 64
        EPS = 1e-06

        def _rms(x, w):
            return x * jax.lax.rsqrt(jnp.mean(x * x, axis=-1, keepdims=True) + EPS) * w
        Bq, Lq, Dd = x.shape
        hd = Dd // H
        scale = 1.0 / np.sqrt(hd).astype(np.float32)
        ws = jnp.broadcast_to(workspace[None], (Bq, S, Dd))
        wq, wk, wv = (in_proj_w[:Dd], in_proj_w[Dd:2 * Dd], in_proj_w[2 * Dd:])
        bq, bk, bv = (in_proj_b[:Dd], in_proj_b[Dd:2 * Dd], in_proj_b[2 * Dd:])
        k_eff = min(K, Lq)
        for _ in range(NB):
            logits = _rms(x, norm_pre_w) @ compete_w.T + compete_b
            slot_logits = jnp.swapaxes(logits, 1, 2)
            vals, idx = jax.lax.top_k(slot_logits, k_eff)
            wgt = jax.nn.softmax(vals, axis=-1)
            wx = x @ write_w.T + write_b
            gathered = jnp.take_along_axis(wx[:, None], idx[..., None], axis=2)
            written = jnp.einsum('bsk,bskd->bsd', wgt, gathered)
            ws = _rms(ws + written, norm_post_w)
            q = (x @ wq.T + bq).reshape(Bq, Lq, H, hd)
            kk = (ws @ wk.T + bk).reshape(Bq, S, H, hd)
            vv = (ws @ wv.T + bv).reshape(Bq, S, H, hd)
            att = jax.nn.softmax(jnp.einsum('blhd,bshd->bhls', q, kk) * scale, axis=-1)
            ctx = jnp.einsum('bhls,bshd->blhd', att, vv).reshape(Bq, Lq, Dd)
            x_b = ctx @ out_proj_w.T + out_proj_b
            x = _rms(x + x_b, norm_post_w)
            ignition = jax.nn.sigmoid(x @ ig_w.T + ig_b)
        return x
    x = _layernorm(x + _L0_attn_ref(x, L0_attn_W_q, L0_attn_W_k, L0_attn_W_v, L0_attn_W_o), axis=-1)
    x = _layernorm(x + _L0_xattn_ref(x, ctx_1024, L0_xattn_Wq, L0_xattn_bq, L0_xattn_Wk, L0_xattn_bk), axis=-1)
    x = _layernorm(x + _L0_ffn_ref(x, L0_ffn_weight, L0_ffn_gate_w, L0_ffn_A_w, L0_ffn_B_w), axis=-1)
    x = _layernorm(x + _L1_attn_ref(x, L1_attn_Wq, L1_attn_bq, L1_attn_Wk, L1_attn_bk, L1_attn_Wv, L1_attn_bv, L1_attn_Wo, L1_attn_bo, L1_attn_qn_w, L1_attn_kn_w, L1_attn_scale), axis=-1)
    x = _layernorm(x + _L1_xattn_ref(x, ctx_1024, L1_xattn_Wq, L1_xattn_Wk, L1_xattn_Wv, L1_xattn_Wo, L1_xattn_gq, L1_xattn_gk), axis=-1)
    x = _layernorm(x + _L1_ffn_ref(x, L1_ffn_workspace, L1_ffn_compete_w, L1_ffn_compete_b, L1_ffn_write_w, L1_ffn_write_b, L1_ffn_in_proj_w, L1_ffn_in_proj_b, L1_ffn_out_proj_w, L1_ffn_out_proj_b, L1_ffn_ig_w, L1_ffn_ig_b, L1_ffn_norm_pre_w, L1_ffn_norm_post_w), axis=-1)
    return x

_drawn_inputs = setup_inputs


def setup_inputs(seed=0):
    import zlib

    import numpy as np

    out = dict(_drawn_inputs(seed))
    spreads = {'L0_xattn_bq': (0.0, 0.1),
     'L0_xattn_bk': (0.0, 0.8),
     'L1_attn_bq': (0.0, 0.341),
     'L1_attn_bk': (0.0, 0.567),
     'L1_attn_bv': (0.0, 0.1),
     'L1_attn_bo': (0.0, 0.1),
     'L1_attn_qn_w': (1.0, 0.2),
     'L1_attn_kn_w': (1.0, 0.2),
     'L1_xattn_gq': (1.0, 0.2),
     'L1_xattn_gk': (1.0, 0.2),
     'L1_ffn_compete_b': (0.0, 0.8),
     'L1_ffn_write_b': (0.0, 0.1),
     'L1_ffn_in_proj_b': (0.0, 0.1),
     'L1_ffn_out_proj_b': (0.0, 0.1),
     'L1_ffn_norm_pre_w': (1.0, 0.6),
     'L1_ffn_norm_post_w': (1.0, 0.2)}
    factors = {'L0_attn_W_q': 8.0,
     'L0_attn_W_k': 8.0,
     'L0_attn_W_v': 4.89,
     'L0_attn_W_o': 4.579,
     'L0_ffn_gate_w': 3.339,
     'L0_ffn_A_w': 2.883,
     'L0_ffn_B_w': 2.895,
     'L1_ffn_workspace': 8.0}
    for name, (base, spread) in spreads.items():
        noise = np.random.default_rng([zlib.crc32(name.encode()), seed]).standard_normal(out[name].shape)
        drawn = base * np.exp(spread * noise) if base else spread * noise
        out[name] = jnp.asarray(drawn.astype(out[name].dtype))
    for name, factor in factors.items():
        out[name] = (out[name] * factor).astype(out[name].dtype)
    return out
```

```python
from contextlib import ExitStack

import numpy as np

import concourse.bass as bass
from concourse import mybir

P = 128
B, S, D = 4, 512, 512
T = S // P
KD = D // P
NH, HD, NKV = 16, 32, 4
NQK = NH + NKV
NK = NKV * HD
NQKV = D + 2 * NK
STK = 3 * HD
DC = 256
KC = DC // P
DX = 128
NE, RANK, TOPK = 8, 16, 2
LORA = NE * RANK
LORA_ALPHA = 16.0
WIN = 64
NS = 16
H6, W6 = 8, 64
NP = H6 // 2
SB = 32
K6 = 4
EPS6 = 1e-6
NEG = -30000.0
LOWEST = -3.0e38

F32 = mybir.dt.float32
F32R = mybir.dt.float32r
BF16 = mybir.dt.bfloat16
ALU = mybir.AluOpType
ACT = mybir.ActivationFunctionType
AX = mybir.AxisListType


class Count:

    def __init__(self, sem, per=0):
        self.sem, self.base, self.per = sem, 0, per

    def open(self, per):
        self.per = per

    def after(self, turn, k):
        return self.sem, turn * self.per + (self.base + k)

    def close(self, turns):
        self.base += turns * self.per


class Buffers:
    pass


class Banks:

    def __init__(self, tensor, filled, freed):
        self.t, self.filled_sems, self.freed_sems = tensor, filled, freed
        self.base = [0] * 8

    def open(self, uses, outer=()):
        self.outer, self.outer_per = {}, [0] * 8
        for key, bank, width in outer:
            self.outer[key] = (bank, width, self.outer_per[bank])
            self.outer_per[bank] += 1
        self.use, self.per = {}, [0] * 8
        last = {}
        before = {}
        for key, bank, width in uses:
            assert key not in self.use
            before[key] = [last.get(k) for k in range(bank, bank + width)]
            self.use[key] = (bank, width, self.per[bank])
            self.per[bank] += 1
            for k in range(bank, bank + width):
                last[k] = key
        self.before = {key: [p if p is not None else ("wrap", last[self.use[key][0] + i])
                             for i, p in enumerate(ps)] for key, ps in before.items()}

    def where(self, key):
        return self.outer[key] if key in self.outer else self.use[key]

    def ap(self, key, j=0):
        return self.t[:, self.where(key)[0] + j, :]

    def pair(self, key):
        bank, width, _ = self.where(key)
        return self.t[:, bank:bank + width, :]

    def filled(self, key):
        return self.filled_sems[self.where(key)[0]]

    def freed(self, key):
        return self.freed_sems[self.where(key)[0]]

    def count(self, turn, bank, inner):
        if not isinstance(turn, tuple):
            return turn * self.per[bank] + self.base[bank]
        o = self.outer_per[bank]
        n = self.base[bank] + (o if inner else 0)
        return turn[1] * self.per[bank] + turn[0] * o + n if o else turn[1] * self.per[bank] + n

    def full(self, turn, key):
        bank, _, i = self.where(key)
        return self.filled_sems[bank], self.count(turn, bank, key in self.use) + (i + 1)

    def released(self, turn, key):
        bank, _, i = self.where(key)
        return self.freed_sems[bank], self.count(turn, bank, key in self.use) + (i + 1 + self.base_freed)

    def wait_empty(self, pe, turn, key):
        if key in self.outer:
            bank, _, i = self.outer[key]
            pe.wait_ge(self.freed_sems[bank], self.count(turn, bank, False) + (i + self.base_freed))
            return
        seen = set()
        for p in self.before[key]:
            if p in seen:
                continue
            seen.add(p)
            if p[0] == "wrap":
                bank = self.use[p[1]][0]
                pe.wait_ge(self.freed_sems[bank], self.count(turn, bank, True) + self.base_freed)
            else:
                pe.wait_ge(*self.released(turn, p))

    def close(self, turns, outer_turns=0):
        for k in range(8):
            self.base[k] += turns * self.per[k] + outer_turns * self.outer_per[k]


def split3(pe, out, lhs, rhs, start, stop):
    pe.matmul(out, lhs[0], rhs[0], start=start, stop=False)
    pe.matmul(out, lhs[0], rhs[1], start=False, stop=False)
    return pe.matmul(out, lhs[1], rhs[0], start=False, stop=stop)


class Core:

    def __init__(self, nc, ctx, d):
        self.nc, self.d = nc, d

        def sem(name):
            return ctx.enter_context(nc.semaphore(name))

        def sb(name, shape, dt=F32):
            return ctx.enter_context(nc.sbuf_tensor(name, shape, dt))

        def primed(name, per):
            count = Count(sem(name), per)
            count.base = 1
            self.prime.append(count.sem)
            return count

        self.sem, self.prime = sem, []
        self.x = sb("x_all", [P, B * T, D])
        self.xcur = sb("x_cur", [P, T, D])
        self.xhi = sb("xT_hi", [P, KD, S], F32R)
        self.xlo = sb("xT_lo", [P, KD, S], F32R)
        self.ident = sb("ident_sb", [P, P])
        self.ones = sb("ones_sb", [P, P])
        self.mhalf = sb("minus_half", [P, 128])
        self.stats = sb("ln_stats", [P, T, 6])
        self.mv = sb("ln_mean_var", [P, T, 2])
        self.veps = sb("ln_var_eps", [P, T])
        self.rstd = sb("ln_rstd", [P, T])
        self.ps = Banks(ctx.enter_context(nc.psum_tensor("banks", [P, 8, 512], F32)),
                        [sem(f"bank{i}_filled") for i in range(8)], [sem(f"bank{i}_freed") for i in range(8)])
        self.cur = Count(sem("x_cur_loaded"), 16)
        self.xT_hi = primed("xT_hi_ready", KD)
        self.var_ready = Count(sem("ln_var_ready"), 1)
        self.rstd_ready = Count(sem("ln_rstd_ready"), 1)
        self.ps.base_freed = 1
        self.prime += self.ps.freed_sems
        self.s1_stacked, self.s4_stacked = primed("s1_stacked", T), primed("s4_stacked", T)
        self.s2_proj_hi = primed("s2_proj_hi_ready", 2)
        self.s4_v_out, self.s4_roped = primed("s4_v_out", T), primed("s4_rope_parts", T)
        self.s5_ctx_lo = primed("s5_ctx_lo_ready", 1)
        self.s6_ssq, self.s6_ms = primed("s6_x_squares_summed", 1), primed("s6_x_mean_sq_ready", 1)
        self.consts = sem("consts_loaded")
        self.pool_consts = sem("pool_consts_set")

    def start(self, stage):
        block = stage.enter_context(self.nc.Block())

        @block.sync
        def _(sp):
            for b in range(B):
                sp.dma_start(self.x[:, b * T:(b + 1) * T, :], self.d["x"][b].rearrange("(t p) d -> p t d", p=P)) \
                  .then_inc(self.consts, 16)
            sp.dma_start(self.ident[:, :], self.d["ident"]).then_inc(self.consts, 16)
            sp.wait_ge(self.consts, 16 * (B + 1))

        @block.gpsimd
        def _(pool):
            pool.memset(self.mhalf[:, :], -0.5)
            pool.memset(self.ones[:, :], 1.0).then_inc(self.pool_consts, 1)
            for s in self.prime:
                pool.nop().then_inc(s, 1)
            pool.wait_ge(self.pool_consts, 1)

    def x_uses(self, banks):
        return [(("x", k), banks[k % len(banks)], 1) for k in range(KD)]

    def close(self, turns, outer_turns=0):
        self.ps.close(turns, outer_turns)
        for c in (self.cur, self.xT_hi, self.var_ready, self.rstd_ready):
            c.close(B)

    def sync_load_x(self, sp, b, src=None, read=None):
        src = self.x if src is None else src
        sp.wait_ge(*(self.xT_hi if read is None else read).after(b, 0))
        sp.dma_start(self.xcur[:, :, :], src[:, bass.ds(b * T, T), :]).then_inc(self.cur.sem, 16)

    def pe_turn_x(self, pe, b, turn=None):
        turn = b if turn is None else turn
        pe.wait_ge(*self.cur.after(b, 16))
        for k in range(KD):
            self.ps.wait_empty(pe, turn, ("x", k))
            for t in range(T):
                mm = pe.transpose(self.ps.ap(("x", k))[:, t * P:(t + 1) * P],
                                  self.xcur[:, t, k * P:(k + 1) * P], self.ident[:, :])
            mm.then_inc(self.ps.filled(("x", k)), 1)

    def act_x_hi(self, act, b, turn=None):
        turn = b if turn is None else turn
        for k in range(KD):
            act.wait_ge(*self.ps.full(turn, ("x", k)))
            act.activation(self.xhi[:, k, :], self.ps.ap(("x", k)), ACT.Copy).then_inc(self.xT_hi.sem, 1)

    def dve_x_lo(self, dve, b, turn=None):
        turn = b if turn is None else turn
        for k in range(KD):
            dve.wait_ge(*self.xT_hi.after(b, k + 1))
            dve.tensor_tensor(self.xlo[:, k, :], self.ps.ap(("x", k)),
                              self.xhi[:, k, :].bitcast(F32), ALU.subtract).then_inc(self.ps.freed(("x", k)), 1)

    def wait_xT(self, pe, turn):
        for k in range(KD):
            pe.wait_ge(*self.ps.released(turn, ("x", k)))

    def y_uses(self, banks):
        return [(("y", t), banks[t % len(banks)], 1) for t in range(T)]

    def dve_layernorm(self, dve, b):
        for t in range(T):
            xt = self.x[:, b * T + t, :]
            dve.wait_ge(*self.ps.full(b, ("y", t)))
            dve.tensor_tensor(xt, self.ps.ap(("y", t)), xt, ALU.add).then_inc(self.ps.freed(("y", t)), 1)
            dve.drain()
            dve.bn_stats(self.stats[:, t, :], xt)
        self.dve_normalize(dve, b)

    def dve_normalize(self, dve, b, eps=1e-5):
        dve.drain()
        for t in range(T):
            dve.bn_aggr(self.mv[:, t, :], self.stats[:, t, :])
        dve.drain()
        dve.tensor_scalar(self.veps[:, :], self.mv[:, :, 1], eps, None, ALU.add).then_inc(self.var_ready.sem, 1)
        dve.wait_ge(*self.rstd_ready.after(b, 1))
        for t in range(T):
            xt = self.x[:, b * T + t, :]
            dve.tensor_scalar(xt, xt, self.mv[:, t, 0:1], self.rstd[:, t:t + 1], ALU.subtract, ALU.mult)

    def pool_rstd(self, pool, b):
        pool.wait_ge(*self.var_ready.after(b, 1))
        pool.tensor_tensor(self.rstd[:, :], self.veps[:, :], self.mhalf[:, 0:T], ALU.pow) \
            .then_inc(self.rstd_ready.sem, 1)


def rope_attention(c):
    nc, d, ps = c.nc, c.d, c.ps
    with ExitStack() as ctx:
        def sb(nm, shape, dt=F32):
            return ctx.enter_context(nc.sbuf_tensor(f"s1_{nm}", shape, dt))

        wq_hi = sb("wqkv_hi", [P, KD, NQKV], F32R)
        wq_lo = sb("wqkv_lo", [P, KD, NQKV], F32R)
        wo = sb("wo", [P, KD, D])
        qs = sb("q_stacks", [P, T, NH, STK])
        ks = sb("k_stacks", [P, T, NKV, STK])
        kT = sb("kT", [P, NKV, S], F32R)
        NQB = 4
        qT = sb("qT", [P, NQB, S], F32R)
        nmax = sb("neg_max", [P, 2, T, HD])
        v = sb("v", [P, T, NK])
        NPB = 6
        probsT = sb("probsT", [P, NPB, T, S])
        outT = sb("outT", [P, 4, S])
        inv = sb("inv_sums", [P, S])
        ra = sb("rope_a", [P, NQK * HD])
        rb = sb("rope_b", [P, NQK * HD])
        cs = sb("cos_sin", [P, T, 2, HD])
        wraw = probsT[:, 0:3, :, :].rearrange("p a b c -> p (a b c)")[:, 0:KD * NQKV] \
            .rearrange("p (k n) -> p k n", k=KD)

        weights = c.sem("s1_weights_loaded")
        w_hi = c.sem("s1_w_hi_ready")
        w_lo = c.sem("s1_w_lo_ready")
        frame = c.sem("s1_constant_rows_set")
        ra_rb = Count(c.sem("s1_rope_parts"), T)
        r_sum = Count(c.sem("s1_rope_sum"), T)
        r_hi = Count(c.sem("s1_rope_hi"), T)
        stacked = c.s1_stacked
        max_ready = Count(c.sem("s1_max_ready"), NH)
        inv_ready = Count(c.sem("s1_inv_ready"), NKV)

        steps = [("q", 0)]
        for i in range(NH + 4):
            if 0 <= i - 1 < NH:
                steps.append(("m", i - 1))
            if i + 1 < NH:
                steps.append(("q", i + 1))
            for t in range(T):
                if i < NH:
                    steps.append(("s", i, t))
                if 0 <= i - 2 < NH:
                    steps.append(("e", i - 2, t))
            g, r = (i - 6) // 4, (i - 6) % 4
            if 0 <= g < 4 and r < 2:
                steps += [("o", g, 2 * r), ("o", g, 2 * r + 1)]
        uses = c.x_uses([2, 3]) + [(("p", t), (0, 4)[t % 2], 2) for t in range(T)]
        uses += [(("k", g), 5, 1) for g in range(NKV)]
        n = {"s": 0, "e": 0}
        for s in steps:
            if s[0] in "qm":
                uses.append((s, 5, 1))
            elif s[0] == "s":
                uses.append((s, n["s"] % 2, 1))
                n["s"] += 1
            elif s[0] == "e":
                uses.append((s, 2 + n["e"] % 3, 1))
                n["e"] += 1
            elif s[2] == 0:
                uses.append((("o", s[1]), 6, 2))
        ps.open(uses + c.y_uses([0, 1]))

        block = ctx.enter_context(nc.Block())

        @block.sync
        def _(sp):
            sp.dma_start(wraw, d["l0a_wqkv"].rearrange("(k p) n -> p k n", p=P)).then_inc(weights, 16)
            sp.dma_start(cs[:, :, :, :], d["cos_sin"].rearrange("(t p) a n -> p t a n", p=P)).then_inc(weights, 16)
            sp.dma_start(wo[:, :, :], d["l0a_wo"].rearrange("(k p) n -> p k n", p=P)).then_inc(weights, 16)
            with sp.Fori(0, B) as b:
                c.sync_load_x(sp, b)

        @block.gpsimd
        def _(pool):
            pool.memset(kT[STK:P, :, :].bitcast(F32), 0.0)
            pool.drain()
            pool.memset(kT[STK:STK + 1, :, :].bitcast(F32), 1.0)
            pool.drain()
            pool.memset(nmax[:, :, :, :], 0.0).then_inc(frame, 1)
            pool.wait_ge(w_hi, 1)
            pool.tensor_tensor(wq_lo[:, :, :], wraw, wq_hi[:, :, :].bitcast(F32), ALU.subtract).then_inc(w_lo, 1)
            with pool.Fori(0, B) as b:
                for t in range(T):
                    pool.wait_ge(*ra_rb.after(b, t + 1))
                    pool.tensor_tensor(ra[:, :], ra[:, :], rb[:, :], ALU.add).then_inc(r_sum.sem, 1)
                    pool.wait_ge(*r_hi.after(b, t + 1))
                    rq = ra[:, 0:D].rearrange("p (h e) -> p h e", e=HD)
                    rk = ra[:, D:].rearrange("p (h e) -> p h e", e=HD)
                    pool.tensor_tensor(qs[:, t, :, 2 * HD:].bitcast(F32R), rq, qs[:, t, :, 0:HD], ALU.subtract)
                    pool.tensor_tensor(ks[:, t, :, HD:2 * HD].bitcast(F32R), rk, ks[:, t, :, 0:HD], ALU.subtract) \
                        .then_inc(stacked.sem, 1)
                c.pool_rstd(pool, b)

        @block.scalar
        def _(act):
            act.wait_ge(weights, 48)
            act.activation(wq_hi[:, :, :], wraw, ACT.Copy).then_inc(w_hi, 1)
            with act.Fori(0, B) as b:
                c.act_x_hi(act, b)
                for t in range(T):
                    act.wait_ge(*ra_rb.after(b, t + 1))
                    act.activation(v[:, t, :], ps.ap(("p", t), 1)[:, NK:2 * NK], ACT.Copy) \
                       .then_inc(ps.freed(("p", t)), 1)
                    act.wait_ge(*r_sum.after(b, t + 1))
                    rq = ra[:, 0:D].rearrange("p (h e) -> p h e", e=HD)
                    rk = ra[:, D:].rearrange("p (h e) -> p h e", e=HD)
                    act.activation(qs[:, t, :, 0:HD].bitcast(F32R), rq, ACT.Copy)
                    act.activation(qs[:, t, :, HD:2 * HD].bitcast(F32R), rq, ACT.Copy)
                    act.activation(ks[:, t, :, 0:HD].bitcast(F32R), rk, ACT.Copy)
                    act.activation(ks[:, t, :, 2 * HD:].bitcast(F32R), rk, ACT.Copy).then_inc(r_hi.sem, 1)
                for g in range(NKV):
                    act.wait_ge(*ps.full(b, ("k", g)))
                    act.activation(kT[0:STK, g, :], ps.ap(("k", g))[0:STK, :], ACT.Copy) \
                       .then_inc(ps.freed(("k", g)), 1)
                for s in steps:
                    if s[0] == "q":
                        h = s[1]
                        act.wait_ge(*ps.full(b, s))
                        if h >= NQB:
                            act.wait_ge(*ps.full(b, ("e", h - NQB, T - 1)))
                        act.activation(qT[0:STK, h % NQB, :], ps.ap(s)[0:STK, :], ACT.Copy).then_inc(ps.freed(s), 1)
                    elif s[0] == "e":
                        h, k = s[1:]
                        act.wait_ge(*ps.full(b, s))
                        if h >= NPB and k == 0:
                            act.wait_ge(*ps.full(b, ("o", (h - NPB) // 4)))
                        act.activation(probsT[:, h % NPB, k, :], ps.ap(s), ACT.Exp).then_inc(ps.freed(s), 1)

        @block.vector
        def _(dve):
            dve.wait_ge(frame, 1)
            with dve.Fori(0, B) as b:
                c.dve_x_lo(dve, b)
                for t in range(T):
                    dve.wait_ge(*ps.full(b, ("p", t)))
                    dve.wait_ge(*stacked.after(b, t))
                    rope_parts(dve, ps.pair(("p", t)).rearrange("p a n -> p (a n)")[:, 0:NQK * HD], ra, rb, cs, t) \
                        .then_inc(ra_rb.sem, 1)

                def divide(g):
                    dve.wait_ge(*ps.full(b, ("o", g)))
                    dve.reciprocal(inv[:, :], ps.ap(("o", g), 1))
                    dve.drain()
                    dve.tensor_tensor(outT[:, g, :], ps.ap(("o", g)), inv[:, :], ALU.mult) \
                       .then_inc(ps.freed(("o", g)), 1)

                for s in steps:
                    if s[0] == "s":
                        h, t = s[1:]
                        dve.wait_ge(*ps.full(b, s))
                        if h >= 2 and t == 0:
                            dve.wait_ge(*ps.full(b, ("m", h - 2)))
                        dve.tensor_reduce(nmax[:, h % 2, t, 0:1], ps.ap(s), AX.X, ALU.max, negate=True) \
                           .then_inc(ps.freed(s), 1)
                    elif s[0] == "m":
                        h = s[1]
                        dve.wait_ge(*ps.full(b, s))
                        dve.tensor_copy(qT[STK:P, h % NQB, :], ps.ap(s)[STK:P, :]).then_inc(ps.freed(s), 1)
                    elif s[0] == "o" and s[2] == T - 1:
                        divide(s[1])
                c.dve_layernorm(dve, b)

        @block.tensor
        def _(pe):
            pe.wait_ge(w_lo, 1)
            pe.wait_ge(frame, 1)
            with pe.Fori(0, B) as b:
                c.pe_turn_x(pe, b)
                c.wait_xT(pe, b)
                for t in range(T):
                    ps.wait_empty(pe, b, ("p", t))
                    for lo, hi, j in ((0, D, 0), (D, NQKV, 1)):
                        for k in range(KD):
                            mm = split3(pe, ps.ap(("p", t), j)[:, 0:hi - lo],
                                        (c.xhi[:, k, t * P:(t + 1) * P], c.xlo[:, k, t * P:(t + 1) * P]),
                                        (wq_hi[:, k, lo:hi], wq_lo[:, k, lo:hi]), k == 0, k == KD - 1)
                    mm.then_inc(ps.filled(("p", t)), 1)
                pe.wait_ge(*stacked.after(b, T))
                for g in range(NKV):
                    ps.wait_empty(pe, b, ("k", g))
                    for t in range(T):
                        mm = pe.transpose(ps.ap(("k", g))[0:STK, t * P:(t + 1) * P], ks[:, t, g, :], c.ident[:, :])
                    mm.then_inc(ps.filled(("k", g)), 1)
                for s in steps:
                    if s[0] != "o":
                        ps.wait_empty(pe, b, s)
                    if s[0] == "q":
                        for t in range(T):
                            mm = pe.transpose(ps.ap(s)[0:STK, t * P:(t + 1) * P], qs[:, t, s[1], :], c.ident[:, :])
                        mm.then_inc(ps.filled(s), 1)
                    elif s[0] == "s":
                        h, t = s[1:]
                        if t == 0:
                            pe.wait_ge(*ps.released(b, ("q", h)))
                        pe.matmul(ps.ap(s), qT[0:STK, h % NQB, t * P:(t + 1) * P], kT[0:STK, h % NKV, :],
                                  start=True, stop=True).then_inc(ps.filled(s), 1)
                    elif s[0] == "m":
                        h = s[1]
                        for t in (T - 2, T - 1):
                            pe.wait_ge(*ps.released(b, ("s", h, t)))
                        for t in range(T):
                            mm = pe.matmul(ps.ap(s)[STK:P, t * P:(t + 1) * P], nmax[:, h % 2, t, :], c.ident[:, :],
                                           start=True, stop=True)
                        mm.then_inc(ps.filled(s), 1)
                    elif s[0] == "e":
                        h, k = s[1:]
                        if k == 0:
                            pe.wait_ge(*ps.released(b, ("m", h)))
                        pe.matmul(ps.ap(s), kT[:, h % NKV, k * P:(k + 1) * P], qT[:, h % NQB, :],
                                  start=True, stop=True).then_inc(ps.filled(s), 1)
                    elif s[0] == "o":
                        g, k = s[1:]
                        if k == 0:
                            ps.wait_empty(pe, b, ("o", g))
                            for kk in range(T - 3, T):
                                pe.wait_ge(*ps.released(b, ("e", 4 * g + 3, kk)))
                        for src, bank in ((v, 0), (None, 1)):
                            for j in range(4):
                                mm = pe.matmul(ps.ap(("o", g), bank)[j * HD:(j + 1) * HD, :],
                                               c.ones[:, 0:HD] if src is None else v[:, k, j * HD:(j + 1) * HD],
                                               probsT[:, (4 * g + j) % NPB, k, :], start=(k == 0), stop=(k == T - 1))
                        if k == T - 1:
                            mm.then_inc(ps.filled(("o", g)), 1)
                pe.wait_ge(*ps.released(b, ("o", 3)))
                for t in range(T):
                    ps.wait_empty(pe, b, ("y", t))
                    for k in range(KD):
                        mm = pe.matmul(ps.ap(("y", t)), outT[:, k, t * P:(t + 1) * P], wo[:, k, :],
                                       start=(k == 0), stop=(k == KD - 1))
                    mm.then_inc(ps.filled(("y", t)), 1)

        c.close(B)


def rope_parts(dve, qk, ra, rb, cs, t):
    nh = qk.shape[1] // HD
    dve.tensor_tensor(ra[:, :].rearrange("p (h e) -> p h e", h=nh), qk.rearrange("p (h e) -> p h e", h=nh),
                      cs[:, t, 0, :].unsqueeze(1).broadcast_to([P, nh, HD]), ALU.mult)
    q4 = qk.rearrange("p (h e two) -> p h e two", h=nh, two=2)
    b4 = rb[:, :].rearrange("p (h e two) -> p h e two", h=nh, two=2)
    w = cs[:, t, 1, :].rearrange("p (e two) -> p e two", two=2)
    for par in range(2):
        last = dve.tensor_tensor(b4[:, :, :, par], q4[:, :, :, 1 - par],
                                 w[:, :, par].unsqueeze(1).broadcast_to([P, nh, HD // 2]), ALU.mult)
    return last


def similarity_mixing(c):
    nc, d, ps = c.nc, c.d, c.ps
    with ExitStack() as ctx:
        def sb(nm, shape, dt=F32):
            return ctx.enter_context(nc.sbuf_tensor(f"s2_{nm}", shape, dt))

        w = sb("w", [P, 2, KC, DX])
        w_h = sb("w_hi", [P, 2, KC, DX], F32R)
        w_l = sb("w_lo", [P, 2, KC, DX], F32R)
        bias = sb("bias", [P, 2])
        cT = sb("ctxT", [P, B, KC, S])
        c_h = sb("ctxT_hi", [P, KC, S], F32R)
        c_l = sb("ctxT_lo", [P, KC, S], F32R)
        f = sb("proj", [P, 2, S])
        f_h = sb("proj_hi", [P, 2, S], F32R)
        f_l = sb("proj_lo", [P, 2, S], F32R)
        nmax = sb("neg_max", [P, T])
        sums = sb("sums", [P, T])
        inv = sb("inv_sums", [P, T])
        probs = sb("probs", [P, T, S])
        a_h = sb("attT_hi", [P, T, S], F32R)
        a_l = sb("attT_lo", [P, T, S], F32R)

        weights = c.sem("s2_weights_loaded")
        w_hi = c.sem("s2_w_hi_ready")
        w_lo = c.sem("s2_w_lo_ready")
        ctx_hi = Count(c.sem("s2_ctx_hi_ready"), 1)
        ctx_lo = Count(c.sem("s2_ctx_lo_ready"), 1)
        max_ready = Count(c.sem("s2_max_ready"), T)
        normed = Count(c.sem("s2_normed"), T)
        att_hi = Count(c.sem("s2_att_hi_ready"), T)
        pr_hi = c.s2_proj_hi

        ps.open(c.x_uses([2, 3]) + [(("f", j), j, 1) for j in range(2)] + [(("e", t), 4 + t % 2, 1) for t in range(T)]
                + [(("a", k), 6 + k % 2, 1) for k in range(T)] + c.y_uses([0, 1]))
        block = ctx.enter_context(nc.Block())

        @block.sync
        def _(sp):
            for j, (wn, bn) in enumerate((("l0x_wqT", "l0x_bq"), ("l0x_wkT", "l0x_bk"))):
                sp.dma_start(w[:, j, :, :], d[wn].rearrange("(k p) n -> p k n", p=P)).then_inc(weights, 16)
                sp.dma_start(bias[:, j:j + 1], d[bn]).then_inc(weights, 16)
            sp.dma_start(cT[:, :, :, :], d["ctxT"].rearrange("b (k p) s -> p b k s", p=P)).then_inc(weights, 16)
            with sp.Fori(0, B) as b:
                c.sync_load_x(sp, b)

        @block.gpsimd
        def _(pool):
            pool.wait_ge(w_hi, 1)
            pool.tensor_tensor(w_l[:, :, :, :], w[:, :, :, :], w_h[:, :, :, :].bitcast(F32), ALU.subtract) \
                .then_inc(w_lo, 1)
            with pool.Fori(0, B) as b:
                c.pool_rstd(pool, b)

        @block.scalar
        def _(act):
            act.wait_ge(weights, 80)
            act.activation(w_h[:, :, :, :], w[:, :, :, :], ACT.Copy).then_inc(w_hi, 1)
            with act.Fori(0, B) as b:
                act.wait_ge(*pr_hi.after(b, 0))
                act.activation(c_h[:, :, :], cT[:, bass.ds(b, 1), :, :].rearrange("p a k s -> p (a k) s"),
                               ACT.Copy).then_inc(ctx_hi.sem, 1)
                c.act_x_hi(act, b)
                for j in range(2):
                    act.wait_ge(*ps.full(b, ("f", j)))
                    act.activation(f[:, j, :], ps.ap(("f", j)), ACT.Identity, bias=bias[:, j:j + 1])
                    act.activation(f_h[:, j, :], ps.ap(("f", j)), ACT.Identity, bias=bias[:, j:j + 1]) \
                       .then_inc(pr_hi.sem, 1)
                for t in range(T):
                    act.wait_ge(*max_ready.after(b, t + 1))
                    act.activation(probs[:, t, :], ps.ap(("e", t)), ACT.Exp, bias=nmax[:, t:t + 1],
                                   accum_out=sums[:, t:t + 1]).then_inc(ps.freed(("e", t)), 1)
                for k in range(T):
                    act.wait_ge(*ps.full(b, ("a", k)))
                    act.activation(a_h[:, k, :], ps.ap(("a", k)), ACT.Copy).then_inc(att_hi.sem, 1)

        @block.vector
        def _(dve):
            with dve.Fori(0, B) as b:
                dve.wait_ge(*ctx_hi.after(b, 1))
                dve.tensor_tensor(c_l[:, :, :], cT[:, bass.ds(b, 1), :, :].rearrange("p a k s -> p (a k) s"),
                                  c_h[:, :, :].bitcast(F32), ALU.subtract).then_inc(ctx_lo.sem, 1)
                c.dve_x_lo(dve, b)
                for j in range(2):
                    dve.wait_ge(*pr_hi.after(b, j + 1))
                    dve.tensor_tensor(f_l[:, j, :], f[:, j, :], f_h[:, j, :].bitcast(F32), ALU.subtract) \
                       .then_inc(ps.freed(("f", j)), 1)
                for t in range(T):
                    dve.wait_ge(*ps.full(b, ("e", t)))
                    dve.tensor_reduce(nmax[:, t:t + 1], ps.ap(("e", t)), AX.X, ALU.max, negate=True) \
                       .then_inc(max_ready.sem, 1)
                for t in range(T):
                    dve.wait_ge(*ps.released(b, ("e", t)))
                    dve.reciprocal(inv[:, t:t + 1], sums[:, t:t + 1])
                    dve.drain()
                    dve.tensor_scalar(probs[:, t, :], probs[:, t, :], inv[:, t:t + 1], None, ALU.mult) \
                       .then_inc(normed.sem, 1)
                for k in range(T):
                    dve.wait_ge(*att_hi.after(b, k + 1))
                    dve.tensor_tensor(a_l[:, k, :], ps.ap(("a", k)), a_h[:, k, :].bitcast(F32), ALU.subtract) \
                       .then_inc(ps.freed(("a", k)), 1)
                c.dve_layernorm(dve, b)

        @block.tensor
        def _(pe):
            pe.wait_ge(w_lo, 1)
            with pe.Fori(0, B) as b:
                c.pe_turn_x(pe, b)
                pe.wait_ge(*ctx_lo.after(b, 1))
                for j in range(2):
                    ps.wait_empty(pe, b, ("f", j))
                    for k in range(KC):
                        mm = split3(pe, ps.ap(("f", j)), (w_h[:, j, k, :], w_l[:, j, k, :]), (c_h[:, k, :], c_l[:, k, :]),
                                    k == 0, k == KC - 1)
                    mm.then_inc(ps.filled(("f", j)), 1)
                for j in range(2):
                    pe.wait_ge(*ps.released(b, ("f", j)))
                for t in range(T):
                    ps.wait_empty(pe, b, ("e", t))
                    split3(pe, ps.ap(("e", t)), (f_h[:, 0, t * P:(t + 1) * P], f_l[:, 0, t * P:(t + 1) * P]),
                           (f_h[:, 1, :], f_l[:, 1, :]), True, True).then_inc(ps.filled(("e", t)), 1)
                pe.wait_ge(*normed.after(b, T))
                for k in range(T):
                    ps.wait_empty(pe, b, ("a", k))
                    for t in range(T):
                        mm = pe.transpose(ps.ap(("a", k))[:, t * P:(t + 1) * P], probs[:, t, k * P:(k + 1) * P],
                                          c.ident[:, :])
                    mm.then_inc(ps.filled(("a", k)), 1)
                for k in (T - 2, T - 1):
                    pe.wait_ge(*ps.released(b, ("a", k)))
                for t in range(T):
                    ps.wait_empty(pe, b, ("y", t))
                    for k in range(KD):
                        mm = split3(pe, ps.ap(("y", t)), (c.xhi[:, k, t * P:(t + 1) * P], c.xlo[:, k, t * P:(t + 1) * P]),
                                    (a_h[:, k, :], a_l[:, k, :]), k == 0, k == KD - 1)
                    mm.then_inc(ps.filled(("y", t)), 1)

        c.close(B)


def lora_experts(c):
    nc, d, ps = c.nc, c.d, c.ps
    with ExitStack() as ctx:
        def sb(nm, shape, dt=F32):
            return ctx.enter_context(nc.sbuf_tensor(f"s3_{nm}", shape, dt))

        NAG = LORA + NE
        w = sb("w", [P, KD, D])
        w_h = sb("w_hi", [P, KD, D], F32R)
        w_l = sb("w_lo", [P, KD, D], F32R)
        a = sb("ag", [P, KD, NAG])
        a_h = sb("ag_hi", [P, KD, NAG], F32R)
        a_l = sb("ag_lo", [P, KD, NAG], F32R)
        bt = sb("bt", [P, D])
        bt_h = sb("bt_hi", [P, D], F32R)
        bt_l = sb("bt_lo", [P, D], F32R)
        lg = sb("logits", [P, T, 2 * NE])
        rest = sb("logits_rest", [P, T, 2 * NE])
        mask = sb("top_mask", [P, T, NE])
        top = sb("top8", [P, T, 8])
        nmax = sb("neg_max", [P, T])
        ex = sb("exps", [P, T, NE])
        exm = sb("exps_masked", [P, T, NE])
        sums = sb("sums", [P, T])
        inv = sb("inv_sums", [P, T])
        tw = sb("t_weighted", [P, T, LORA])
        tT_h = sb("tT_hi", [P, S], F32R)
        tT_l = sb("tT_lo", [P, S], F32R)

        weights = c.sem("s3_weights_loaded")
        w_hi = c.sem("s3_w_hi_ready")
        w_lo = c.sem("s3_w_lo_ready")
        pad = c.sem("s3_pad_set")
        masked = Count(c.sem("s3_top_found"), 1)
        exps = Count(c.sem("s3_exps_ready"), 1)
        weighted = Count(c.sem("s3_weighted"), 1)
        t_hi = Count(c.sem("s3_tT_hi_ready"), 1)

        ps.open(c.x_uses([2, 3]) + [(("g", t), t, 1) for t in range(T)]
                + [(("tT", 0), 4, 1)] + c.y_uses([5, 6, 7]))
        block = ctx.enter_context(nc.Block())

        @block.sync
        def _(sp):
            sp.dma_start(a[:, :, :], d["l0f_agT"].rearrange("(k p) n -> p k n", p=P)).then_inc(weights, 16)
            sp.dma_start(w[:, :, :], d["l0f_wT"].rearrange("(k p) n -> p k n", p=P)).then_inc(weights, 16)
            sp.dma_start(bt[:, :], d["l0f_bT"]).then_inc(weights, 16)
            with sp.Fori(0, B) as b:
                c.sync_load_x(sp, b)

        @block.gpsimd
        def _(pool):
            pool.memset(lg[:, :, :], LOWEST).then_inc(pad, 1)
            pool.wait_ge(w_hi, 1)
            pool.tensor_tensor(a_l[:, :, :], a[:, :, :], a_h[:, :, :].bitcast(F32), ALU.subtract)
            pool.tensor_tensor(bt_l[:, :], bt[:, :], bt_h[:, :].bitcast(F32), ALU.subtract)
            pool.tensor_tensor(w_l[:, :, :], w[:, :, :], w_h[:, :, :].bitcast(F32), ALU.subtract).then_inc(w_lo, 1)
            with pool.Fori(0, B) as b:
                c.pool_rstd(pool, b)

        @block.scalar
        def _(act):
            act.wait_ge(weights, 48)
            act.activation(a_h[:, :, :], a[:, :, :], ACT.Copy)
            act.activation(w_h[:, :, :], w[:, :, :], ACT.Copy)
            act.activation(bt_h[:, :], bt[:, :], ACT.Copy).then_inc(w_hi, 1)
            with act.Fori(0, B) as b:
                c.act_x_hi(act, b)
                act.wait_ge(*masked.after(b, 1))
                for t in range(T):
                    e = act.activation(ex[:, t, :], lg[:, t, 0:NE], ACT.Exp, bias=nmax[:, t:t + 1])
                e.then_inc(exps.sem, 1)
                act.wait_ge(*ps.full(b, ("tT", 0)))
                act.activation(tT_h[:, :], ps.ap(("tT", 0)), ACT.Copy).then_inc(t_hi.sem, 1)

        @block.vector
        def _(dve):
            dve.wait_ge(pad, 1)
            with dve.Fori(0, B) as b:
                c.dve_x_lo(dve, b)
                for t in range(T):
                    dve.wait_ge(*ps.full(b, ("g", t)))
                    dve.tensor_copy(lg[:, t, 0:NE], ps.ap(("g", t))[:, LORA:NAG])
                dve.drain()
                for t in range(T):
                    dve.max(top[:, t, :], lg[:, t, :])
                dve.drain()
                dve.tensor_scalar(nmax[:, :], top[:, :, 0], -1.0, None, ALU.mult)
                dve.memset(top[:, :, TOPK:], LOWEST)
                dve.drain()
                for t in range(T):
                    dve.match_replace(rest[:, t, :], top[:, t, :], lg[:, t, :], LOWEST)
                dve.drain()
                dve.tensor_tensor(mask[:, :, :], rest[:, :, 0:NE], lg[:, :, 0:NE], ALU.not_equal) \
                   .then_inc(masked.sem, 1)
                dve.wait_ge(*exps.after(b, 1))
                dve.tensor_tensor(exm[:, :, :], ex[:, :, :], mask[:, :, :], ALU.mult)
                dve.drain()
                dve.tensor_reduce(sums[:, :], exm[:, :, :], AX.X, ALU.add)
                dve.drain()
                dve.reciprocal(inv[:, :], sums[:, :])
                dve.drain()
                dve.tensor_scalar(inv[:, :], inv[:, :], LORA_ALPHA, None, ALU.mult)
                dve.drain()
                dve.tensor_tensor(exm[:, :, :], exm[:, :, :], inv[:, :].unsqueeze(2).broadcast_to([P, T, NE]), ALU.mult)
                dve.drain()
                for t in range(T):
                    dve.tensor_tensor(tw[:, t, :].rearrange("p (e r) -> p e r", e=NE),
                                      ps.ap(("g", t))[:, 0:LORA].rearrange("p (e r) -> p e r", e=NE),
                                      exm[:, t, :].unsqueeze(2).broadcast_to([P, NE, RANK]), ALU.mult) \
                       .then_inc(ps.freed(("g", t)), 1)
                dve.wait_ge(*t_hi.after(b, 1))
                dve.tensor_tensor(tT_l[:, :], ps.ap(("tT", 0)), tT_h[:, :].bitcast(F32), ALU.subtract) \
                   .then_inc(ps.freed(("tT", 0)), 1)
                c.dve_layernorm(dve, b)

        @block.tensor
        def _(pe):
            pe.wait_ge(w_lo, 1)
            with pe.Fori(0, B) as b:
                c.pe_turn_x(pe, b)
                c.wait_xT(pe, b)

                def xs(k, t):
                    return c.xhi[:, k, t * P:(t + 1) * P], c.xlo[:, k, t * P:(t + 1) * P]

                for t in range(T):
                    ps.wait_empty(pe, b, ("g", t))
                    for k in range(KD):
                        mm = split3(pe, ps.ap(("g", t))[:, 0:NAG], xs(k, t), (a_h[:, k, :], a_l[:, k, :]),
                                    k == 0, k == KD - 1)
                    mm.then_inc(ps.filled(("g", t)), 1)

                def dense(t):
                    ps.wait_empty(pe, b, ("y", t))
                    for k in range(KD):
                        split3(pe, ps.ap(("y", t)), xs(k, t), (w_h[:, k, :], w_l[:, k, :]), k == 0, False)

                def lora(t):
                    split3(pe, ps.ap(("y", t)), (tT_h[:, t * P:(t + 1) * P], tT_l[:, t * P:(t + 1) * P]),
                           (bt_h[:, :], bt_l[:, :]), False, True).then_inc(ps.filled(("y", t)), 1)

                for t in range(3):
                    dense(t)
                for t in range(T):
                    pe.wait_ge(*ps.released(b, ("g", t)))
                ps.wait_empty(pe, b, ("tT", 0))
                for t in range(T):
                    mm = pe.transpose(ps.ap(("tT", 0))[:, t * P:(t + 1) * P], tw[:, t, :], c.ident[:, :])
                mm.then_inc(ps.filled(("tT", 0)), 1)
                pe.wait_ge(*ps.released(b, ("tT", 0)))
                for t in range(3):
                    lora(t)
                dense(3)
                lora(3)

        c.close(B)


def window_attention(c):
    nc, d, ps = c.nc, c.d, c.ps
    with ExitStack() as ctx:
        def sb(nm, shape, dt=F32):
            return ctx.enter_context(nc.sbuf_tensor(f"s4_{nm}", shape, dt))

        w = sb("wqkv", [P, KD, NQKV])
        w_h = sb("wqkv_hi", [P, KD, NQKV], F32R)
        w_l = sb("wqkv_lo", [P, KD, NQKV], F32R)
        wo = sb("wo", [P, KD, D])
        b_qkv = sb("b_qkv", [P, NQKV])
        b_o = sb("b_o", [P, D])
        gain = sb("qk_gain", [P, 2, HD])
        gmax = sb("gain_max", [P, 2])
        scale = sb("scale", [P, 1])
        bound = sb("minus_bound", [P, 1])
        cs = sb("cos_sin", [P, T, 2, HD])
        csg = sb("cos_sin_gain", [P, 2, T, 2, HD])
        maskf = sb("mask_f32", [P, 4 * P])
        mask = sb("mask", [P, 4 * P], BF16)
        idb = sb("ident_bf16", [P, P], BF16)
        pj = sb("proj", [P, NQKV])
        sq = sb("squares", [P, NQK * HD])
        ms = sb("mean_sq", [P, NQK])
        rs = sb("qk_rstd", [P, NQK])
        ra = sb("rope_a", [P, NQK * HD])
        rb = sb("rope_b", [P, NQK * HD])
        qs = sb("q_stacks", [P, T, NH, STK])
        ks = sb("k_stacks", [P, T, NKV, STK])
        kT = sb("kT", [STK, NKV, S], F32R)
        NQB = 3
        qT = sb("qT", [STK, NQB, S], F32R)
        v = sb("v", [P, T, NK])
        NPB = 8
        probsT = sb("probsT", [P, NPB, 2, S])
        inv = sb("inv_sums", [P, S])
        outT = w[:, :, 0:S]

        weights = c.sem("s4_weights_loaded")
        w_hi = c.sem("s4_w_hi_ready")
        w_lo = c.sem("s4_w_lo_ready")
        tables = c.sem("s4_tables_ready")
        bf_ready = c.sem("s4_mask_bf16_ready")
        squared = Count(c.sem("s4_squared"), T)
        ms_ready = Count(c.sem("s4_mean_sq_ready"), T)
        rs_ready = Count(c.sem("s4_qk_rstd_ready"), T)
        v_out = c.s4_v_out
        roped = c.s4_roped
        r_sum = Count(c.sem("s4_rope_sum"), T)
        r_hi = Count(c.sem("s4_rope_hi"), T)
        stacked = c.s4_stacked

        BLOCKS = [(0, 0), (0, 1), (1, 1), (1, 2), (2, 2), (2, 3), (3, 3)]
        NBL = len(BLOCKS)

        steps = [("q", 0)]
        for i in range(NH + 3):
            if i + 1 < NH:
                steps.append(("q", i + 1))
            if i < NH:
                steps.append(("e", i))
            if i >= 5 and (i - 5) % 4 == 0 and (i - 5) // 4 < 4:
                steps.append(("o", (i - 5) // 4))
        uses = c.x_uses([2, 3]) + [(("p", t), (0, 4)[t % 2], 2) for t in range(T)]
        uses += [(("k", g), 2 + g % 2, 1) for g in range(NKV)]
        for s in steps:
            if s[0] == "q":
                uses.append((s, 2 + s[1] % 2, 1))
            elif s[0] == "e":
                uses.append((s, (0, 4)[s[1] % 2], 2))
            else:
                uses.append((s, 6, 2))
        ps.open(uses + c.y_uses([0, 1, 4, 5]))
        block = ctx.enter_context(nc.Block())

        @block.sync
        def _(sp):
            sp.dma_start(w[:, :, :], d["l1a_wqkvT"].rearrange("(k p) n -> p k n", p=P)).then_inc(weights, 16)
            sp.dma_start(wo[:, :, :], d["l1a_woT"].rearrange("(k p) n -> p k n", p=P)).then_inc(weights, 16)
            sp.dma_start(b_qkv[:, :], d["l1a_bqkv"].broadcast_to([P, NQKV])).then_inc(weights, 16)
            sp.dma_start(b_o[:, :], d["l1a_bo"].broadcast_to([P, D])).then_inc(weights, 16)
            sp.dma_start(gain[:, 0, :], d["l1a_qn"].broadcast_to([P, HD])).then_inc(weights, 16)
            sp.dma_start(gain[:, 1, :], d["l1a_kn"].broadcast_to([P, HD])).then_inc(weights, 16)
            sp.dma_start(scale[:, :], d["l1a_scale"].broadcast_to([P, 1])).then_inc(weights, 16)
            sp.dma_start(cs[:, :, :, :], d["cos_sin_plain"].rearrange("(t p) a n -> p t a n", p=P)).then_inc(weights, 16)
            sp.dma_start(maskf[:, :], d["window_mask"]).then_inc(weights, 16)
            with sp.Fori(0, B) as b:
                c.sync_load_x(sp, b)

        @block.gpsimd
        def _(pool):
            pool.wait_ge(w_hi, 1)
            pool.tensor_tensor(w_l[:, :, :], w[:, :, :], w_h[:, :, :].bitcast(F32), ALU.subtract).then_inc(w_lo, 1)
            with pool.Fori(0, B) as b:
                for t in range(T):
                    pool.wait_ge(*ms_ready.after(b, t + 1))
                    pool.tensor_tensor(rs[:, :], ms[:, :], c.mhalf[:, 0:NQK], ALU.pow).then_inc(rs_ready.sem, 1)
                    pool.wait_ge(*roped.after(b, t + 1))
                    pool.tensor_tensor(ra[:, :], ra[:, :], rb[:, :], ALU.add).then_inc(r_sum.sem, 1)
                    pool.wait_ge(*r_hi.after(b, t + 1))
                    rq = ra[:, 0:D].rearrange("p (h e) -> p h e", e=HD)
                    rk = ra[:, D:].rearrange("p (h e) -> p h e", e=HD)
                    pool.tensor_tensor(qs[:, t, :, 2 * HD:].bitcast(F32R), rq, qs[:, t, :, 0:HD], ALU.subtract)
                    pool.tensor_tensor(ks[:, t, :, HD:2 * HD].bitcast(F32R), rk, ks[:, t, :, 0:HD], ALU.subtract) \
                        .then_inc(stacked.sem, 1)
                c.pool_rstd(pool, b)

        @block.scalar
        def _(act):
            act.wait_ge(weights, 16 * 9)
            act.activation(w_h[:, :, :], w[:, :, :], ACT.Copy).then_inc(w_hi, 1)
            act.activation(idb[:, :], c.ident[:, :], ACT.Copy)
            act.activation(mask[:, :], maskf[:, :], ACT.Copy).then_inc(bf_ready, 1)
            act.wait_ge(tables, 1)
            with act.Fori(0, B) as b:
                c.act_x_hi(act, b)
                for t in range(T):
                    act.wait_ge(*ps.released(b, ("p", t)))
                    act.activation(sq[:, :], pj[:, 0:NQK * HD], ACT.Square).then_inc(squared.sem, 1)
                    act.activation(v[:, t, :], pj[:, NQK * HD:], ACT.Copy).then_inc(v_out.sem, 1)
                    act.wait_ge(*r_sum.after(b, t + 1))
                    rq = ra[:, 0:D].rearrange("p (h e) -> p h e", e=HD)
                    rk = ra[:, D:].rearrange("p (h e) -> p h e", e=HD)
                    act.activation(qs[:, t, :, 0:HD].bitcast(F32R), rq, ACT.Copy)
                    act.activation(qs[:, t, :, HD:2 * HD].bitcast(F32R), rq, ACT.Copy)
                    act.activation(ks[:, t, :, 0:HD].bitcast(F32R), rk, ACT.Copy)
                    act.activation(ks[:, t, :, 2 * HD:].bitcast(F32R), rk, ACT.Copy).then_inc(r_hi.sem, 1)
                for g in range(NKV):
                    act.wait_ge(*ps.full(b, ("k", g)))
                    act.activation(kT[:, g, :], ps.ap(("k", g))[0:STK, :], ACT.Copy).then_inc(ps.freed(("k", g)), 1)
                for s in steps:
                    if s[0] == "e":
                        h = s[1]
                        act.wait_ge(*ps.full(b, s))
                        if h >= NPB and h % 4 == 0:
                            act.wait_ge(*ps.full(b, ("o", (h - NPB) // 4)))
                        act.activation(probsT[:, h % NPB, :, :].rearrange("p a n -> p (a n)")[:, 0:NBL * P],
                                       ps.pair(s).rearrange("p a n -> p (a n)")[:, 0:NBL * P], ACT.Exp,
                                       bias=bound[:, 0:1]).then_inc(ps.freed(s), 1)

        @block.vector
        def _(dve):
            dve.wait_ge(weights, 16 * 9)
            dve.tensor_reduce(gmax[:, :], gain[:, :, :], AX.X, ALU.max, apply_absolute_value=True)
            dve.tensor_tensor(bound[:, :], scale[:, :], scale[:, :], ALU.mult)
            g_even = [gain[:, j, :].rearrange("p (e two) -> p e two", two=2) for j in range(2)]
            for j in range(2):
                dve.tensor_tensor(csg[:, j, :, 0, :], cs[:, :, 0, :], gain[:, j, :].unsqueeze(1).broadcast_to([P, T, HD]),
                                  ALU.mult)
                for par in range(2):
                    out = csg[:, j, :, 1, :].rearrange("p t (e two) -> p t e two", two=2)[:, :, :, par]
                    src = cs[:, :, 1, :].rearrange("p t (e two) -> p t e two", two=2)[:, :, :, par]
                    dve.tensor_tensor(out, src, g_even[j][:, :, 1 - par].unsqueeze(1).broadcast_to([P, T, HD // 2]),
                                      ALU.mult)
            dve.drain()
            dve.tensor_scalar(csg[:, 0, :, :, :], csg[:, 0, :, :, :], scale[:, 0:1], None, ALU.mult)
            dve.tensor_scalar(ms[:, 0:1], scale[:, :], -1.0, None, ALU.mult)
            dve.drain()
            dve.tensor_tensor(ms[:, 0:1], ms[:, 0:1], scale[:, :], ALU.min)
            dve.tensor_tensor(gmax[:, 0:1], gmax[:, 0:1], gmax[:, 1:2], ALU.mult)
            dve.drain()
            dve.tensor_tensor(bound[:, :], ms[:, 0:1], gmax[:, 0:1], ALU.mult)
            dve.drain()
            dve.tensor_scalar(bound[:, :], bound[:, :], float(HD), None, ALU.mult).then_inc(tables, 1)
            dve.wait_ge(tables, 1)
            with dve.Fori(0, B) as b:
                dve.wait_ge(*c.cur.after(b, 16))
                xb = c.x[:, bass.ds(b * T, T), :]
                dve.tensor_tensor(xb, xb, b_o[:, :].unsqueeze(1).broadcast_to([P, T, D]), ALU.add)
                c.dve_x_lo(dve, b)
                for t in range(T):
                    dve.wait_ge(*ps.full(b, ("p", t)))
                    dve.wait_ge(*v_out.after(b, t))
                    dve.wait_ge(*roped.after(b, t))
                    dve.tensor_tensor(pj[:, :], ps.pair(("p", t)).rearrange("p a n -> p (a n)")[:, 0:NQKV],
                                      b_qkv[:, :], ALU.add).then_inc(ps.freed(("p", t)), 1)
                    dve.wait_ge(*squared.after(b, t + 1))
                    dve.tensor_reduce(ms[:, :], sq[:, :].rearrange("p (h e) -> p h e", e=HD), AX.X, ALU.add)
                    dve.drain()
                    dve.tensor_scalar(ms[:, :], ms[:, :], 1.0 / HD, 1e-8, ALU.mult, ALU.add).then_inc(ms_ready.sem, 1)
                    dve.wait_ge(*rs_ready.after(b, t + 1))
                    qk = pj[:, 0:NQK * HD]
                    dve.tensor_tensor(qk.rearrange("p (h e) -> p h e", e=HD), qk.rearrange("p (h e) -> p h e", e=HD),
                                      rs[:, :].unsqueeze(2).broadcast_to([P, NQK, HD]), ALU.mult)
                    dve.drain()
                    dve.wait_ge(*stacked.after(b, t))
                    rope_parts(dve, qk[:, 0:D], ra[:, 0:D], rb[:, 0:D], csg[:, 0, :, :, :], t)
                    rope_parts(dve, qk[:, D:], ra[:, D:], rb[:, D:], csg[:, 1, :, :, :], t).then_inc(roped.sem, 1)
                for s in steps:
                    if s[0] == "q":
                        h = s[1]
                        dve.wait_ge(*ps.full(b, s))
                        if h >= NQB:
                            dve.wait_ge(*ps.full(b, ("e", h - NQB)))
                        dve.tensor_copy(qT[:, h % NQB, :], ps.ap(s)[0:STK, :]).then_inc(ps.freed(s), 1)
                    elif s[0] == "o":
                        g = s[1]
                        dve.wait_ge(*ps.full(b, s))
                        dve.reciprocal(inv[:, :], ps.ap(s, 1))
                        dve.drain()
                        dve.tensor_tensor(outT[:, g, :], ps.ap(s), inv[:, :], ALU.mult).then_inc(ps.freed(s), 1)
                c.dve_layernorm(dve, b)

        @block.tensor
        def _(pe):
            pe.wait_ge(w_lo, 1)
            pe.wait_ge(bf_ready, 1)
            with pe.Fori(0, B) as b:
                c.pe_turn_x(pe, b)
                c.wait_xT(pe, b)
                for t in range(T):
                    ps.wait_empty(pe, b, ("p", t))
                    for lo, hi, j in ((0, D, 0), (D, NQKV, 1)):
                        for k in range(KD):
                            mm = split3(pe, ps.ap(("p", t), j)[:, 0:hi - lo],
                                        (c.xhi[:, k, t * P:(t + 1) * P], c.xlo[:, k, t * P:(t + 1) * P]),
                                        (w_h[:, k, lo:hi], w_l[:, k, lo:hi]), k == 0, k == KD - 1)
                    mm.then_inc(ps.filled(("p", t)), 1)
                pe.wait_ge(*stacked.after(b, T))
                for g in range(NKV):
                    ps.wait_empty(pe, b, ("k", g))
                    for t in range(T):
                        mm = pe.transpose(ps.ap(("k", g))[0:STK, t * P:(t + 1) * P], ks[:, t, g, :], c.ident[:, :])
                    mm.then_inc(ps.filled(("k", g)), 1)
                for s in steps:
                    ps.wait_empty(pe, b, s)
                    if s[0] == "q":
                        for t in range(T):
                            mm = pe.transpose(ps.ap(s)[0:STK, t * P:(t + 1) * P], qs[:, t, s[1], :], c.ident[:, :])
                        mm.then_inc(ps.filled(s), 1)
                    elif s[0] == "e":
                        h = s[1]
                        pe.wait_ge(*ps.released(b, ("q", h)))
                        for j, n in ((0, 4), (1, NBL - 4)):
                            pe.matmul(ps.ap(s, j)[:, 0:n * P], idb[:, :], mask[:, 0:n * P], start=True, stop=False)
                        i = 0
                        for k in range(T):
                            n = 2 if k < T - 1 else 1
                            mm = pe.matmul(ps.ap(s, i // 4)[:, i % 4 * P:(i % 4 + n) * P],
                                           kT[:, h // 4, k * P:(k + 1) * P],
                                           qT[:, h % NQB, k * P:(k + n) * P], start=False, stop=k % 2 == 1)
                            i += n
                        mm.then_inc(ps.filled(s), 1)
                    elif s[0] == "o":
                        g = s[1]
                        for kk in (2, 3):
                            pe.wait_ge(*ps.released(b, ("e", 4 * g + kk)))
                        for t in range(T):
                            blocks = [(i, kt) for i, (kt, qt) in enumerate(BLOCKS) if qt == t]
                            for m, (i, kt) in enumerate(blocks):
                                for src, bank in ((v, 0), (None, 1)):
                                    for j in range(4):
                                        mm = pe.matmul(ps.ap(s, bank)[j * HD:(j + 1) * HD, t * P:(t + 1) * P],
                                                       c.ones[:, 0:HD] if src is None else v[:, kt, g * HD:(g + 1) * HD],
                                                       probsT[:, (4 * g + j) % NPB, i // 4, i % 4 * P:(i % 4 + 1) * P],
                                                       start=(m == 0), stop=(m == len(blocks) - 1))
                        mm.then_inc(ps.filled(s), 1)
                pe.wait_ge(*ps.released(b, ("o", 3)))
                for t in range(T):
                    ps.wait_empty(pe, b, ("y", t))
                    for k in range(KD):
                        mm = pe.matmul(ps.ap(("y", t)), outT[:, k, t * P:(t + 1) * P], wo[:, k, :],
                                       start=(k == 0), stop=(k == KD - 1))
                    mm.then_inc(ps.filled(("y", t)), 1)

        c.close(B)


def cross_attention(c):
    nc, d, ps = c.nc, c.d, c.ps
    HP = 2
    G = 16 // HP
    NW = HP * DX
    with ExitStack() as ctx:
        def sb(nm, shape, dt=F32):
            return ctx.enter_context(nc.sbuf_tensor(f"s5_{nm}", shape, dt))

        OQ, OKV, OO = 0, KD * NW, KD * NW + KC * 2 * NW
        NALL = OO + HP * D
        raw = sb("w_raw", [P, NALL])
        w_h = sb("w_hi", [P, 2, NALL], F32R)
        w_l = sb("w_lo", [P, 2, NALL], F32R)
        gains = sb("gains", [P, 2, DX])
        gk = sb("gain_product", [P, DX])
        gmax = sb("gain_max", [P, 1])
        bound = sb("minus_bound", [P, 1])
        cT = sb("ctxT", [P, KC, S])
        c_h = sb("ctxT_hi", [P, KC, S], F32R)
        c_l = sb("ctxT_lo", [P, KC, S], F32R)
        q = sb("q", [P, T, NW])
        kk = sb("k", [P, T, NW])
        v = sb("v", [P, T, NW])
        sq = sb("squares", [P, T, NW])
        ms = sb("mean_sq", [P, 2, T, HP])
        rs = sb("qk_rstd", [P, 2, T, HP])
        f_h = sb("qkT_hi", [P, 2, HP, S], F32R)
        f_l = sb("qkT_lo", [P, 2, HP, S], F32R)
        probsT = sb("probsT", [P, HP, T, S])
        psum2 = sb("probs_pair_sum", [P, 2, S])
        inv = sb("inv_sums", [P, S])
        o = sb("outT", [P, HP, S])
        o_h = sb("outT_hi", [P, HP, S], F32R)
        o_l = sb("outT_lo", [P, HP, S], F32R)

        consts = c.sem("s5_gains_loaded")
        bound_ready = c.sem("s5_bound_ready")
        raw_in = Count(c.sem("s5_weights_loaded"), 64)
        w_hi = Count(c.sem("s5_w_hi_ready"), 1)
        w_lo = Count(c.sem("s5_w_lo_ready"), 1)
        ctx_in = Count(c.sem("s5_ctx_loaded"), 16)
        ctx_hi = Count(c.sem("s5_ctx_hi_ready"), 1)
        ctx_lo = c.s5_ctx_lo
        squared = Count(c.sem("s5_squared"), 2)
        summed = Count(c.sem("s5_squares_summed"), 2)
        rs_ready = Count(c.sem("s5_qk_rstd_ready"), 2)
        q_normed = Count(c.sem("s5_q_normed"), 1)
        k_normed = Count(c.sem("s5_k_normed"), 1)
        k_gained = Count(c.sem("s5_k_gained"), 1)
        f_hi = Count(c.sem("s5_qkT_hi_ready"), 2 * HP)
        p_sum = Count(c.sem("s5_probs_summed"), HP)
        o_ready = Count(c.sem("s5_out_ready"), HP)
        o_hi = Count(c.sem("s5_out_hi_ready"), HP)
        o_lo = Count(c.sem("s5_out_lo_ready"), HP)
        y_added = Count(c.sem("s5_y_added"), 1)

        uses = [(("kv", t), t, 1) for t in range(T)] + [(("q", i), 4 + i, 1) for i in range(2)]
        uses += [(("kT", h), 6 + h, 1) for h in range(HP)] + [(("qT", h), h, 1) for h in range(HP)]
        for h in range(HP):
            uses += [(("e", h, k), 2 + k, 1) for k in range(T)]
            uses += [(("o", h), 6, 2)]
        uses += [(("y", t), t % 2, 1) for t in range(T)]
        ps.open(uses, outer=c.x_uses([0, 1]))
        block = ctx.enter_context(nc.Block())

        def load_weights(sp, g):
            sp.dma_start(raw[:, OQ:OKV].rearrange("p (k n) -> p k n", k=KD),
                         d["l1x_wq"].rearrange("(k p) n -> p k n", p=P)[:, :, bass.ds(g * NW, NW)]).then_inc(raw_in.sem, 16)
            kv = raw[:, OKV:OO].rearrange("p (k a n) -> p k a n", k=KC, a=2)
            for a, nm in ((0, "l1x_wk"), (1, "l1x_wv")):
                sp.dma_start(kv[:, :, a, :],
                             d[nm].rearrange("(k p) n -> p k n", p=P)[:, :, bass.ds(g * NW, NW)]).then_inc(raw_in.sem, 16)
            sp.dma_start(raw[:, OO:].rearrange("p (h n) -> p h n", h=HP),
                         d["l1x_wo"].rearrange("(h p) n -> p h n", p=P)[:, bass.ds(g * HP, HP), :]).then_inc(raw_in.sem, 16)

        @block.sync
        def _(sp):
            sp.dma_start(gains[:, 0, :], d["l1x_gq"].broadcast_to([P, DX])).then_inc(consts, 16)
            sp.dma_start(gains[:, 1, :], d["l1x_gk"].broadcast_to([P, DX])).then_inc(consts, 16)
            load_weights(sp, 0)
            with sp.Fori(0, B) as b:
                c.sync_load_x(sp, b)
                sp.wait_ge(*ctx_lo.after(b, 0))
                sp.dma_start(cT[:, :, :], d["ctxT"][bass.ds(b, 1)].rearrange("a (k p) s -> p (a k) s", p=P)) \
                  .then_inc(ctx_in.sem, 16)
                with sp.Fori(0, G) as g:
                    turn = b * G + g
                    sp.wait_ge(*w_lo.after(turn, 1))
                    load_weights(sp, (g + 1) % G)

        @block.gpsimd
        def _(pool):
            def weights_lo(turn, par):
                pool.wait_ge(*w_hi.after(turn, 1))
                pool.tensor_tensor(w_l[:, par, :], raw[:, :], w_h[:, par, :].bitcast(F32), ALU.subtract) \
                    .then_inc(w_lo.sem, 1)
            weights_lo(0, 0)
            with pool.Fori(0, B) as b:
                with pool.Fori(0, G) as g:
                    turn = b * G + g
                    for j in range(2):
                        pool.wait_ge(*summed.after(turn, j + 1))
                        pool.tensor_tensor(rs[:, j, :, :], ms[:, j, :, :],
                                           c.mhalf[:, 0:T * HP].rearrange("p (t h) -> p t h", h=HP), ALU.pow) \
                            .then_inc(rs_ready.sem, 1)
                        if j == 0:
                            pool.wait_ge(*k_normed.after(turn, 1))
                            k3 = kk[:, :, :].rearrange("p t (h n) -> p (t h) n", h=HP)
                            pool.tensor_tensor(k3, k3, gk[:, :].unsqueeze(1).broadcast_to([P, T * HP, DX]), ALU.mult) \
                                .then_inc(k_gained.sem, 1)
                    pool.wait_ge(*w_hi.after(turn, 2))
                    pool.wait_ge(c.pool_consts, 1)
                    pool.tensor_tensor(w_l[:, bass.ds((turn + 1) % 2, 1), :].rearrange("p a n -> p (a n)"), raw[:, :],
                                       w_h[:, bass.ds((turn + 1) % 2, 1), :].rearrange("p a n -> p (a n)").bitcast(F32),
                                       ALU.subtract).then_inc(w_lo.sem, 1)
                    for h in range(HP):
                        for k in (T - 2, T - 1):
                            pool.wait_ge(*ps.released((b, turn), ("e", h, k)))
                        if h > 0:
                            pool.wait_ge(*ps.full((b, turn), ("o", h - 1)))
                        pool.tensor_tensor(psum2[:, :, :], probsT[:, h, 0:2, :], probsT[:, h, 2:4, :], ALU.add)
                        pool.drain()
                        pool.tensor_tensor(psum2[:, 0, :], psum2[:, 0, :], psum2[:, 1, :], ALU.add).then_inc(p_sum.sem, 1)
                c.pool_rstd(pool, b)

        @block.scalar
        def _(act):
            act.wait_ge(*raw_in.after(0, 64))
            act.activation(w_h[:, 0, :], raw[:, :], ACT.Copy).then_inc(w_hi.sem, 1)
            act.wait_ge(bound_ready, 1)
            with act.Fori(0, B) as b:
                c.act_x_hi(act, b, (b, b * G))
                act.wait_ge(*ctx_in.after(b, 16))
                act.activation(c_h[:, :, :], cT[:, :, :], ACT.Copy).then_inc(ctx_hi.sem, 1)
                with act.Fori(0, G) as g:
                    turn = b * G + g
                    bt = (b, turn)
                    for t in range(T):
                        act.wait_ge(*ps.full(bt, ("kv", t)))
                        act.activation(kk[:, t, :], ps.ap(("kv", t))[:, 0:NW], ACT.Copy)
                        s = act.activation(sq[:, t, :], ps.ap(("kv", t))[:, 0:NW], ACT.Square)
                        act.activation(v[:, t, :], ps.ap(("kv", t))[:, NW:], ACT.Copy).then_inc(ps.freed(("kv", t)), 1)
                        if t == T - 1:
                            s.then_inc(squared.sem, 1)
                    act.wait_ge(*summed.after(turn, 1))
                    for i in range(2):
                        act.wait_ge(*ps.full(bt, ("q", i)))
                        s = act.activation(sq[:, 2 * i:2 * i + 2, :].rearrange("p t n -> p (t n)"), ps.ap(("q", i)),
                                           ACT.Square)
                        if i == 1:
                            s.then_inc(squared.sem, 1)
                        act.activation(q[:, 2 * i:2 * i + 2, :].rearrange("p t n -> p (t n)"), ps.ap(("q", i)), ACT.Copy) \
                           .then_inc(ps.freed(("q", i)), 1)
                    for j, nm in enumerate(("kT", "qT")):
                        for h in range(HP):
                            act.wait_ge(*ps.full(bt, (nm, h)))
                            act.activation(f_h[:, j, h, :], ps.ap((nm, h)), ACT.Copy).then_inc(f_hi.sem, 1)
                    act.wait_ge(*raw_in.after(turn, 128))
                    act.activation(w_h[:, bass.ds((turn + 1) % 2, 1), :].rearrange("p a n -> p (a n)"), raw[:, :],
                                   ACT.Copy).then_inc(w_hi.sem, 1)
                    for h in range(HP):
                        for k in range(T):
                            act.wait_ge(*ps.full(bt, ("e", h, k)))
                            act.activation(probsT[:, h, k, :], ps.ap(("e", h, k)), ACT.Exp, bias=bound[:, 0:1],
                                           scale=DX ** -0.5).then_inc(ps.freed(("e", h, k)), 1)
                    for h in range(HP):
                        act.wait_ge(*o_ready.after(turn, h + 1))
                        act.activation(o_h[:, h, :], o[:, h, :], ACT.Copy).then_inc(o_hi.sem, 1)

        @block.vector
        def _(dve):
            dve.wait_ge(consts, 32)
            dve.tensor_tensor(gk[:, :], gains[:, 0, :], gains[:, 1, :], ALU.mult)
            dve.drain()
            dve.tensor_reduce(gmax[:, :], gk[:, :], AX.X, ALU.max, apply_absolute_value=True)
            dve.drain()
            dve.tensor_scalar(bound[:, :], gmax[:, :], -DX ** 0.5, None, ALU.mult).then_inc(bound_ready, 1)
            with dve.Fori(0, B) as b:
                c.dve_x_lo(dve, b, (b, b * G))
                dve.wait_ge(*ctx_hi.after(b, 1))
                dve.tensor_tensor(c_l[:, :, :], cT[:, :, :], c_h[:, :, :].bitcast(F32), ALU.subtract).then_inc(ctx_lo.sem, 1)
                with dve.Fori(0, G) as g:
                    turn = b * G + g
                    bt = (b, turn)
                    for j, (x_, done) in enumerate(((kk, k_normed), (q, q_normed))):
                        dve.wait_ge(*squared.after(turn, j + 1))
                        dve.tensor_reduce(ms[:, j, :, :], sq[:, :, :].rearrange("p t (h n) -> p t h n", h=HP), AX.X, ALU.add)
                        dve.drain()
                        dve.tensor_scalar(ms[:, j, :, :], ms[:, j, :, :], 1.0 / DX, 1e-5, ALU.mult, ALU.add) \
                           .then_inc(summed.sem, 1)
                        dve.wait_ge(*rs_ready.after(turn, j + 1))
                        if j == 0:
                            dve.wait_ge(*ps.released(bt, ("kv", T - 1)))
                        else:
                            dve.wait_ge(*ps.released(bt, ("q", 1)))
                        x3 = x_[:, :, :].rearrange("p t (h n) -> p (t h) n", h=HP)
                        dve.tensor_tensor(x3, x3, rs[:, j, :, :].rearrange("p t h -> p (t h)").unsqueeze(2)
                                          .broadcast_to([P, T * HP, DX]), ALU.mult).then_inc(done.sem, 1)
                    for j, nm in enumerate(("kT", "qT")):
                        for h in range(HP):
                            dve.wait_ge(*f_hi.after(turn, j * HP + h + 1))
                            dve.tensor_tensor(f_l[:, j, h, :], ps.ap((nm, h)), f_h[:, j, h, :].bitcast(F32), ALU.subtract) \
                               .then_inc(ps.freed((nm, h)), 1)
                    for h in range(HP):
                        dve.wait_ge(*ps.full(bt, ("o", h)))
                        dve.reciprocal(inv[:, :], ps.ap(("o", h), 1))
                        dve.drain()
                        dve.tensor_tensor(o[:, h, :], ps.ap(("o", h)), inv[:, :], ALU.mult).then_inc(ps.freed(("o", h)), 1)
                        dve.drain()
                        dve.nop().then_inc(o_ready.sem, 1)
                        dve.wait_ge(*o_hi.after(turn, h + 1))
                        dve.tensor_tensor(o_l[:, h, :], o[:, h, :], o_h[:, h, :].bitcast(F32), ALU.subtract) \
                           .then_inc(o_lo.sem, 1)
                    for t in range(T):
                        xt = c.x[:, b * T + t, :]
                        dve.wait_ge(*ps.full(bt, ("y", t)))
                        dve.tensor_tensor(xt, ps.ap(("y", t)), xt, ALU.add).then_inc(ps.freed(("y", t)), 1)
                dve.drain()
                for t in range(T):
                    dve.bn_stats(c.stats[:, t, :], c.x[:, b * T + t, :])
                c.dve_normalize(dve, b)

        @block.tensor
        def _(pe):
            with pe.Fori(0, B) as b:
                c.pe_turn_x(pe, b, (b, b * G))
                with pe.Fori(0, G) as g:
                    turn = b * G + g
                    bt = (b, turn)
                    pe.wait_ge(*ctx_lo.after(b, 1))

                    def w(off, n):
                        return tuple(a[:, bass.ds(turn % 2, 1), off:off + n].rearrange("p a n -> p (a n)")
                                     for a in (w_h, w_l))

                    pe.wait_ge(*w_lo.after(turn, 1))
                    for t in range(T):
                        ps.wait_empty(pe, bt, ("kv", t))
                        for k in range(KC):
                            mm = split3(pe, ps.ap(("kv", t)), (c_h[:, k, t * P:(t + 1) * P], c_l[:, k, t * P:(t + 1) * P]),
                                        w(OKV + k * 2 * NW, 2 * NW), k == 0, k == KC - 1)
                        mm.then_inc(ps.filled(("kv", t)), 1)
                    for i in range(2):
                        ps.wait_empty(pe, bt, ("q", i))
                        for t in (2 * i, 2 * i + 1):
                            for k in range(KD):
                                mm = split3(pe, ps.ap(("q", i))[:, t % 2 * NW:(t % 2 + 1) * NW],
                                            (c.xhi[:, k, t * P:(t + 1) * P], c.xlo[:, k, t * P:(t + 1) * P]),
                                            w(OQ + k * NW, NW), k == 0, k == KD - 1)
                        mm.then_inc(ps.filled(("q", i)), 1)
                    for nm, src, done in (("kT", kk, k_gained), ("qT", q, q_normed)):
                        pe.wait_ge(*done.after(turn, 1))
                        for h in range(HP):
                            ps.wait_empty(pe, bt, (nm, h))
                            for t in range(T):
                                mm = pe.transpose(ps.ap((nm, h))[:, t * P:(t + 1) * P], src[:, t, h * DX:(h + 1) * DX],
                                                  c.ident[:, :])
                            mm.then_inc(ps.filled((nm, h)), 1)
                    for h in range(HP):
                        for nm in ("kT", "qT"):
                            pe.wait_ge(*ps.released(bt, (nm, h)))
                        for k in range(T):
                            ps.wait_empty(pe, bt, ("e", h, k))
                            split3(pe, ps.ap(("e", h, k)), (f_h[:, 0, h, k * P:(k + 1) * P], f_l[:, 0, h, k * P:(k + 1) * P]),
                                   (f_h[:, 1, h, :], f_l[:, 1, h, :]), True, True).then_inc(ps.filled(("e", h, k)), 1)
                    for h in range(HP):
                        ps.wait_empty(pe, bt, ("o", h))
                        for k in range(T):
                            pe.wait_ge(*ps.released(bt, ("e", h, k)))
                            pe.matmul(ps.ap(("o", h)), v[:, k, h * DX:(h + 1) * DX], probsT[:, h, k, :],
                                      start=(k == 0), stop=(k == T - 1))
                        pe.wait_ge(*p_sum.after(turn, h + 1))
                        pe.matmul(ps.ap(("o", h), 1), c.ones[:, :], psum2[:, 0, :], start=True, stop=True) \
                          .then_inc(ps.filled(("o", h)), 1)
                    pe.wait_ge(*o_lo.after(turn, HP))
                    for t in range(T):
                        ps.wait_empty(pe, bt, ("y", t))
                        for h in range(HP):
                            mm = split3(pe, ps.ap(("y", t)), (o_h[:, h, t * P:(t + 1) * P], o_l[:, h, t * P:(t + 1) * P]),
                                        w(OO + h * D, D), h == 0, h == HP - 1)
                        mm.then_inc(ps.filled(("y", t)), 1)

        c.close(B * G, B)


def workspace_rounds(c):
    nc, d, ps = c.nc, c.d, c.ps
    g = Buffers()
    with ExitStack() as ctx:
        def sb(nm, shape, dt=F32):
            return ctx.enter_context(nc.sbuf_tensor(f"s6_{nm}", shape, dt))

        g.xw = sb("x_work", [P, B * T, D])
        g.cw = sb("compete", [P, KD, SB])
        g.cw_h = sb("compete_hi", [P, KD, SB], F32R)
        g.cw_l = sb("compete_lo", [P, KD, SB], F32R)
        g.cb = sb("compete_b", [P, 1])
        g.pre = sb("pre_w", [P, KD])
        g.ww, g.wk, g.wv, g.wq, g.wo = (sb(nm, [P, KD, D]) for nm in ("write_w", "wk", "wv", "wq", "wo"))
        g.wb, g.post, g.ob = (sb(nm, [P, D]) for nm in ("write_b", "post_w", "out_b"))
        g.bqkv = sb("b_qkv", [P, 3, NP])
        g.bq_rep = sb("bq_replicated", [P, NP, P])
        g.junk = sb("squares", [P, T, D])
        g.ssq = sb("sum_sq", [P, T])
        g.ms = sb("mean_sq", [P, T])
        g.rs = sb("row_rstd", [P, T])
        g.ltok = sb("slot_logits_by_token", [P, T, B * SB])
        g.lrow = sb("slot_logits", [P, S + 8])
        g.rest = sb("slot_logits_rest", [P, S + 8])
        g.mask = sb("top_mask", [P, S])
        g.top = sb("top8", [P, 8])
        g.nmax = sb("neg_max", [P, 1])
        g.ssum = sb("row_sum", [P, 1])
        g.gw = sb("slot_weights", [P, S])
        g.gt = sb("slot_weights_by_token", [P, T, B * SB])
        g.gx = sb("gathered", [P, D])
        g.gxT = sb("gatheredT", [P, KD, B * SB])
        g.ws = sb("slots", [P, D])
        g.wsn = sb("slots_new", [P, D])
        g.wsT = sb("slotsT", [P, KD, B * SB])
        g.bdk = sb("kkT_by_head", [P, NP, B, SB])
        g.bdv = sb("vvT_by_head", [P, NP, B, SB])
        g.m_h = sb("folded_k_hi", [P, KD, B, P], F32R)
        g.m_l = sb("folded_k_lo", [P, KD, B, P], F32R)
        g.lb = sb("logit_bias", [P, B, P])
        g.u = sb("folded_v", [P, B, D])
        g.lg = sb("token_logits", [P, T, P])
        g.mx8 = sb("token_max", [P, T * H6])
        g.att = sb("att", [P, T, P])
        g.attT = sb("attT", [P, S])

        def cnt(name, per=1):
            return Count(c.sem("s6_" + name), per)

        weights = c.sem("s6_weights_loaded")
        consts = c.sem("s6_constants_set")
        cw_hi_s, cw_lo_s = c.sem("s6_compete_hi_ready"), c.sem("s6_compete_lo_ready")
        g.ssq_ready = c.s6_ssq
        g.ms_ready = c.s6_ms
        g.rs_ready = cnt("x_rstd_ready")
        g.top_found, g.exps, g.weighted = cnt("top_found"), cnt("slot_exps_ready"), cnt("slot_weights_ready")
        g.ws_sum, g.ws_sq, g.ws_ms, g.ws_rs, g.ws_ready = (cnt(x) for x in (
            "slots_added", "slots_squared", "slots_mean_sq_ready", "slots_rstd_ready", "slots_ready"))
        g.m_hi = cnt("folded_k_hi_ready", KD)
        g.shifted, g.att_exps, g.att_ready = cnt("token_logits_shifted"), cnt("token_exps_ready"), cnt("att_ready")
        g.added = cnt("y_added", T)

        with ExitStack() as blk:
            block = blk.enter_context(nc.Block())

            @block.sync
            def _(sp):
                for dst, nm in ((g.ww, "l1f_wwT"), (g.wk, "l1f_wkT"), (g.wv, "l1f_wvT"), (g.wq, "l1f_wq"), (g.wo, "l1f_woT")):
                    sp.dma_start(dst[:, :, :], d[nm].rearrange("(k p) n -> p k n", p=P)).then_inc(weights, 16)
                for dst, nm in ((g.wb, "l1f_wb"), (g.post, "l1f_post"), (g.ob, "l1f_ob")):
                    sp.dma_start(dst[:, :], d[nm].broadcast_to([P, D])).then_inc(weights, 16)
                for j, nm in enumerate(("l1f_bq", "l1f_bk", "l1f_bv")):
                    sp.dma_start(g.bqkv[:, j, :], d[nm]).then_inc(weights, 16)
                sp.dma_start(g.pre[:, :], d["l1f_pre"]).then_inc(weights, 16)
                sp.wait_ge(consts, 2)
                sp.dma_start(g.cw[:, :, 0:NS], d["l1f_cwT"].rearrange("(k p) n -> p k n", p=P)).then_inc(weights, 16)
                for b in range(B):
                    sp.dma_start(g.cb[b * SB:b * SB + NS, :], d["l1f_cb"]).then_inc(weights, 16)
                    sp.dma_start(g.ws[b * SB:b * SB + NS, :], d["l1f_ws"]).then_inc(weights, 16)
                sp.wait_ge(weights, 16 * 21)

            @block.gpsimd
            def _(pool):
                for tns in (g.cw[:, :, :], g.cb[:, :], g.ws[:, :]):
                    pool.memset(tns, 0.0)
                    pool.drain()
                pool.memset(g.lrow[:, :], LOWEST).then_inc(consts, 1)

            @block.vector
            def _(dve):
                dve.memset(g.bdk[:, :, :, :], 0.0)
                dve.memset(g.bdv[:, :, :, :], 0.0).then_inc(consts, 1)
                dve.wait_ge(weights, 16 * 21)
                for k in range(KD):
                    dve.tensor_scalar(g.cw[:, k, :], g.cw[:, k, :], g.pre[:, k:k + 1], None, ALU.mult)
                    dve.tensor_scalar(g.bq_rep[:, k, :], c.ones[:, :], g.bqkv[:, 0, k:k + 1], None, ALU.mult)
                dve.drain()
                dve.tensor_copy(g.cw_h[:, :, :], g.cw[:, :, :])
                dve.drain()
                dve.tensor_tensor(g.cw_l[:, :, :], g.cw[:, :, :], g.cw_h[:, :, :].bitcast(F32), ALU.subtract).then_inc(cw_lo_s, 1)
                dve.wait_ge(cw_lo_s, 1)

        for r in range(2):
            g.src = c.x if r == 0 else g.xw
            g.last_round = r == 1
            workspace_collect(c, g)
            workspace_slots(c, g)
            workspace_attend(c, g)




def pow_rstd(c, pool, out, src, n):
    return pool.tensor_tensor(out, src, c.mhalf[:, 0:n], ALU.pow)


def workspace_collect(c, g):
    nc, ps = c.nc, c.ps
    ps.open(c.x_uses([0, 1]) + [(("l", 0), 2, 1)])
    with ExitStack() as ctx:
        block = ctx.enter_context(nc.Block())

        @block.sync
        def _(sp):
            with sp.Fori(0, B) as b:
                c.sync_load_x(sp, b, g.src, g.ssq_ready)

        @block.gpsimd
        def _(pool):
            with pool.Fori(0, B) as b:
                pool.wait_ge(*g.ms_ready.after(b, 1))
                pow_rstd(c, pool, g.rs[:, :], g.ms[:, :], T).then_inc(g.rs_ready.sem, 1)

        @block.scalar
        def _(act):
            with act.Fori(0, B) as b:
                c.act_x_hi(act, b)
                act.wait_ge(*g.ms_ready.after(b, 0))
                for t in range(T):
                    s = act.activation(g.junk[:, t, :], c.xcur[:, t, :], ACT.Square, accum_out=g.ssq[:, t:t + 1])
                s.then_inc(g.ssq_ready.sem, 1)

        @block.vector
        def _(dve):
            with dve.Fori(0, B) as b:
                c.dve_x_lo(dve, b)
                dve.wait_ge(*g.ssq_ready.after(b, 1))
                dve.tensor_scalar(g.ms[:, :], g.ssq[:, :], 1.0 / D, EPS6, ALU.mult, ALU.add).then_inc(g.ms_ready.sem, 1)
                dve.wait_ge(*ps.full(b, ("l", 0)))
                dve.wait_ge(*g.rs_ready.after(b, 1))
                dve.tensor_tensor(g.ltok[:, :, bass.ds(b * SB, SB)],
                                  ps.ap(("l", 0))[:, 0:T * SB].rearrange("p (t s) -> p t s", t=T),
                                  g.rs[:, :].unsqueeze(2).broadcast_to([P, T, SB]), ALU.mult).then_inc(ps.freed(("l", 0)), 1)

        @block.tensor
        def _(pe):
            with pe.Fori(0, B) as b:
                c.pe_turn_x(pe, b)
                c.wait_xT(pe, b)
                ps.wait_empty(pe, b, ("l", 0))
                for t in range(T):
                    for k in range(KD):
                        mm = split3(pe, ps.ap(("l", 0))[:, t * SB:(t + 1) * SB],
                                    (c.xhi[:, k, t * P:(t + 1) * P], c.xlo[:, k, t * P:(t + 1) * P]),
                                    (g.cw_h[:, k, :], g.cw_l[:, k, :]), k == 0, k == KD - 1)
                mm.then_inc(ps.filled(("l", 0)), 1)

    ps.close(B)
    for x in (c.cur, c.xT_hi, g.ssq_ready, g.ms_ready, g.rs_ready):
        x.close(B)


def workspace_slots(c, g):
    nc, ps = c.nc, c.ps
    BS = B * SB
    banks = [("L", 0), ("G", 1), ("gx", 2), ("gxT", 3), ("w", 4), ("wsT", 5), ("k", 6), ("v", 7)]
    banks += [(("m", m), m) for m in range(KD)] + [("lb", 4)] + [(("u", b), (5, 6, 7, 0)[b]) for b in range(B)]
    ps.open([(k, bank, 1) for k, bank in banks])

    with ExitStack() as ctx:
        block = ctx.enter_context(nc.Block())

        @block.gpsimd
        def _(pool):
            pool.wait_ge(*g.ws_ms.after(0, 1))
            pow_rstd(c, pool, g.rs[:, 0:1], g.ms[:, 0:1], 1).then_inc(g.ws_rs.sem, 1)

        @block.scalar
        def _(act):
            act.wait_ge(*ps.full(0, "L"))
            act.activation(g.lrow[:, 0:S], ps.ap("L"), ACT.Identity, bias=g.cb[:, 0:1]).then_inc(ps.freed("L"), 1)
            act.wait_ge(*g.top_found.after(0, 1))
            act.activation(g.gw[:, :], g.lrow[:, 0:S], ACT.Exp, bias=g.nmax[:, 0:1]).then_inc(g.exps.sem, 1)
            act.wait_ge(*ps.full(0, "gx"))
            act.activation(g.gx[:, :], ps.ap("gx"), ACT.Copy).then_inc(ps.freed("gx"), 1)
            act.wait_ge(*g.ws_sum.after(0, 1))
            act.activation(g.junk[:, 0, :], g.wsn[:, :], ACT.Square, accum_out=g.ssq[:, 0:1]).then_inc(g.ws_sq.sem, 1)
            act.wait_ge(*ps.full(0, "wsT"))
            act.activation(g.wsT[:, :, :].rearrange("p k n -> p (k n)"), ps.ap("wsT"), ACT.Copy) \
               .then_inc(ps.freed("wsT"), 1)
            for m in range(KD):
                act.wait_ge(*ps.full(0, ("m", m)))
                act.activation(g.m_h[:, m, :, :].rearrange("p b (q n) -> p q b n", q=NP),
                               ps.ap(("m", m)).rearrange("p (q b n) -> p q b n", q=NP, b=B), ACT.Copy) \
                   .then_inc(g.m_hi.sem, 1)
            for b in range(B):
                act.wait_ge(*ps.full(0, ("u", b)))
                act.activation(g.u[:, b, :], ps.ap(("u", b)), ACT.Copy).then_inc(ps.freed(("u", b)), 1)

        @block.vector
        def _(dve):
            dve.wait_ge(*ps.released(0, "L"))
            dve.max(g.top[:, :], g.lrow[:, :])
            dve.drain()
            dve.tensor_scalar(g.nmax[:, :], g.top[:, 0:1], -1.0, None, ALU.mult)
            dve.memset(g.top[:, K6:], LOWEST)
            dve.drain()
            dve.match_replace(g.rest[:, :], g.top[:, :], g.lrow[:, :], LOWEST)
            dve.drain()
            dve.tensor_tensor(g.mask[:, :], g.rest[:, 0:S], g.lrow[:, 0:S], ALU.not_equal).then_inc(g.top_found.sem, 1)
            dve.wait_ge(*g.exps.after(0, 1))
            dve.wait_ge(*g.top_found.after(0, 1))
            dve.tensor_tensor(g.gw[:, :], g.gw[:, :], g.mask[:, :], ALU.mult)
            dve.drain()
            dve.tensor_reduce(g.ssum[:, :], g.gw[:, :], AX.X, ALU.add)
            dve.drain()
            dve.reciprocal(g.ssum[:, :], g.ssum[:, :])
            dve.drain()
            dve.tensor_scalar(g.gw[:, :], g.gw[:, :], g.ssum[:, 0:1], None, ALU.mult).then_inc(g.weighted.sem, 1)
            dve.wait_ge(*ps.full(0, "G"))
            dve.tensor_copy(g.gt[:, :, :].rearrange("p t n -> p (t n)"), ps.ap("G")).then_inc(ps.freed("G"), 1)
            dve.wait_ge(*ps.full(0, "gxT"))
            dve.tensor_copy(g.gxT[:, :, :].rearrange("p t n -> p (t n)"), ps.ap("gxT")).then_inc(ps.freed("gxT"), 1)
            dve.wait_ge(*ps.full(0, "w"))
            dve.tensor_tensor(g.wsn[:, :], ps.ap("w"), g.wb[:, :], ALU.add).then_inc(ps.freed("w"), 1)
            dve.drain()
            dve.tensor_tensor(g.wsn[:, :], g.wsn[:, :], g.ws[:, :], ALU.add).then_inc(g.ws_sum.sem, 1)
            dve.wait_ge(*g.ws_sq.after(0, 1))
            dve.tensor_scalar(g.ms[:, 0:1], g.ssq[:, 0:1], 1.0 / D, EPS6, ALU.mult, ALU.add).then_inc(g.ws_ms.sem, 1)
            dve.wait_ge(*g.ws_rs.after(0, 1))
            dve.tensor_scalar(g.ws[:, :], g.wsn[:, :], g.rs[:, 0:1], None, ALU.mult)
            dve.drain()
            dve.tensor_tensor(g.ws[:, :], g.ws[:, :], g.post[:, :], ALU.mult).then_inc(g.ws_ready.sem, 1)
            for key, dst, j in (("k", g.bdk, 1), ("v", g.bdv, 2)):
                dve.wait_ge(*ps.full(0, key))
                for hh in range(2):
                    rows = slice(hh * W6, (hh + 1) * W6)
                    o = dve.tensor_tensor(dst[rows, :, :, hh * NS:(hh + 1) * NS],
                                          ps.ap(key)[rows, :].rearrange("p (q b n) -> p q b n", q=NP, b=B)[:, :, :, 0:NS],
                                          g.bqkv[rows, j, :].unsqueeze(2).unsqueeze(3).broadcast_to([W6, NP, B, NS]),
                                          ALU.add)
                o.then_inc(ps.freed(key), 1)
            for m in range(KD):
                dve.wait_ge(*g.m_hi.after(0, m + 1))
                dve.tensor_tensor(g.m_l[:, m, :, :].rearrange("p b (q n) -> p q b n", q=NP),
                                  ps.ap(("m", m)).rearrange("p (q b n) -> p q b n", q=NP, b=B),
                                  g.m_h[:, m, :, :].bitcast(F32).rearrange("p b (q n) -> p q b n", q=NP), ALU.subtract) \
                   .then_inc(ps.freed(("m", m)), 1)
            dve.wait_ge(*ps.full(0, "lb"))
            dve.tensor_copy(g.lb[:, :, :].rearrange("p b (q n) -> p q b n", q=NP),
                            ps.ap("lb").rearrange("p (q b n) -> p q b n", q=NP, b=B)).then_inc(ps.freed("lb"), 1)

        @block.tensor
        def _(pe):
            def transposes(key, src_of):
                for t in range(T):
                    mm = pe.transpose(ps.ap(key)[:, t * P:(t + 1) * P], src_of(t), c.ident[:, :])
                mm.then_inc(ps.filled(key), 1)

            transposes("L", lambda t: g.ltok[:, t, :])
            pe.wait_ge(*g.weighted.after(0, 1))
            transposes("G", lambda t: g.gw[:, t * P:(t + 1) * P])
            pe.wait_ge(*ps.released(0, "G"))
            for t in range(T):
                for b in range(B):
                    mm = pe.matmul(ps.ap("gx")[b * SB:(b + 1) * SB, :], g.gt[:, t, b * SB:(b + 1) * SB],
                                   g.src[:, b * T + t, :], start=(t == 0), stop=(t == T - 1))
            mm.then_inc(ps.filled("gx"), 1)
            pe.wait_ge(*ps.released(0, "gx"))
            transposes("gxT", lambda t: g.gx[:, t * P:(t + 1) * P])
            pe.wait_ge(*ps.released(0, "gxT"))
            for k in range(KD):
                mm = pe.matmul(ps.ap("w"), g.gxT[:, k, :], g.ww[:, k, :], start=(k == 0), stop=(k == KD - 1))
            mm.then_inc(ps.filled("w"), 1)
            pe.wait_ge(*g.ws_ready.after(0, 1))
            transposes("wsT", lambda t: g.ws[:, t * P:(t + 1) * P])
            pe.wait_ge(*ps.released(0, "wsT"))
            for key, w in (("k", g.wk), ("v", g.wv)):
                for p in range(NP):
                    for k in range(KD):
                        mm = pe.matmul(ps.ap(key)[:, p * P:(p + 1) * P], w[:, k, p * P:(p + 1) * P], g.wsT[:, k, :],
                                       start=(k == 0), stop=(k == KD - 1))
                mm.then_inc(ps.filled(key), 1)
            pe.wait_ge(*ps.released(0, "k"))
            for m in range(KD):
                for p in range(NP):
                    mm = pe.matmul(ps.ap(("m", m))[:, p * P:(p + 1) * P], g.wq[:, p, m * P:(m + 1) * P],
                                   g.bdk[:, p, :, :].rearrange("p b n -> p (b n)"), start=True, stop=True)
                mm.then_inc(ps.filled(("m", m)), 1)
            for p in range(NP):
                mm = pe.matmul(ps.ap("lb")[:, p * P:(p + 1) * P], g.bq_rep[:, p, :],
                               g.bdk[:, p, :, :].rearrange("p b n -> p (b n)"), start=True, stop=True)
            mm.then_inc(ps.filled("lb"), 1)
            pe.wait_ge(*ps.released(0, "v"))
            for b in range(B):
                if b == 3:
                    ps.wait_empty(pe, 0, ("u", b))
                for p in range(NP):
                    mm = pe.matmul(ps.ap(("u", b))[p * SB:(p + 1) * SB, :], g.bdv[:, p, b, :], g.wo[:, p, :],
                                   start=True, stop=True)
                mm.then_inc(ps.filled(("u", b)), 1)

    ps.close(1)
    for x in (g.top_found, g.exps, g.weighted, g.ws_sum, g.ws_sq, g.ws_ms, g.ws_rs, g.ws_ready, g.m_hi):
        x.close(1)


def workspace_attend(c, g):
    nc, ps = c.nc, c.ps
    ps.open(c.x_uses([0, 1]) + [(("l", 0), 2, 1), (("aT", 0), 3, 1)] + c.y_uses([4, 5, 6, 7]))

    def heads(ap):
        return ap.rearrange("p t (h n) -> p (t h) n", n=NS)

    with ExitStack() as ctx:
        block = ctx.enter_context(nc.Block())

        @block.sync
        def _(sp):
            with sp.Fori(0, B) as b:
                c.sync_load_x(sp, b, g.src)

        @block.gpsimd
        def _(pool):
            with pool.Fori(0, B) as b:
                pool.wait_ge(*g.ms_ready.after(b, 1))
                pow_rstd(c, pool, g.rs[:, :], g.ms[:, :], T).then_inc(g.rs_ready.sem, 1)
                if g.last_round:
                    c.pool_rstd(pool, b)

        @block.scalar
        def _(act):
            with act.Fori(0, B) as b:
                c.act_x_hi(act, b)
                act.wait_ge(*g.shifted.after(b, 1))
                act.activation(g.att[:, :, :], g.lg[:, :, :], ACT.Exp, scale=W6 ** -0.5).then_inc(g.att_exps.sem, 1)
                act.wait_ge(*ps.full(b, ("aT", 0)))
                act.activation(g.attT[:, :], ps.ap(("aT", 0)), ACT.Copy).then_inc(ps.freed(("aT", 0)), 1)
                act.wait_ge(*g.ms_ready.after(b, 0))
                for t in range(T):
                    act.wait_ge(*g.added.after(b, t + 1))
                    s = act.activation(g.junk[:, t, :], g.xw[:, bass.ds(b * T + t, 1), :].rearrange("p a n -> p (a n)"),
                                       ACT.Square, accum_out=g.ssq[:, t:t + 1])
                s.then_inc(g.ssq_ready.sem, 1)

        @block.vector
        def _(dve):
            with dve.Fori(0, B) as b:
                c.dve_x_lo(dve, b)
                dve.wait_ge(*ps.full(b, ("l", 0)))
                dve.tensor_tensor(g.lg[:, :, :], ps.ap(("l", 0)).rearrange("p (t n) -> p t n", t=T),
                                  g.lb[:, bass.ds(b, 1), :].broadcast_to([P, T, P]), ALU.add).then_inc(ps.freed(("l", 0)), 1)
                dve.drain()
                dve.tensor_reduce(g.mx8[:, :], heads(g.lg[:, :, :]), AX.X, ALU.max)
                dve.drain()
                dve.tensor_tensor(heads(g.lg[:, :, :]), heads(g.lg[:, :, :]),
                                  g.mx8[:, :].unsqueeze(2).broadcast_to([P, T * H6, NS]), ALU.subtract) \
                   .then_inc(g.shifted.sem, 1)
                dve.wait_ge(*g.att_exps.after(b, 1))
                dve.tensor_reduce(g.mx8[:, :], heads(g.att[:, :, :]), AX.X, ALU.add)
                dve.drain()
                dve.reciprocal(g.mx8[:, :], g.mx8[:, :])
                dve.drain()
                dve.tensor_tensor(heads(g.att[:, :, :]), heads(g.att[:, :, :]),
                                  g.mx8[:, :].unsqueeze(2).broadcast_to([P, T * H6, NS]), ALU.mult) \
                   .then_inc(g.att_ready.sem, 1)
                for t in range(T):
                    xt = g.xw[:, b * T + t, :]
                    dve.wait_ge(*ps.full(b, ("y", t)))
                    dve.tensor_tensor(xt, ps.ap(("y", t)), g.src[:, b * T + t, :], ALU.add).then_inc(ps.freed(("y", t)), 1)
                    dve.drain()
                    dve.tensor_tensor(xt, xt, g.ob[:, :], ALU.add).then_inc(g.added.sem, 1)
                dve.wait_ge(*g.ssq_ready.after(b, 1))
                dve.tensor_scalar(g.ms[:, :], g.ssq[:, :], 1.0 / D, EPS6, ALU.mult, ALU.add).then_inc(g.ms_ready.sem, 1)
                dve.wait_ge(*g.rs_ready.after(b, 1))
                for t in range(T):
                    xt = g.xw[:, b * T + t, :]
                    dve.tensor_scalar(xt, xt, g.rs[:, t:t + 1], None, ALU.mult)
                    dve.drain()
                    dve.tensor_tensor(xt, xt, g.post[:, :], ALU.mult)
                    if g.last_round:
                        dve.drain()
                        xo = c.x[:, b * T + t, :]
                        dve.tensor_tensor(xo, xo, xt, ALU.add)
                        dve.drain()
                        dve.bn_stats(c.stats[:, t, :], xo)
                if g.last_round:
                    c.dve_normalize(dve, b)

        @block.tensor
        def _(pe):
            with pe.Fori(0, B) as b:
                c.pe_turn_x(pe, b)
                c.wait_xT(pe, b)
                ps.wait_empty(pe, b, ("l", 0))
                for t in range(T):
                    for k in range(KD):
                        rhs = tuple(a[:, k, bass.ds(b, 1), :].rearrange("p a n -> p (a n)") for a in (g.m_h, g.m_l))
                        mm = split3(pe, ps.ap(("l", 0))[:, t * P:(t + 1) * P],
                                    (c.xhi[:, k, t * P:(t + 1) * P], c.xlo[:, k, t * P:(t + 1) * P]),
                                    rhs, k == 0, k == KD - 1)
                mm.then_inc(ps.filled(("l", 0)), 1)
                pe.wait_ge(*g.att_ready.after(b, 1))
                ps.wait_empty(pe, b, ("aT", 0))
                for t in range(T):
                    mm = pe.transpose(ps.ap(("aT", 0))[:, t * P:(t + 1) * P], g.att[:, t, :], c.ident[:, :])
                mm.then_inc(ps.filled(("aT", 0)), 1)
                pe.wait_ge(*ps.released(b, ("aT", 0)))
                for t in range(T):
                    ps.wait_empty(pe, b, ("y", t))
                    pe.matmul(ps.ap(("y", t)), g.attT[:, t * P:(t + 1) * P],
                              g.u[:, bass.ds(b, 1), :].rearrange("p a n -> p (a n)"), start=True, stop=True) \
                      .then_inc(ps.filled(("y", t)), 1)

    ps.close(B)
    for x in (c.cur, c.xT_hi, g.ssq_ready, g.ms_ready, g.rs_ready, g.shifted, g.att_exps, g.att_ready, g.added):
        x.close(B)
    if g.last_round:
        c.var_ready.close(B)
        c.rstd_ready.close(B)


def store_x(c, out):
    with ExitStack() as ctx:
        stored = c.sem("out_stored")
        block = ctx.enter_context(c.nc.Block())

        @block.sync
        def _(sp):
            for b in range(B):
                sp.dma_start(out[b].rearrange("(t p) d -> p t d", p=P), c.x[:, b * T:(b + 1) * T, :]).then_inc(stored, 16)
            sp.wait_ge(stored, 16 * B)


STAGES = [rope_attention, similarity_mixing, lora_experts, window_attention, cross_attention, workspace_rounds]


def build(nc, d, out, stages=STAGES):
    with ExitStack() as ctx:
        c = Core(nc, ctx, d)
        with ExitStack() as s:
            c.start(s)
        for stage in stages:
            stage(c)
        store_x(c, out)


def rope_tables(s, hd, scale):
    half = hd // 2
    freqs = np.float32(1.0) / np.float32(10000.0) ** (np.arange(half, dtype=np.float32) / np.float32(half))
    angles = np.arange(s, dtype=np.float32)[:, None] * freqs[None, :]
    cos, sin = np.cos(angles) * np.float32(scale), np.sin(angles) * np.float32(scale)
    out = np.zeros((s, 2, hd), np.float32)
    out[:, 0, 0::2], out[:, 0, 1::2] = cos, cos
    out[:, 1, 0::2], out[:, 1, 1::2] = -sin, sin
    return out


def window_mask():
    k, q = np.arange(P)[:, None], np.arange(P)[None, :]
    own = np.where((k <= q) & (q - k <= WIN), 0.0, NEG)
    nxt = np.where(q + P - k <= WIN, 0.0, NEG)
    return np.concatenate([own, nxt, own, nxt], 1).astype(np.float32)


def layout(i):
    def f(a):
        return np.ascontiguousarray(a)

    def row(a):
        return f(a.reshape(1, -1))

    def column(a):
        return f(a.reshape(-1, 1))

    def columns(a):
        return f(a.reshape(-1, P).T)

    w, ib = i['L1_ffn_in_proj_w'], i['L1_ffn_in_proj_b']
    return {
        'x': f(i['x']), 'ident': np.eye(P, dtype=np.float32),
        'cos_sin': rope_tables(S, HD, HD ** -0.25), 'cos_sin_plain': rope_tables(S, HD, 1.0),
        'window_mask': window_mask(),
        'l0a_wqkv': f(np.concatenate([i['L0_attn_W_q'], i['L0_attn_W_k'], i['L0_attn_W_v']], 1)),
        'l0a_wo': f(i['L0_attn_W_o']),
        'ctxT': f(i['ctx_1024'].transpose(0, 2, 1)),
        'l0x_wqT': f(i['L0_xattn_Wq'].T), 'l0x_bq': column(i['L0_xattn_bq']),
        'l0x_wkT': f(i['L0_xattn_Wk'].T), 'l0x_bk': column(i['L0_xattn_bk']),
        'l0f_wT': f(i['L0_ffn_weight'].T),
        'l0f_agT': f(np.concatenate([i['L0_ffn_A_w'].reshape(LORA, D), i['L0_ffn_gate_w']], 0).T),
        'l0f_bT': f(i['L0_ffn_B_w'].transpose(0, 2, 1).reshape(LORA, D)),
        'l1a_wqkvT': f(np.concatenate([i['L1_attn_Wq'], i['L1_attn_Wk'], i['L1_attn_Wv']], 0).T),
        'l1a_bqkv': row(np.concatenate([i['L1_attn_bq'], i['L1_attn_bk'], i['L1_attn_bv']])),
        'l1a_woT': f(i['L1_attn_Wo'].T), 'l1a_bo': row(i['L1_attn_bo']),
        'l1a_qn': row(i['L1_attn_qn_w']), 'l1a_kn': row(i['L1_attn_kn_w']),
        'l1a_scale': f(i['L1_attn_scale'].reshape(1, 1)),
        'l1x_wq': f(i['L1_xattn_Wq']), 'l1x_wk': f(i['L1_xattn_Wk']), 'l1x_wv': f(i['L1_xattn_Wv']),
        'l1x_wo': f(i['L1_xattn_Wo']), 'l1x_gq': row(i['L1_xattn_gq']), 'l1x_gk': row(i['L1_xattn_gk']),
        'l1f_ws': f(i['L1_ffn_workspace']), 'l1f_cwT': f(i['L1_ffn_compete_w'].T),
        'l1f_cb': column(i['L1_ffn_compete_b']),
        'l1f_wwT': f(i['L1_ffn_write_w'].T), 'l1f_wb': row(i['L1_ffn_write_b']),
        'l1f_wq': f(w[0:D]), 'l1f_wkT': f(w[D:2 * D].T), 'l1f_wvT': f(w[2 * D:].T),
        'l1f_bq': columns(ib[0:D]), 'l1f_bk': columns(ib[D:2 * D]), 'l1f_bv': columns(ib[2 * D:]),
        'l1f_woT': f(i['L1_ffn_out_proj_w'].T), 'l1f_ob': row(i['L1_ffn_out_proj_b']),
        'l1f_pre': columns(i['L1_ffn_norm_pre_w']), 'l1f_post': row(i['L1_ffn_norm_post_w']),
    }


def kernel(**inputs):
    import concourse.bacc as bacc
    from concourse.bass_utils import run_bass_kernel_spmd

    arrays = layout({name: np.asarray(a) for name, a in inputs.items()})
    nc = bacc.Bacc("TRN2", target_bir_lowering=False, num_devices=1)
    d = {name: nc.dram_tensor(name, a.shape, mybir.dt.from_np(a.dtype), kind="ExternalInput").ap()
         for name, a in arrays.items()}
    out = nc.dram_tensor("out", (B, S, D), F32, kind="ExternalOutput").ap()
    build(nc, d, out)
    return run_bass_kernel_spmd(nc, [arrays], core_ids=[0]).results[0]["out"]
```

```python
from contextlib import ExitStack

import numpy as np

import concourse.bass as bass
from concourse import mybir

P = 128
B, S, D = 4, 512, 512
T = S // P
KD = D // P
NH, HD, NKV = 16, 32, 4
NQK = NH + NKV
NK = NKV * HD
NQKV = D + 2 * NK
STK = 3 * HD
DC = 256
KC = DC // P
DX = 128
NE, RANK, TOPK = 8, 16, 2
LORA = NE * RANK
LORA_ALPHA = 16.0
WIN = 64
NS = 16
H6, W6 = 8, 64
NP = H6 // 2
SB = 32
K6 = 4
EPS6 = 1e-6
NEG = -30000.0
LOWEST = -3.0e38

F32 = mybir.dt.float32
F32R = mybir.dt.float32r
BF16 = mybir.dt.bfloat16
ALU = mybir.AluOpType
ACT = mybir.ActivationFunctionType
AX = mybir.AxisListType


class Count:

    def __init__(self, sem, per=0):
        self.sem, self.base, self.per = sem, 0, per

    def open(self, per):
        self.per = per

    def after(self, turn, k):
        return self.sem, turn * self.per + (self.base + k)

    def close(self, turns):
        self.base += turns * self.per


class Buffers:
    pass


class Banks:

    def __init__(self, tensor, filled, freed, base=None):
        self.t, self.filled_sems, self.freed_sems = tensor, filled, freed
        self.base = [0] * 8 if base is None else base
        self.base_freed = 1

    def part(self):
        return Banks(self.t, self.filled_sems, self.freed_sems, self.base)

    def open(self, uses, outer=()):
        self.outer, self.outer_per = {}, [0] * 8
        for key, bank, width in outer:
            self.outer[key] = (bank, width, self.outer_per[bank])
            self.outer_per[bank] += 1
        self.use, self.per = {}, [0] * 8
        last = {}
        before = {}
        for key, bank, width in uses:
            assert key not in self.use
            before[key] = [last.get(k) for k in range(bank, bank + width)]
            self.use[key] = (bank, width, self.per[bank])
            self.per[bank] += 1
            for k in range(bank, bank + width):
                last[k] = key
        self.before = {key: [p if p is not None else ("wrap", last[self.use[key][0] + i])
                             for i, p in enumerate(ps)] for key, ps in before.items()}

    def open_segments(self, segments):
        self.outer, self.outer_per = {}, [0] * 8
        self.use, self.per, self.segment, self.seg_per, self.before = {}, [0] * 8, {}, {}, {}
        for seg, uses in segments.items():
            per, last = [0] * 8, {}
            for key, bank, width in uses:
                assert key not in self.use
                covered = range(bank, bank + width)
                self.before[key] = [last.get(k, ("wrap", k)) for k in covered]
                self.use[key], self.segment[key] = (bank, width, per[bank]), seg
                per[bank] += 1
                for k in covered:
                    last[k] = key
            self.seg_per[seg] = per
            self.per = [a + n for a, n in zip(self.per, per)]
        self.cover = {k: {k} for k in range(8)}
        for bank, width, _ in self.use.values():
            for k in range(bank, bank + width):
                self.cover[k].add(bank)

    def where(self, key):
        return self.outer[key] if key in self.outer else self.use[key]

    def ap(self, key, j=0):
        return self.t[:, self.where(key)[0] + j, :]

    def pair(self, key):
        bank, width, _ = self.where(key)
        return self.t[:, bank:bank + width, :]

    def filled(self, key):
        return self.filled_sems[self.where(key)[0]]

    def freed(self, key):
        return self.freed_sems[self.where(key)[0]]

    def count(self, turn, bank, inner):
        if not isinstance(turn, tuple):
            return turn * self.per[bank] + self.base[bank]
        if isinstance(turn[1], dict):
            return turn[0] * self.per[bank] + (self.base[bank] + sum(n * self.seg_per[s][bank] for s, n in turn[1].items()))
        o = self.outer_per[bank]
        n = self.base[bank] + (o if inner else 0)
        return turn[1] * self.per[bank] + turn[0] * o + n if o else turn[1] * self.per[bank] + n

    def full(self, turn, key):
        bank, _, i = self.where(key)
        return self.filled_sems[bank], self.count(turn, bank, key in self.use) + (i + 1)

    def released(self, turn, key):
        bank, _, i = self.where(key)
        return self.freed_sems[bank], self.count(turn, bank, key in self.use) + (i + 1 + self.base_freed)

    def wait_empty(self, pe, turn, key):
        if key in self.outer:
            bank, _, i = self.outer[key]
            pe.wait_ge(self.freed_sems[bank], self.count(turn, bank, False) + (i + self.base_freed))
            return
        seen = set()
        for p in self.before[key]:
            if p in seen:
                continue
            seen.add(p)
            if p[0] == "wrap" and isinstance(turn, tuple) and isinstance(turn[1], dict):
                for bank in sorted(self.cover[p[1]]):
                    if ("bank", bank) not in seen and self.per[bank]:
                        seen.add(("bank", bank))
                        pe.wait_ge(self.freed_sems[bank], self.count(turn, bank, True) + self.base_freed)
                continue
            if p[0] == "wrap":
                bank = self.use[p[1]][0]
                pe.wait_ge(self.freed_sems[bank], self.count(turn, bank, True) + self.base_freed)
            else:
                pe.wait_ge(*self.released(turn, p))

    def close(self, turns, outer_turns=0):
        for k in range(8):
            self.base[k] += turns * self.per[k] + outer_turns * self.outer_per[k]


def split3(pe, out, lhs, rhs, start, stop):
    pe.matmul(out, lhs[0], rhs[0], start=start, stop=False)
    pe.matmul(out, lhs[0], rhs[1], start=False, stop=False)
    return pe.matmul(out, lhs[1], rhs[0], start=False, stop=stop)


class Core:

    def __init__(self, nc, ctx, d):
        self.nc, self.d = nc, d

        def sem(name):
            return ctx.enter_context(nc.semaphore(name))

        def sb(name, shape, dt=F32):
            return ctx.enter_context(nc.sbuf_tensor(name, shape, dt))

        def primed(name, per):
            count = Count(sem(name), per)
            count.base = 1
            self.prime.append(count.sem)
            return count

        self.sem, self.prime = sem, []
        self.x = sb("x_all", [P, B * T, D])
        self.xcur = sb("x_cur", [P, T, D])
        self.xhi = sb("xT_hi", [P, KD, S], F32R)
        self.xlo = sb("xT_lo", [P, KD, S], F32R)
        self.ident = sb("ident_sb", [P, P])
        self.ones = sb("ones_sb", [P, P])
        self.mhalf = sb("minus_half", [P, 128])
        self.stats = sb("ln_stats", [P, T, 6])
        self.mv = sb("ln_mean_var", [P, T, 2])
        self.veps = sb("ln_var_eps", [P, T])
        self.rstd = sb("ln_rstd", [P, T])
        self.ps = Banks(ctx.enter_context(nc.psum_tensor("banks", [P, 8, 512], F32)),
                        [sem(f"bank{i}_filled") for i in range(8)], [sem(f"bank{i}_freed") for i in range(8)])
        self.cur = Count(sem("x_cur_loaded"), 16)
        self.xT_hi = primed("xT_hi_ready", KD)
        self.var_ready = Count(sem("ln_var_ready"), 1)
        self.rstd_ready = Count(sem("ln_rstd_ready"), 1)
        self.prime += self.ps.freed_sems
        self.s1_stacked, self.s4_stacked = primed("s1_stacked", T), primed("s4_stacked", T)
        self.s2_proj_hi = primed("s2_proj_hi_ready", 2)
        self.s4_v_out, self.s4_roped = primed("s4_v_out", T), primed("s4_rope_parts", T)
        self.s5_ctx_lo = primed("s5_ctx_lo_ready", 1)
        self.s6_ssq, self.s6_ms = primed("s6_x_squares_summed", 1), primed("s6_x_mean_sq_ready", 1)
        self.consts = sem("consts_loaded")
        self.pool_consts = sem("pool_consts_set")

    def start(self, stage):
        block = stage.enter_context(self.nc.Block())

        @block.sync
        def _(sp):
            for b in range(B):
                sp.dma_start(self.x[:, b * T:(b + 1) * T, :], self.d["x"][b].rearrange("(t p) d -> p t d", p=P)) \
                  .then_inc(self.consts, 16)
            sp.dma_start(self.ident[:, :], self.d["ident"]).then_inc(self.consts, 16)
            sp.wait_ge(self.consts, 16 * (B + 1))

        @block.gpsimd
        def _(pool):
            pool.memset(self.mhalf[:, :], -0.5)
            pool.memset(self.ones[:, :], 1.0).then_inc(self.pool_consts, 1)
            for s in self.prime:
                pool.nop().then_inc(s, 1)
            pool.wait_ge(self.pool_consts, 1)

    def x_uses(self, banks):
        return [(("x", k), banks[k % len(banks)], 1) for k in range(KD)]

    def close(self, turns):
        self.ps.close(turns)
        self.close_common()

    def close_common(self):
        for c in (self.cur, self.xT_hi, self.var_ready, self.rstd_ready):
            c.close(B)

    def sync_load_x(self, sp, b, src=None, read=None):
        src = self.x if src is None else src
        sp.wait_ge(*(self.xT_hi if read is None else read).after(b, 0))
        sp.dma_start(self.xcur[:, :, :], src[:, bass.ds(b * T, T), :]).then_inc(self.cur.sem, 16)

    def pe_turn_x(self, pe, b, turn=None, ps=None):
        ps = self.ps if ps is None else ps
        turn = b if turn is None else turn
        pe.wait_ge(*self.cur.after(b, 16))
        for k in range(KD):
            ps.wait_empty(pe, turn, ("x", k))
            for t in range(T):
                mm = pe.transpose(ps.ap(("x", k))[:, t * P:(t + 1) * P],
                                  self.xcur[:, t, k * P:(k + 1) * P], self.ident[:, :])
            mm.then_inc(ps.filled(("x", k)), 1)

    def act_x_hi(self, act, b, turn=None, ps=None):
        ps = self.ps if ps is None else ps
        turn = b if turn is None else turn
        for k in range(KD):
            act.wait_ge(*ps.full(turn, ("x", k)))
            act.activation(self.xhi[:, k, :], ps.ap(("x", k)), ACT.Copy).then_inc(self.xT_hi.sem, 1)

    def dve_x_lo(self, dve, b, turn=None, ps=None):
        ps = self.ps if ps is None else ps
        turn = b if turn is None else turn
        for k in range(KD):
            dve.wait_ge(*self.xT_hi.after(b, k + 1))
            dve.tensor_tensor(self.xlo[:, k, :], ps.ap(("x", k)),
                              self.xhi[:, k, :].bitcast(F32), ALU.subtract).then_inc(ps.freed(("x", k)), 1)

    def wait_xT(self, pe, turn):
        for k in range(KD):
            pe.wait_ge(*self.ps.released(turn, ("x", k)))

    def y_uses(self, banks):
        return [(("y", t), banks[t % len(banks)], 1) for t in range(T)]

    def dve_layernorm(self, dve, b, pos=None, between=None):
        pos = b if pos is None else pos
        for t in range(T):
            xt = self.x[:, b * T + t, :]
            dve.wait_ge(*self.ps.full(pos, ("y", t)))
            dve.tensor_tensor(xt, self.ps.ap(("y", t)), xt, ALU.add).then_inc(self.ps.freed(("y", t)), 1)
            dve.drain()
            dve.bn_stats(self.stats[:, t, :], xt)
        if between is not None:
            between()
        self.dve_normalize(dve, b)

    def dve_normalize(self, dve, b, eps=1e-5):
        dve.drain()
        for t in range(T):
            dve.bn_aggr(self.mv[:, t, :], self.stats[:, t, :])
        dve.drain()
        dve.tensor_scalar(self.veps[:, :], self.mv[:, :, 1], eps, None, ALU.add).then_inc(self.var_ready.sem, 1)
        dve.wait_ge(*self.rstd_ready.after(b, 1))
        for t in range(T):
            xt = self.x[:, b * T + t, :]
            dve.tensor_scalar(xt, xt, self.mv[:, t, 0:1], self.rstd[:, t:t + 1], ALU.subtract, ALU.mult)

    def pool_rstd(self, pool, b):
        pool.wait_ge(*self.var_ready.after(b, 1))
        pool.tensor_tensor(self.rstd[:, :], self.veps[:, :], self.mhalf[:, 0:T], ALU.pow) \
            .then_inc(self.rstd_ready.sem, 1)


def rope_attention(c):
    nc, d, ps = c.nc, c.d, c.ps
    with ExitStack() as ctx:
        def sb(nm, shape, dt=F32):
            return ctx.enter_context(nc.sbuf_tensor(f"s1_{nm}", shape, dt))

        wq_hi = sb("wqkv_hi", [P, KD, NQKV], F32R)
        wq_lo = sb("wqkv_lo", [P, KD, NQKV], F32R)
        wo = sb("wo", [P, KD, D])
        qs = sb("q_stacks", [P, T, NH, STK])
        ks = sb("k_stacks", [P, T, NKV, STK])
        kT = sb("kT", [P, NKV, S], F32R)
        NQB = 4
        qT = sb("qT", [P, NQB, S], F32R)
        nmax = sb("neg_max", [P, 2, T, HD])
        v = sb("v", [P, T, NK])
        v_next = sb("v_next", [P, T, NK])
        NPB = 6
        probsT = sb("probsT", [P, NPB, T, S])
        outT = sb("outT", [P, 4, S])
        inv = sb("inv_sums", [P, S])
        ra = sb("rope_a", [P, 2, NQK * HD])
        rb = sb("rope_b", [P, NQK * HD])
        cs = sb("cos_sin", [P, T, 2, HD])
        wraw = probsT[:, 0:3, :, :].rearrange("p a b c -> p (a b c)")[:, 0:KD * NQKV] \
            .rearrange("p (k n) -> p k n", k=KD)

        weights = c.sem("s1_weights_loaded")
        w_hi = c.sem("s1_w_hi_ready")
        w_lo = c.sem("s1_w_lo_ready")
        frame = c.sem("s1_constant_rows_set")
        roped = Count(c.sem("s1_roped"), T)
        v_out = Count(c.sem("s1_v_out"), 1)
        r_hi = Count(c.sem("s1_rope_hi"), T)
        stacked = c.s1_stacked
        max_ready = Count(c.sem("s1_max_ready"), NH)
        inv_ready = Count(c.sem("s1_inv_ready"), NKV)

        steps = [("q", 0)]
        for i in range(NH + 4):
            g, r = (i - 6) // 4, (i - 6) % 4
            for t in range(T):
                if i < NH:
                    steps.append(("s", i, t))
                if 0 <= i - 2 < NH:
                    steps.append(("e", i - 2, t))
                if t == 0 and 0 <= i - 1 < NH:
                    steps.append(("m", i - 1))
                if t == 2 and i + 1 < NH:
                    steps.append(("q", i + 1))
                if 0 <= g < 4 and r < 2:
                    steps.append(("o", g, 2 * r + t // 2, t % 2))
                if 0 <= g < 4 and r >= 2 and t % 2:
                    steps.append(("d", g, 2 * (r - 2) + t // 2))
        steps = [s for s in steps if s[:2] != ("d", NKV - 1)]
        uses = []
        n = {"s": 0, "e": 0}
        for s in steps:
            if s[0] in "qm":
                uses.append((s, 5, 1))
            elif s[0] == "s":
                uses.append((s, n["s"] % 2, 1))
                n["s"] += 1
            elif s[0] == "e":
                uses.append((s, 2 + n["e"] % 3, 1))
                n["e"] += 1
            elif s[0] == "o" and s[2:] == (0, 0):
                uses.append((("o", s[1]), 6, 2))
        ps.open_segments({
            "heads": uses,
            "project": c.x_uses([2, 3]) + [(("p", t), (0, 3)[t % 2], 2) for t in range(T)],
            "output": c.y_uses([2, 5]),
            "keys": [(("k", g), (0, 1)[g % 2], 1) for g in range(NKV)]})

        block = ctx.enter_context(nc.Block())

        @block.sync
        def _(sp):
            sp.dma_start(wraw, d["l0a_wqkv"].rearrange("(k p) n -> p k n", p=P)).then_inc(weights, 16)
            sp.dma_start(cs[:, :, :, :], d["cos_sin"].rearrange("(t p) a n -> p t a n", p=P)).then_inc(weights, 16)
            sp.dma_start(wo[:, :, :], d["l0a_wo"].rearrange("(k p) n -> p k n", p=P)).then_inc(weights, 16)
            with sp.Fori(0, B) as b:
                c.sync_load_x(sp, b)

        @block.gpsimd
        def _(pool):
            pool.memset(kT[STK:P, :, :].bitcast(F32), 0.0)
            pool.drain()
            pool.memset(kT[STK:STK + 1, :, :].bitcast(F32), 1.0)
            pool.drain()
            pool.memset(nmax[:, :, :, :], 0.0).then_inc(frame, 1)
            pool.wait_ge(w_hi, 1)
            pool.tensor_tensor(wq_lo[:, :, :], wraw, wq_hi[:, :, :].bitcast(F32), ALU.subtract).then_inc(w_lo, 1)

            def project(b, pos, heads_before):
                for t in range(T):
                    pool.wait_ge(*r_hi.after(b, t + 1))
                    rq = ra[:, t % 2, 0:D].rearrange("p (h e) -> p h e", e=HD)
                    rk = ra[:, t % 2, D:].rearrange("p (h e) -> p h e", e=HD)
                    pool.tensor_tensor(qs[:, t, :, 2 * HD:].bitcast(F32R), rq, qs[:, t, :, 0:HD], ALU.subtract)
                    pool.tensor_tensor(ks[:, t, :, HD:2 * HD].bitcast(F32R), rk, ks[:, t, :, 0:HD], ALU.subtract) \
                        .then_inc(stacked.sem, 1)

            def output(b, pos):
                c.pool_rstd(pool, b)

            turns(pool, project, nothing, nothing, output)

        @block.scalar
        def _(act):
            act.wait_ge(weights, 48)
            act.activation(wq_hi[:, :, :], wraw, ACT.Copy).then_inc(w_hi, 1)

            def project(b, pos, heads_before):
                c.act_x_hi(act, b, pos)
                for t in range(T):
                    act.wait_ge(*roped.after(b, t + 1))
                    act.activation(v_next[:, t, :], ps.ap(("p", t), 1)[:, NK:2 * NK], ACT.Copy) \
                       .then_inc(ps.freed(("p", t)), 1)
                    rq = ra[:, t % 2, 0:D].rearrange("p (h e) -> p h e", e=HD)
                    rk = ra[:, t % 2, D:].rearrange("p (h e) -> p h e", e=HD)
                    act.activation(qs[:, t, :, 0:HD].bitcast(F32R), rq, ACT.Copy)
                    act.activation(qs[:, t, :, HD:2 * HD].bitcast(F32R), rq, ACT.Copy)
                    act.activation(ks[:, t, :, 0:HD].bitcast(F32R), rk, ACT.Copy)
                    act.activation(ks[:, t, :, 2 * HD:].bitcast(F32R), rk, ACT.Copy).then_inc(r_hi.sem, 1)

            def keys(b, pos, heads_before):
                act.wait_ge(*r_hi.after(b, T))
                if heads_before is not None:
                    act.wait_ge(*ps.full(heads_before, ("o", NKV - 1)))
                act.activation(v[:, :, :], v_next[:, :, :], ACT.Copy).then_inc(v_out.sem, 1)
                for g in range(NKV):
                    act.wait_ge(*ps.full(pos, ("k", g)))
                    act.activation(kT[0:STK, g, :], ps.ap(("k", g))[0:STK, :], ACT.Copy) \
                       .then_inc(ps.freed(("k", g)), 1)

            def heads(b, pos):
                for s in steps:
                    if s[0] == "q":
                        h = s[1]
                        act.wait_ge(*ps.full(pos, s))
                        if h >= NQB:
                            act.wait_ge(*ps.full(pos, ("e", h - NQB, T - 1)))
                        act.activation(qT[0:STK, h % NQB, :], ps.ap(s)[0:STK, :], ACT.Copy).then_inc(ps.freed(s), 1)
                    elif s[0] == "m":
                        h = s[1]
                        act.wait_ge(*ps.full(pos, s))
                        act.activation(qT[STK:P, h % NQB, :], ps.ap(s)[STK:P, :], ACT.Copy).then_inc(ps.freed(s), 1)
                    elif s[0] == "e":
                        h, k = s[1:]
                        act.wait_ge(*ps.full(pos, s))
                        if h >= NPB and k == 0:
                            act.wait_ge(*ps.full(pos, ("o", (h - NPB) // 4)))
                        act.activation(probsT[:, h % NPB, k, :], ps.ap(s), ACT.Exp).then_inc(ps.freed(s), 1)

            turns(act, project, keys, heads, nothing)

        @block.vector
        def _(dve):
            dve.wait_ge(frame, 1)

            def project(b, pos, heads_before):
                c.dve_x_lo(dve, b, pos)
                if heads_before is not None:
                    last_quotients(heads_before)
                for t in range(T):
                    dve.wait_ge(*ps.full(pos, ("p", t)))
                    if t >= 2:
                        dve.wait_ge(*stacked.after(b, t - 1))
                    qk = ps.pair(("p", t)).rearrange("p a n -> p (a n)")[:, 0:NQK * HD]
                    rope_cos(dve, qk, ra[:, t % 2, :], cs, t)
                    rope_sin(dve, qk, rb, cs, t)
                    dve.drain()
                    dve.tensor_tensor(ra[:, t % 2, :], ra[:, t % 2, :], rb[:, :], ALU.add).then_inc(roped.sem, 1)
                    dve.drain()

            def quotient(pos, g, t):
                cols = slice(t * P, (t + 1) * P)
                if t == 0:
                    dve.wait_ge(*ps.full(pos, ("o", g)))
                dve.reciprocal(inv[:, cols], ps.ap(("o", g), 1)[:, cols])
                dve.drain()
                out = dve.tensor_tensor(outT[:, g, cols], ps.ap(("o", g))[:, cols], inv[:, cols], ALU.mult)
                if t == T - 1:
                    out.then_inc(ps.freed(("o", g)), 1)

            def heads(b, pos):
                for s in steps:
                    if s[0] == "s":
                        h, t = s[1:]
                        dve.wait_ge(*ps.full(pos, s))
                        if h >= 2 and t == 0:
                            dve.wait_ge(*ps.full(pos, ("m", h - 2)))
                        dve.tensor_reduce(nmax[:, h % 2, t, 0:1], ps.ap(s), AX.X, ALU.max, negate=True) \
                           .then_inc(ps.freed(s), 1)
                    elif s[0] == "d":
                        quotient(pos, *s[1:])

            def last_quotients(pos):
                for t in range(T):
                    quotient(pos, NKV - 1, t)

            def output(b, pos):
                if pos is LAST_OUTPUT:
                    last_quotients(at("heads", pos[0]))
                c.dve_layernorm(dve, b, pos)

            turns(dve, project, nothing, heads, output)

        @block.tensor
        def _(pe):
            pe.wait_ge(w_lo, 1)
            pe.wait_ge(frame, 1)

            def project(b, pos, heads_before):
                c.pe_turn_x(pe, b, pos)
                c.wait_xT(pe, pos)
                for t in range(T):
                    ps.wait_empty(pe, pos, ("p", t))
                    for lo, hi, j in ((0, D, 0), (D, NQKV, 1)):
                        for k in range(KD):
                            mm = split3(pe, ps.ap(("p", t), j)[:, 0:hi - lo],
                                        (c.xhi[:, k, t * P:(t + 1) * P], c.xlo[:, k, t * P:(t + 1) * P]),
                                        (wq_hi[:, k, lo:hi], wq_lo[:, k, lo:hi]), k == 0, k == KD - 1)
                    mm.then_inc(ps.filled(("p", t)), 1)

            def keys(b, pos, heads_before):
                pe.wait_ge(*stacked.after(b, T))
                for g in range(NKV):
                    ps.wait_empty(pe, pos, ("k", g))
                    for t in range(T):
                        mm = pe.transpose(ps.ap(("k", g))[0:STK, t * P:(t + 1) * P], ks[:, t, g, :], c.ident[:, :])
                    mm.then_inc(ps.filled(("k", g)), 1)

            def heads(b, pos):
                pe.wait_ge(*v_out.after(b, 1))
                for s in steps:
                    if s[0] not in "od":
                        ps.wait_empty(pe, pos, s)
                    if s[0] == "q":
                        for t in range(T):
                            mm = pe.transpose(ps.ap(s)[0:STK, t * P:(t + 1) * P], qs[:, t, s[1], :], c.ident[:, :])
                        mm.then_inc(ps.filled(s), 1)
                    elif s[0] == "s":
                        h, t = s[1:]
                        if t == 0:
                            pe.wait_ge(*ps.released(pos, ("q", h)))
                        pe.matmul(ps.ap(s), qT[0:STK, h % NQB, t * P:(t + 1) * P], kT[0:STK, h % NKV, :],
                                  start=True, stop=True).then_inc(ps.filled(s), 1)
                    elif s[0] == "m":
                        h = s[1]
                        for t in (T - 2, T - 1):
                            pe.wait_ge(*ps.released(pos, ("s", h, t)))
                        for t in range(T):
                            mm = pe.matmul(ps.ap(s)[STK:P, t * P:(t + 1) * P], nmax[:, h % 2, t, :], c.ident[:, :],
                                           start=True, stop=True)
                        mm.then_inc(ps.filled(s), 1)
                    elif s[0] == "e":
                        h, k = s[1:]
                        if k == 0:
                            pe.wait_ge(*ps.released(pos, ("m", h)))
                        pe.matmul(ps.ap(s), kT[:, h % NKV, k * P:(k + 1) * P], qT[:, h % NQB, :],
                                  start=True, stop=True).then_inc(ps.filled(s), 1)
                    elif s[0] == "o":
                        g, k, half = s[1:]
                        if k == 0 and half == 0:
                            ps.wait_empty(pe, pos, ("o", g))
                            for kk in range(T - 3, T):
                                pe.wait_ge(*ps.released(pos, ("e", 4 * g + 3, kk)))
                        for j in range(4):
                            mm = pe.matmul(ps.ap(("o", g), half)[j * HD:(j + 1) * HD, :],
                                           c.ones[:, 0:HD] if half else v[:, k, j * HD:(j + 1) * HD],
                                           probsT[:, (4 * g + j) % NPB, k, :], start=(k == 0), stop=(k == T - 1))
                        if k == T - 1 and half == 1:
                            mm.then_inc(ps.filled(("o", g)), 1)

            def output(b, pos):
                pe.wait_ge(*ps.released(at("heads", pos[0]), ("o", NKV - 1)))
                for t in range(T):
                    ps.wait_empty(pe, pos, ("y", t))
                    for k in range(KD):
                        mm = pe.matmul(ps.ap(("y", t)), outT[:, k, t * P:(t + 1) * P], wo[:, k, :],
                                       start=(k == 0), stop=(k == KD - 1))
                    mm.then_inc(ps.filled(("y", t)), 1)

            turns(pe, project, keys, heads, output)

        c.close(B)


def at(part, b, offset=0):
    if offset == 0:
        return {"heads": (b, {"project": 1, "keys": 1}),
                "output": (b, {"project": 2, "keys": 1, "heads": 1})}[part]
    return {"project": (b, {"project": 1, "keys": 1, "heads": 1}),
            "keys": (b, {"project": 2, "keys": 1, "heads": 1, "output": 1})}[part]

FIRST_PROJECT, FIRST_KEYS = (0, {}), (0, {"project": 1})
LAST_OUTPUT = (B - 1, {"project": 1, "keys": 1, "heads": 1})

def turns(eng, project, keys, heads, output):
    project(0, FIRST_PROJECT, None)
    keys(0, FIRST_KEYS, None)
    with eng.Fori(0, B - 1) as b:
        heads(b, at("heads", b))
        project(b + 1, at("project", b, 1), at("heads", b))
        output(b, at("output", b))
        keys(b + 1, at("keys", b, 1), at("heads", b))
    heads(B - 1, at("heads", B - 1))
    output(B - 1, LAST_OUTPUT)


def nothing(*_):
    pass


def rope_cos(eng, qk, ra, cs, t):
    nh = qk.shape[1] // HD
    return eng.tensor_tensor(ra[:, :].rearrange("p (h e) -> p h e", h=nh), qk.rearrange("p (h e) -> p h e", h=nh),
                             cs[:, t, 0, :].unsqueeze(1).broadcast_to([P, nh, HD]), ALU.mult)


def rope_sin(dve, qk, rb, cs, t):
    nh = qk.shape[1] // HD
    q4 = qk.rearrange("p (h e two) -> p h e two", h=nh, two=2)
    b4 = rb[:, :].rearrange("p (h e two) -> p h e two", h=nh, two=2)
    w = cs[:, t, 1, :].rearrange("p (e two) -> p e two", two=2)
    for par in range(2):
        last = dve.tensor_tensor(b4[:, :, :, par], q4[:, :, :, 1 - par],
                                 w[:, :, par].unsqueeze(1).broadcast_to([P, nh, HD // 2]), ALU.mult)
    return last


def similarity_mixing(c):
    nc, d, ps = c.nc, c.d, c.ps
    with ExitStack() as ctx:
        def sb(nm, shape, dt=F32):
            return ctx.enter_context(nc.sbuf_tensor(f"s2_{nm}", shape, dt))

        w = sb("w", [P, 2, KC, DX])
        w_h = sb("w_hi", [P, 2, KC, DX], F32R)
        w_l = sb("w_lo", [P, 2, KC, DX], F32R)
        bias = sb("bias", [P, 2])
        cT = sb("ctxT", [P, B, KC, S])
        c_h = sb("ctxT_hi", [P, KC, S], F32R)
        c_l = sb("ctxT_lo", [P, KC, S], F32R)
        f = sb("proj", [P, 2, S])
        f_h = sb("proj_hi", [P, 2, S], F32R)
        f_l = sb("proj_lo", [P, 2, S], F32R)
        nmax = sb("neg_max", [P, T])
        sums = sb("sums", [P, T])
        inv = sb("inv_sums", [P, T])
        probs = sb("probs", [P, T, S])
        a_h = sb("attT_hi", [P, T, S], F32R)
        a_l = sb("attT_lo", [P, T, S], F32R)

        weights = c.sem("s2_weights_loaded")
        w_hi = c.sem("s2_w_hi_ready")
        w_lo = c.sem("s2_w_lo_ready")
        ctx_hi = Count(c.sem("s2_ctx_hi_ready"), 1)
        ctx_lo = Count(c.sem("s2_ctx_lo_ready"), 1)
        max_ready = Count(c.sem("s2_max_ready"), T)
        normed = Count(c.sem("s2_normed"), T)
        att_hi = Count(c.sem("s2_att_hi_ready"), T)
        pr_hi = c.s2_proj_hi

        ps.open([(("f", j), j, 1) for j in range(2)] + c.x_uses([0, 1]) + [(("e", t), 2 + t % 2, 1) for t in range(T)]
                + [(("a", k), 4 + k % 2, 1) for k in range(T)] + c.y_uses([6, 7]))

        def turns(eng, similarity, transpose_x, mixing):
            similarity(0)
            transpose_x(0)
            with eng.Fori(0, B - 1) as b:
                mixing(b, lambda: similarity(b + 1), lambda: transpose_x(b + 1))
            mixing(B - 1, lambda: None, None)

        block = ctx.enter_context(nc.Block())

        @block.sync
        def _(sp):
            for j, (wn, bn) in enumerate((("l0x_wqT", "l0x_bq"), ("l0x_wkT", "l0x_bk"))):
                sp.dma_start(w[:, j, :, :], d[wn].rearrange("(k p) n -> p k n", p=P)).then_inc(weights, 16)
                sp.dma_start(bias[:, j:j + 1], d[bn]).then_inc(weights, 16)
            sp.dma_start(cT[:, :, :, :], d["ctxT"].rearrange("b (k p) s -> p b k s", p=P)).then_inc(weights, 16)
            with sp.Fori(0, B) as b:
                c.sync_load_x(sp, b)

        @block.gpsimd
        def _(pool):
            pool.wait_ge(w_hi, 1)
            pool.tensor_tensor(w_l[:, :, :, :], w[:, :, :, :], w_h[:, :, :, :].bitcast(F32), ALU.subtract) \
                .then_inc(w_lo, 1)
            with pool.Fori(0, B) as b:
                c.pool_rstd(pool, b)

        @block.scalar
        def _(act):
            act.wait_ge(weights, 80)
            act.activation(w_h[:, :, :, :], w[:, :, :, :], ACT.Copy).then_inc(w_hi, 1)

            def similarity(b):
                act.wait_ge(*pr_hi.after(b, 0))
                act.activation(c_h[:, :, :], cT[:, bass.ds(b, 1), :, :].rearrange("p a k s -> p (a k) s"),
                               ACT.Copy).then_inc(ctx_hi.sem, 1)
                for j in range(2):
                    act.wait_ge(*ps.full(b, ("f", j)))
                    act.activation(f[:, j, :], ps.ap(("f", j)), ACT.Identity, bias=bias[:, j:j + 1])
                    act.activation(f_h[:, j, :], ps.ap(("f", j)), ACT.Identity, bias=bias[:, j:j + 1]) \
                       .then_inc(pr_hi.sem, 1)
                for t in range(T):
                    act.wait_ge(*max_ready.after(b, t + 1))
                    act.activation(probs[:, t, :], ps.ap(("e", t)), ACT.Exp, bias=nmax[:, t:t + 1],
                                   accum_out=sums[:, t:t + 1]).then_inc(ps.freed(("e", t)), 1)

            def mixing(b, next_similarity, next_x):
                for k in range(T):
                    act.wait_ge(*ps.full(b, ("a", k)))
                    act.activation(a_h[:, k, :], ps.ap(("a", k)), ACT.Copy).then_inc(att_hi.sem, 1)
                next_similarity()
                if next_x is not None:
                    next_x()

            turns(act, similarity, lambda b: c.act_x_hi(act, b), mixing)

        @block.vector
        def _(dve):
            def similarity(b):
                dve.wait_ge(*ctx_hi.after(b, 1))
                dve.tensor_tensor(c_l[:, :, :], cT[:, bass.ds(b, 1), :, :].rearrange("p a k s -> p (a k) s"),
                                  c_h[:, :, :].bitcast(F32), ALU.subtract).then_inc(ctx_lo.sem, 1)
                for j in range(2):
                    dve.wait_ge(*pr_hi.after(b, j + 1))
                    dve.tensor_tensor(f_l[:, j, :], f[:, j, :], f_h[:, j, :].bitcast(F32), ALU.subtract) \
                       .then_inc(ps.freed(("f", j)), 1)
                for t in range(T):
                    dve.wait_ge(*ps.full(b, ("e", t)))
                    dve.tensor_reduce(nmax[:, t:t + 1], ps.ap(("e", t)), AX.X, ALU.max, negate=True) \
                       .then_inc(max_ready.sem, 1)
                for t in range(T):
                    dve.wait_ge(*ps.released(b, ("e", t)))
                    dve.reciprocal(inv[:, t:t + 1], sums[:, t:t + 1])
                    dve.drain()
                    dve.tensor_scalar(probs[:, t, :], probs[:, t, :], inv[:, t:t + 1], None, ALU.mult) \
                       .then_inc(normed.sem, 1)

            def mixing(b, next_similarity, next_x):
                for k in range(T):
                    dve.wait_ge(*att_hi.after(b, k + 1))
                    dve.tensor_tensor(a_l[:, k, :], ps.ap(("a", k)), a_h[:, k, :].bitcast(F32), ALU.subtract) \
                       .then_inc(ps.freed(("a", k)), 1)
                next_similarity()
                c.dve_layernorm(dve, b, between=next_x)

            turns(dve, similarity, lambda b: c.dve_x_lo(dve, b), mixing)

        @block.tensor
        def _(pe):
            pe.wait_ge(w_lo, 1)

            def similarity(b):
                pe.wait_ge(*ctx_lo.after(b, 1))
                for j in range(2):
                    ps.wait_empty(pe, b, ("f", j))
                    for k in range(KC):
                        mm = split3(pe, ps.ap(("f", j)), (w_h[:, j, k, :], w_l[:, j, k, :]), (c_h[:, k, :], c_l[:, k, :]),
                                    k == 0, k == KC - 1)
                    mm.then_inc(ps.filled(("f", j)), 1)
                for j in range(2):
                    pe.wait_ge(*ps.released(b, ("f", j)))
                for t in range(T):
                    ps.wait_empty(pe, b, ("e", t))
                    split3(pe, ps.ap(("e", t)), (f_h[:, 0, t * P:(t + 1) * P], f_l[:, 0, t * P:(t + 1) * P]),
                           (f_h[:, 1, :], f_l[:, 1, :]), True, True).then_inc(ps.filled(("e", t)), 1)

            def mixing(b, next_similarity, next_x):
                pe.wait_ge(*normed.after(b, T))
                for k in range(T):
                    ps.wait_empty(pe, b, ("a", k))
                    for t in range(T):
                        mm = pe.transpose(ps.ap(("a", k))[:, t * P:(t + 1) * P], probs[:, t, k * P:(k + 1) * P],
                                          c.ident[:, :])
                    mm.then_inc(ps.filled(("a", k)), 1)
                next_similarity()
                c.wait_xT(pe, b)
                for k in (T - 2, T - 1):
                    pe.wait_ge(*ps.released(b, ("a", k)))
                for t in range(T):
                    ps.wait_empty(pe, b, ("y", t))
                    for k in range(KD):
                        mm = split3(pe, ps.ap(("y", t)), (c.xhi[:, k, t * P:(t + 1) * P], c.xlo[:, k, t * P:(t + 1) * P]),
                                    (a_h[:, k, :], a_l[:, k, :]), k == 0, k == KD - 1)
                    mm.then_inc(ps.filled(("y", t)), 1)
                if next_x is not None:
                    next_x()

            turns(pe, similarity, lambda b: c.pe_turn_x(pe, b), mixing)

        c.close(B)


def lora_experts(c):
    nc, d, ps = c.nc, c.d, c.ps
    with ExitStack() as ctx:
        def sb(nm, shape, dt=F32):
            return ctx.enter_context(nc.sbuf_tensor(f"s3_{nm}", shape, dt))

        NAG = LORA + NE
        w = sb("w", [P, KD, D])
        w_h = sb("w_hi", [P, KD, D], F32R)
        w_l = sb("w_lo", [P, KD, D], F32R)
        a = sb("ag", [P, KD, NAG])
        a_h = sb("ag_hi", [P, KD, NAG], F32R)
        a_l = sb("ag_lo", [P, KD, NAG], F32R)
        bt = sb("bt", [P, D])
        bt_h = sb("bt_hi", [P, D], F32R)
        bt_l = sb("bt_lo", [P, D], F32R)
        lg = sb("logits", [P, T, 2 * NE])
        rest = sb("logits_rest", [P, T, 2 * NE])
        mask = sb("top_mask", [P, T, NE])
        top = sb("top8", [P, T, 8])
        nmax = sb("neg_max", [P, T])
        ex = sb("exps", [P, T, NE])
        exm = sb("exps_masked", [P, T, NE])
        sums = sb("sums", [P, T])
        inv = sb("inv_sums", [P, T])
        tw = sb("t_weighted", [P, T, LORA])
        tT_h = sb("tT_hi", [P, S], F32R)
        tT_l = sb("tT_lo", [P, S], F32R)

        weights = c.sem("s3_weights_loaded")
        w_hi = c.sem("s3_w_hi_ready")
        w_lo = c.sem("s3_w_lo_ready")
        pad = c.sem("s3_pad_set")
        masked = Count(c.sem("s3_top_found"), 1)
        exps = Count(c.sem("s3_exps_ready"), 1)
        weighted = Count(c.sem("s3_weighted"), 1)
        t_hi = Count(c.sem("s3_tT_hi_ready"), 1)

        ps.open(c.x_uses([2, 3]) + [(("g", t), t, 1) for t in range(T)]
                + [(("tT", 0), 4, 1)] + c.y_uses([5, 6, 7]))
        block = ctx.enter_context(nc.Block())

        @block.sync
        def _(sp):
            sp.dma_start(a[:, :, :], d["l0f_agT"].rearrange("(k p) n -> p k n", p=P)).then_inc(weights, 16)
            sp.dma_start(w[:, :, :], d["l0f_wT"].rearrange("(k p) n -> p k n", p=P)).then_inc(weights, 16)
            sp.dma_start(bt[:, :], d["l0f_bT"]).then_inc(weights, 16)
            with sp.Fori(0, B) as b:
                c.sync_load_x(sp, b)

        @block.gpsimd
        def _(pool):
            pool.memset(lg[:, :, :], LOWEST).then_inc(pad, 1)
            pool.wait_ge(w_hi, 1)
            pool.tensor_tensor(a_l[:, :, :], a[:, :, :], a_h[:, :, :].bitcast(F32), ALU.subtract)
            pool.tensor_tensor(bt_l[:, :], bt[:, :], bt_h[:, :].bitcast(F32), ALU.subtract)
            pool.tensor_tensor(w_l[:, :, :], w[:, :, :], w_h[:, :, :].bitcast(F32), ALU.subtract).then_inc(w_lo, 1)
            with pool.Fori(0, B) as b:
                c.pool_rstd(pool, b)

        @block.scalar
        def _(act):
            act.wait_ge(weights, 48)
            act.activation(a_h[:, :, :], a[:, :, :], ACT.Copy)
            act.activation(w_h[:, :, :], w[:, :, :], ACT.Copy)
            act.activation(bt_h[:, :], bt[:, :], ACT.Copy).then_inc(w_hi, 1)

            def experts(b, following):
                act.wait_ge(*masked.after(b, 1))
                for t in range(T):
                    e = act.activation(ex[:, t, :], lg[:, t, 0:NE], ACT.Exp, bias=nmax[:, t:t + 1])
                e.then_inc(exps.sem, 1)
                act.wait_ge(*ps.full(b, ("tT", 0)))
                act.activation(tT_h[:, :], ps.ap(("tT", 0)), ACT.Copy).then_inc(t_hi.sem, 1)
                if following is not None:
                    following(b + 1)

            pipelined(act, lambda b: c.act_x_hi(act, b), experts)

        @block.vector
        def _(dve):
            dve.wait_ge(pad, 1)

            def experts(b, following):
                for t in range(T):
                    dve.wait_ge(*ps.full(b, ("g", t)))
                    dve.tensor_copy(lg[:, t, 0:NE], ps.ap(("g", t))[:, LORA:NAG])
                dve.drain()
                for t in range(T):
                    dve.max(top[:, t, :], lg[:, t, :])
                dve.drain()
                dve.tensor_scalar(nmax[:, :], top[:, :, 0], -1.0, None, ALU.mult)
                dve.memset(top[:, :, TOPK:], LOWEST)
                dve.drain()
                for t in range(T):
                    dve.match_replace(rest[:, t, :], top[:, t, :], lg[:, t, :], LOWEST)
                dve.drain()
                dve.tensor_tensor(mask[:, :, :], rest[:, :, 0:NE], lg[:, :, 0:NE], ALU.not_equal) \
                   .then_inc(masked.sem, 1)
                dve.wait_ge(*exps.after(b, 1))
                dve.tensor_tensor(exm[:, :, :], ex[:, :, :], mask[:, :, :], ALU.mult)
                dve.drain()
                dve.tensor_reduce(sums[:, :], exm[:, :, :], AX.X, ALU.add)
                dve.drain()
                dve.reciprocal(inv[:, :], sums[:, :])
                dve.drain()
                dve.tensor_scalar(inv[:, :], inv[:, :], LORA_ALPHA, None, ALU.mult)
                dve.drain()
                dve.tensor_tensor(exm[:, :, :], exm[:, :, :], inv[:, :].unsqueeze(2).broadcast_to([P, T, NE]), ALU.mult)
                dve.drain()
                for t in range(T):
                    dve.tensor_tensor(tw[:, t, :].rearrange("p (e r) -> p e r", e=NE),
                                      ps.ap(("g", t))[:, 0:LORA].rearrange("p (e r) -> p e r", e=NE),
                                      exm[:, t, :].unsqueeze(2).broadcast_to([P, NE, RANK]), ALU.mult) \
                       .then_inc(ps.freed(("g", t)), 1)
                dve.wait_ge(*t_hi.after(b, 1))
                dve.tensor_tensor(tT_l[:, :], ps.ap(("tT", 0)), tT_h[:, :].bitcast(F32), ALU.subtract) \
                   .then_inc(ps.freed(("tT", 0)), 1)
                c.dve_layernorm(dve, b, between=None if following is None else lambda: following(b + 1))

            pipelined(dve, lambda b: c.dve_x_lo(dve, b), experts)

        @block.tensor
        def _(pe):
            def experts(b, following):
                c.wait_xT(pe, b)
                pe.wait_ge(w_lo, 1)

                def xs(k, t):
                    return c.xhi[:, k, t * P:(t + 1) * P], c.xlo[:, k, t * P:(t + 1) * P]

                for t in range(T):
                    ps.wait_empty(pe, b, ("g", t))
                    for k in range(KD):
                        mm = split3(pe, ps.ap(("g", t))[:, 0:NAG], xs(k, t), (a_h[:, k, :], a_l[:, k, :]),
                                    k == 0, k == KD - 1)
                    mm.then_inc(ps.filled(("g", t)), 1)

                def dense(t):
                    ps.wait_empty(pe, b, ("y", t))
                    for k in range(KD):
                        split3(pe, ps.ap(("y", t)), xs(k, t), (w_h[:, k, :], w_l[:, k, :]), k == 0, False)

                def lora(t):
                    split3(pe, ps.ap(("y", t)), (tT_h[:, t * P:(t + 1) * P], tT_l[:, t * P:(t + 1) * P]),
                           (bt_h[:, :], bt_l[:, :]), False, True).then_inc(ps.filled(("y", t)), 1)

                for t in range(3):
                    dense(t)
                for t in range(T):
                    pe.wait_ge(*ps.released(b, ("g", t)))
                ps.wait_empty(pe, b, ("tT", 0))
                for t in range(T):
                    mm = pe.transpose(ps.ap(("tT", 0))[:, t * P:(t + 1) * P], tw[:, t, :], c.ident[:, :])
                mm.then_inc(ps.filled(("tT", 0)), 1)
                pe.wait_ge(*ps.released(b, ("tT", 0)))
                for t in range(3):
                    lora(t)
                dense(3)
                lora(3)
                if following is not None:
                    following(b + 1)

            pipelined(pe, lambda b: c.pe_turn_x(pe, b), experts)

        c.close(B)


def pipelined(eng, front, back):
    front(0)
    with eng.Fori(0, B - 1) as b:
        back(b, front)
    back(B - 1, None)


def window_attention(c):
    nc, d, ps = c.nc, c.d, c.ps
    with ExitStack() as ctx:
        def sb(nm, shape, dt=F32):
            return ctx.enter_context(nc.sbuf_tensor(f"s4_{nm}", shape, dt))

        w = sb("wqkv", [P, KD, NQKV])
        w_h = sb("wqkv_hi", [P, KD, NQKV], F32R)
        w_l = sb("wqkv_lo", [P, KD, NQKV], F32R)
        wo = sb("wo", [P, KD, D])
        b_qkv = sb("b_qkv", [P, NQKV])
        b_o = sb("b_o", [P, D])
        gain = sb("qk_gain", [P, 2, HD])
        gmax = sb("gain_max", [P, 2])
        scale = sb("scale", [P, 1])
        bound = sb("minus_bound", [P, 1])
        cs = sb("cos_sin", [P, T, 2, HD])
        csg = sb("cos_sin_gain", [P, 2, T, 2, HD])
        maskf = sb("mask_f32", [P, NQK * HD])
        mask = sb("mask", [P, 4 * P], BF16)
        idb = sb("ident_bf16", [P, P], BF16)
        pj = sb("proj", [P, 2, NQKV])
        sq = sb("squares", [P, NQK * HD])
        ms = sb("mean_sq", [P, 2, NQK])
        rms = sb("rms", [P, 2, NQK])
        rs = sb("qk_rstd", [P, NQK])
        ra = sb("rope_a", [P, 2, NQK * HD])
        rb = maskf[:, 0:NQK * HD]
        qs = sb("q_stacks", [P, T, NH, STK])
        ks = sb("k_stacks", [P, T, NKV, STK])
        kT = sb("kT", [STK, NKV, S], F32R)
        NQB = 3
        qT = sb("qT", [STK, NQB, S], F32R)
        v = sb("v", [P, T, NK])
        v_next = sb("v_next", [P, T, NK])
        NPB = 8
        probsT = sb("probsT", [P, NPB, 2, S])
        zeros_f32 = probsT[:, 0, 1, S - P // 2:]
        zeros = zeros_f32.bitcast(BF16)
        inv = w[:, :, S:S + P]
        outT = w[:, :, 0:S]

        weights = c.sem("s4_weights_loaded")
        w_hi = c.sem("s4_w_hi_ready")
        w_lo = c.sem("s4_w_lo_ready")
        zeros_set = c.sem("s4_zeros_set")
        tables = c.sem("s4_tables_ready")
        bf_ready = c.sem("s4_mask_bf16_ready")
        squared = Count(c.sem("s4_squared"), T)
        ms_ready = Count(c.sem("s4_mean_sq_ready"), T)
        rms_ready = Count(c.sem("s4_qk_rms_ready"), T)
        v_out = c.s4_v_out
        roped = c.s4_roped
        normed = Count(c.sem("s4_qk_normed"), T)
        cos_done = Count(c.sem("s4_cos_half_done"), T)
        x_biased = Count(c.sem("s4_x_biased"), 1)
        v_in = Count(c.sem("s4_v_in_place"), 1)
        r_hi = Count(c.sem("s4_rope_hi"), T)
        stacked = c.s4_stacked

        BLOCKS = [(0, 0), (0, 1), (1, 1), (1, 2), (2, 2), (2, 3), (3, 3)]
        NBL = len(BLOCKS)

        steps = [("q", 0)]
        for i in range(NH + 5):
            if i + 1 < NH:
                steps.append(("q", i + 1))
            if i < NH:
                steps.append(("e", i))
            g, r = (i - 5) // 4, (i - 5) % 4
            if 0 <= g < 4:
                steps += [("o" if r < 2 else "d", g, r % 2 * 2 + j) for j in range(2)]
        steps = [s for s in steps if s[:2] != ("d", NKV - 1)]
        uses = []
        for s in steps:
            if s[0] == "q":
                uses.append((s, 2 + s[1] % 2, 1))
            elif s[0] == "e":
                uses.append((s, (0, 4)[s[1] % 2], 2))
            elif s[0] == "o" and s[2] == 0:
                uses.append((("o", s[1]), 6, 2))
        ps.open_segments({
            "heads": uses,
            "project": c.x_uses([2, 3]) + [(("p", t), (0, 4)[t % 2], 2) for t in range(T)],
            "output": c.y_uses([2, 3]),
            "keys": [(("k", g), (0, 4)[g % 2], 1) for g in range(NKV)]})
        block = ctx.enter_context(nc.Block())

        @block.sync
        def _(sp):
            sp.dma_start(w[:, :, :], d["l1a_wqkvT"].rearrange("(k p) n -> p k n", p=P)).then_inc(weights, 16)
            sp.dma_start(wo[:, :, :], d["l1a_woT"].rearrange("(k p) n -> p k n", p=P)).then_inc(weights, 16)
            sp.dma_start(b_qkv[:, :], d["l1a_bqkv"].broadcast_to([P, NQKV])).then_inc(weights, 16)
            sp.dma_start(b_o[:, :], d["l1a_bo"].broadcast_to([P, D])).then_inc(weights, 16)
            sp.dma_start(gain[:, 0, :], d["l1a_qn"].broadcast_to([P, HD])).then_inc(weights, 16)
            sp.dma_start(gain[:, 1, :], d["l1a_kn"].broadcast_to([P, HD])).then_inc(weights, 16)
            sp.dma_start(scale[:, :], d["l1a_scale"].broadcast_to([P, 1])).then_inc(weights, 16)
            sp.dma_start(cs[:, :, :, :], d["cos_sin_plain"].rearrange("(t p) a n -> p t a n", p=P)).then_inc(weights, 16)
            sp.dma_start(maskf[:, 0:4 * P], d["window_mask"]).then_inc(weights, 16)
            with sp.Fori(0, B) as b:
                c.sync_load_x(sp, b)

        @block.gpsimd
        def _(pool):
            pool.memset(zeros_f32, 0.0).then_inc(zeros_set, 1)
            pool.wait_ge(w_hi, 1)
            pool.tensor_tensor(w_l[:, :, :], w[:, :, :], w_h[:, :, :].bitcast(F32), ALU.subtract).then_inc(w_lo, 1)

            def project(b, pos, heads_before):
                pool.wait_ge(*c.cur.after(b, 16))
                pool.wait_ge(c.pool_consts, 1)
                xb = c.x[:, bass.ds(b * T, T), :]
                pool.tensor_tensor(xb, xb, b_o[:, :].unsqueeze(1).broadcast_to([P, T, D]), ALU.add) \
                    .then_inc(x_biased.sem, 1)

                def lo(t):
                    pool.wait_ge(*r_hi.after(b, t + 1))
                    rq = ra[:, t % 2, 0:D].rearrange("p (h e) -> p h e", e=HD)
                    rk = ra[:, t % 2, D:].rearrange("p (h e) -> p h e", e=HD)
                    pool.tensor_tensor(qs[:, t, :, 2 * HD:].bitcast(F32R), rq, qs[:, t, :, 0:HD], ALU.subtract)
                    pool.tensor_tensor(ks[:, t, :, HD:2 * HD].bitcast(F32R), rk, ks[:, t, :, 0:HD], ALU.subtract) \
                        .then_inc(stacked.sem, 1)
                    pool.drain()

                for t in range(T):
                    pool.wait_ge(*normed.after(b, t + 1))
                    rope_cos(pool, pj[:, t % 2, 0:D], ra[:, t % 2, 0:D], csg[:, 0, :, :, :], t)
                    rope_cos(pool, pj[:, t % 2, D:NQK * HD], ra[:, t % 2, D:], csg[:, 1, :, :, :], t) \
                        .then_inc(cos_done.sem, 1)
                    if t > 0:
                        lo(t - 1)
                lo(T - 1)

            def output(b, pos):
                c.pool_rstd(pool, b)

            turns(pool, project, nothing, nothing, output)

        @block.scalar
        def _(act):
            act.wait_ge(weights, 16 * 9)
            act.activation(w_h[:, :, :], w[:, :, :], ACT.Copy).then_inc(w_hi, 1)
            act.activation(idb[:, :], c.ident[:, :], ACT.Copy)
            act.activation(mask[:, :], maskf[:, 0:4 * P], ACT.Copy).then_inc(bf_ready, 1)
            act.wait_ge(tables, 1)

            def squares(b, pos, t):
                act.wait_ge(*ps.released(pos, ("p", t)))
                act.activation(sq[:, :], pj[:, t % 2, 0:NQK * HD], ACT.Square).then_inc(squared.sem, 1)
                act.activation(v_next[:, t, :], pj[:, t % 2, NQK * HD:], ACT.Copy).then_inc(v_out.sem, 1)
                act.wait_ge(*ms_ready.after(b, t + 1))
                act.activation(rms[:, t % 2, :], ms[:, t % 2, :], ACT.Sqrt).then_inc(rms_ready.sem, 1)

            def hi(b, t):
                act.wait_ge(*roped.after(b, t + 1))
                rq = ra[:, t % 2, 0:D].rearrange("p (h e) -> p h e", e=HD)
                rk = ra[:, t % 2, D:].rearrange("p (h e) -> p h e", e=HD)
                act.activation(qs[:, t, :, 0:HD].bitcast(F32R), rq, ACT.Copy)
                act.activation(qs[:, t, :, HD:2 * HD].bitcast(F32R), rq, ACT.Copy)
                act.activation(ks[:, t, :, 0:HD].bitcast(F32R), rk, ACT.Copy)
                act.activation(ks[:, t, :, 2 * HD:].bitcast(F32R), rk, ACT.Copy).then_inc(r_hi.sem, 1)

            def project(b, pos, heads_before):
                c.act_x_hi(act, b, pos)
                for t in range(T):
                    squares(b, pos, t)
                    if t > 0:
                        hi(b, t - 1)
                hi(b, T - 1)

            def keys(b, pos, heads_before):
                act.wait_ge(*v_out.after(b, T))
                if heads_before is not None:
                    act.wait_ge(*ps.full(heads_before, ("o", NKV - 1)))
                act.activation(v[:, :, :], v_next[:, :, :], ACT.Copy).then_inc(v_in.sem, 1)
                for g in range(NKV):
                    act.wait_ge(*ps.full(pos, ("k", g)))
                    act.activation(kT[:, g, :], ps.ap(("k", g))[0:STK, :], ACT.Copy).then_inc(ps.freed(("k", g)), 1)

            def heads(b, pos):
                for s in steps:
                    if s[0] == "e":
                        h = s[1]
                        act.wait_ge(*ps.full(pos, s))
                        if h >= NPB and h % 4 == 0:
                            act.wait_ge(*ps.full(pos, ("o", (h - NPB) // 4)))
                        act.activation(probsT[:, h % NPB, :, :].rearrange("p a n -> p (a n)")[:, 0:NBL * P],
                                       ps.pair(s).rearrange("p a n -> p (a n)")[:, 0:NBL * P], ACT.Exp,
                                       bias=bound[:, 0:1]).then_inc(ps.freed(s), 1)

            turns(act, project, keys, heads, nothing)

        @block.vector
        def _(dve):
            dve.wait_ge(weights, 16 * 9)
            dve.tensor_reduce(gmax[:, :], gain[:, :, :], AX.X, ALU.max, apply_absolute_value=True)
            dve.tensor_tensor(bound[:, :], scale[:, :], scale[:, :], ALU.mult)
            g_even = [gain[:, j, :].rearrange("p (e two) -> p e two", two=2) for j in range(2)]
            for j in range(2):
                dve.tensor_tensor(csg[:, j, :, 0, :], cs[:, :, 0, :], gain[:, j, :].unsqueeze(1).broadcast_to([P, T, HD]),
                                  ALU.mult)
                for par in range(2):
                    out = csg[:, j, :, 1, :].rearrange("p t (e two) -> p t e two", two=2)[:, :, :, par]
                    src = cs[:, :, 1, :].rearrange("p t (e two) -> p t e two", two=2)[:, :, :, par]
                    dve.tensor_tensor(out, src, g_even[j][:, :, 1 - par].unsqueeze(1).broadcast_to([P, T, HD // 2]),
                                      ALU.mult)
            dve.drain()
            dve.tensor_scalar(csg[:, 0, :, :, :], csg[:, 0, :, :, :], scale[:, 0:1], None, ALU.mult)
            dve.tensor_scalar(ms[:, 0, 0:1], scale[:, :], -1.0, None, ALU.mult)
            dve.drain()
            dve.tensor_tensor(ms[:, 0, 0:1], ms[:, 0, 0:1], scale[:, :], ALU.min)
            dve.tensor_tensor(gmax[:, 0:1], gmax[:, 0:1], gmax[:, 1:2], ALU.mult)
            dve.drain()
            dve.tensor_tensor(bound[:, :], ms[:, 0, 0:1], gmax[:, 0:1], ALU.mult)
            dve.drain()
            dve.tensor_scalar(bound[:, :], bound[:, :], float(HD), None, ALU.mult).then_inc(tables, 1)
            dve.wait_ge(tables, 1)
            dve.wait_ge(bf_ready, 1)

            def projected(b, pos, t):
                dve.wait_ge(*ps.full(pos, ("p", t)))
                if t >= 2:
                    dve.wait_ge(*roped.after(b, t - 1))
                dve.tensor_tensor(pj[:, t % 2, :], ps.pair(("p", t)).rearrange("p a n -> p (a n)")[:, 0:NQKV],
                                  b_qkv[:, :], ALU.add).then_inc(ps.freed(("p", t)), 1)

            def mean_squares(b, t):
                dve.wait_ge(*squared.after(b, t + 1))
                dve.tensor_reduce(ms[:, t % 2, :], sq[:, :].rearrange("p (h e) -> p h e", e=HD), AX.X, ALU.add)
                dve.drain()
                dve.tensor_scalar(ms[:, t % 2, :], ms[:, t % 2, :], 1.0 / HD, 1e-8, ALU.mult, ALU.add) \
                   .then_inc(ms_ready.sem, 1)

            def rotate(b, t):
                dve.wait_ge(*rms_ready.after(b, t + 1))
                dve.reciprocal(rs[:, :], rms[:, t % 2, :])
                dve.drain()
                qk = pj[:, t % 2, 0:NQK * HD]
                dve.tensor_tensor(qk.rearrange("p (h e) -> p h e", e=HD), qk.rearrange("p (h e) -> p h e", e=HD),
                                  rs[:, :].unsqueeze(2).broadcast_to([P, NQK, HD]), ALU.mult).then_inc(normed.sem, 1)
                dve.drain()
                rope_sin(dve, qk[:, 0:D], rb[:, 0:D], csg[:, 0, :, :, :], t)
                rope_sin(dve, qk[:, D:], rb[:, D:], csg[:, 1, :, :, :], t)
                dve.drain()
                dve.wait_ge(*cos_done.after(b, t + 1))
                dve.tensor_tensor(ra[:, t % 2, :], ra[:, t % 2, :], rb[:, :], ALU.add).then_inc(roped.sem, 1)
                dve.drain()

            def project(b, pos, heads_before):
                c.dve_x_lo(dve, b, pos)
                if heads_before is not None:
                    last_quotients(heads_before)
                for t in range(T):
                    projected(b, pos, t)
                    if t > 0:
                        rotate(b, t - 1)
                    mean_squares(b, t)
                rotate(b, T - 1)

            def heads(b, pos):
                for s in steps:
                    if s[0] == "q":
                        h = s[1]
                        dve.wait_ge(*ps.full(pos, s))
                        if h >= NQB:
                            dve.wait_ge(*ps.full(pos, ("e", h - NQB)))
                        dve.tensor_copy(qT[:, h % NQB, :], ps.ap(s)[0:STK, :]).then_inc(ps.freed(s), 1)
                    elif s[0] == "d":
                        quotient(pos, *s[1:])

            def quotient(pos, g, t):
                cols = slice(t * P, (t + 1) * P)
                if t == 0:
                    dve.wait_ge(*ps.full(pos, ("o", g)))
                dve.reciprocal(inv[:, t, :], ps.ap(("o", g), 1)[:, cols])
                dve.drain()
                out = dve.tensor_tensor(outT[:, g, cols], ps.ap(("o", g))[:, cols], inv[:, t, :], ALU.mult)
                if t == T - 1:
                    out.then_inc(ps.freed(("o", g)), 1)

            def last_quotients(pos):
                for t in range(T):
                    quotient(pos, NKV - 1, t)

            def output(b, pos):
                if pos is LAST_OUTPUT:
                    last_quotients(at("heads", pos[0]))
                dve.wait_ge(*x_biased.after(b, 1))
                c.dve_layernorm(dve, b, pos)

            turns(dve, project, nothing, heads, output)

        @block.tensor
        def _(pe):
            pe.wait_ge(w_lo, 1)
            pe.wait_ge(bf_ready, 1)
            pe.wait_ge(zeros_set, 1)
            def project(b, pos, heads_before):
                c.pe_turn_x(pe, b, pos)
                c.wait_xT(pe, pos)
                for t in range(T):
                    ps.wait_empty(pe, pos, ("p", t))
                    for lo, hi, j in ((0, D, 0), (D, NQKV, 1)):
                        for k in range(KD):
                            mm = split3(pe, ps.ap(("p", t), j)[:, 0:hi - lo],
                                        (c.xhi[:, k, t * P:(t + 1) * P], c.xlo[:, k, t * P:(t + 1) * P]),
                                        (w_h[:, k, lo:hi], w_l[:, k, lo:hi]), k == 0, k == KD - 1)
                    mm.then_inc(ps.filled(("p", t)), 1)

            def keys(b, pos, heads_before):
                pe.wait_ge(*stacked.after(b, T))
                for g in range(NKV):
                    ps.wait_empty(pe, pos, ("k", g))
                    for t in range(T):
                        mm = pe.transpose(ps.ap(("k", g))[0:STK, t * P:(t + 1) * P], ks[:, t, g, :], c.ident[:, :])
                    mm.then_inc(ps.filled(("k", g)), 1)

            def heads(b, pos):
                pe.wait_ge(*v_in.after(b, 1))
                for s in steps:
                    if s[0] in "qe":
                        ps.wait_empty(pe, pos, s)
                    if s[0] == "q":
                        for t in range(T):
                            mm = pe.transpose(ps.ap(s)[0:STK, t * P:(t + 1) * P], qs[:, t, s[1], :], c.ident[:, :])
                        mm.then_inc(ps.filled(s), 1)
                    elif s[0] == "e":
                        h = s[1]
                        pe.wait_ge(*ps.released(pos, ("q", h)))
                        for j, n in ((0, 4), (1, NBL - 4)):
                            pe.matmul(ps.ap(s, j)[:, 0:n * P], idb[:, :], mask[:, 0:n * P], start=True, stop=False)
                        i = 0
                        for k in range(T):
                            n = 2 if k < T - 1 else 1
                            mm = pe.matmul(ps.ap(s, i // 4)[:, i % 4 * P:(i % 4 + n) * P],
                                           kT[:, h // 4, k * P:(k + 1) * P],
                                           qT[:, h % NQB, k * P:(k + n) * P], start=False, stop=k % 2 == 1)
                            i += n
                        mm.then_inc(ps.filled(s), 1)
                    elif s[0] == "o":
                        g, k = s[1:]
                        if k == 0:
                            ps.wait_empty(pe, pos, ("o", g))
                            for bank in range(2):
                                pe.matmul(ps.ap(("o", g), bank), zeros, mask[:, :], start=True, stop=False)
                            for kk in (2, 3):
                                pe.wait_ge(*ps.released(pos, ("e", 4 * g + kk)))
                        n = 2 if k < T - 1 else 1
                        for src, bank in ((v, 0), (None, 1)):
                            for j in range(4):
                                mm = pe.matmul(ps.ap(("o", g), bank)[j * HD:(j + 1) * HD, k * P:(k + n) * P],
                                               c.ones[:, 0:HD] if src is None else v[:, k, g * HD:(g + 1) * HD],
                                               probsT[:, (4 * g + j) % NPB, k // 2, k % 2 * 2 * P:(k % 2 * 2 + n) * P],
                                               start=False, stop=k == T - 1)
                        if k == T - 1:
                            mm.then_inc(ps.filled(("o", g)), 1)

            def output(b, pos):
                pe.wait_ge(*ps.released(at("heads", pos[0]), ("o", NKV - 1)))
                for t in range(T):
                    ps.wait_empty(pe, pos, ("y", t))
                    for k in range(KD):
                        mm = pe.matmul(ps.ap(("y", t)), outT[:, k, t * P:(t + 1) * P], wo[:, k, :],
                                       start=(k == 0), stop=(k == KD - 1))
                    mm.then_inc(ps.filled(("y", t)), 1)

            turns(pe, project, keys, heads, output)

        c.close(B)


def cross_attention(c):
    nc, d = c.nc, c.d
    HP = 2
    G = 16 // HP
    NW = HP * DX
    with ExitStack() as ctx:
        def sb(nm, shape, dt=F32):
            return ctx.enter_context(nc.sbuf_tensor(f"s5_{nm}", shape, dt))

        OQ, OKV = 0, KD * NW
        NX = OKV + KC * 2 * NW
        raw_x = sb("w_proj_raw", [P, NX])
        wx_h = sb("w_proj_hi", [P, 2, NX], F32R)
        wx_l = sb("w_proj_lo", [P, 2, NX], F32R)
        raw_o = sb("w_out_raw", [P, HP * D])
        wo_h = sb("w_out_hi", [P, 2, HP * D], F32R)
        wo_l = sb("w_out_lo", [P, 2, HP * D], F32R)
        gains = sb("gains", [P, 2, DX])
        gqk = sb("gain_product", [P, DX])
        gmax = sb("gain_max", [P, 1])
        bound = sb("minus_bound", [P, 1])
        cT = sb("ctxT", [P, KC, S])
        c_h = sb("ctxT_hi", [P, KC, S], F32R)
        c_l = sb("ctxT_lo", [P, KC, S], F32R)
        q = sb("q", [P, T, NW])
        kk = sb("k", [P, T, NW])
        v = sb("v", [P, T, NW])
        sq = sb("squares", [P, T, NW])
        ms = sb("mean_sq", [P, 2, T, HP])
        rs = sb("qk_rstd", [P, 2, T, HP])
        f_h = sb("qkT_hi", [P, 2, HP, S], F32R)
        f_l = sb("qkT_lo", [P, 2, HP, S], F32R)
        probsT = sb("probsT", [P, HP, T, S])
        psum2 = sb("probs_pair_sums", [P, 2, S])
        psum1 = sb("probs_sum", [P, HP, S])
        inv = sb("inv_sums", [P, HP, S])
        o_h = sb("outT_hi", [P, HP, S], F32R)
        o_l = sb("outT_lo", [P, HP, S], F32R)

        consts = c.sem("s5_gains_loaded")
        bound_ready = c.sem("s5_bound_ready")
        rawx_in = Count(c.sem("s5_w_proj_loaded"), 48)
        rawo_in = Count(c.sem("s5_w_out_loaded"), 16)
        wx_hi = Count(c.sem("s5_w_proj_hi_ready"), 1)
        wx_lo = Count(c.sem("s5_w_proj_lo_ready"), 1)
        wo_hi = Count(c.sem("s5_w_out_hi_ready"), 1)
        wo_lo = Count(c.sem("s5_w_out_lo_ready"), 1)
        ctx_in = Count(c.sem("s5_ctx_loaded"), 16)
        ctx_hi = Count(c.sem("s5_ctx_hi_ready"), 1)
        ctx_lo = c.s5_ctx_lo
        squared = {"q": Count(c.sem("s5_q_squared"), 1), "k": Count(c.sem("s5_k_squared"), 1)}
        ms_ready = {"q": Count(c.sem("s5_q_mean_sq_ready"), 1), "k": Count(c.sem("s5_k_mean_sq_ready"), 1)}
        rs_ready = {"q": Count(c.sem("s5_q_rstd_ready"), 1), "k": Count(c.sem("s5_k_rstd_ready"), 1)}
        q_gained = Count(c.sem("s5_q_gained"), 1)
        normed = {"q": Count(c.sem("s5_q_normed"), 1), "k": Count(c.sem("s5_k_normed"), 1)}
        f_hi = {"qT": Count(c.sem("s5_qT_hi_ready"), HP), "kT": Count(c.sem("s5_kT_hi_ready"), HP)}
        p_sum = Count(c.sem("s5_probs_summed"), HP)
        inv_ready = Count(c.sem("s5_inv_sums_ready"), HP)
        o_hi = Count(c.sem("s5_out_hi_ready"), HP)

        pa, pb = c.ps.part(), c.ps.part()
        pa_keys = [("q", 0), ("q", 1)] + [("kv", t) for t in range(T)] + [("qT", 0), ("qT", 1), ("kT", 0), ("kT", 1)]
        pa.open([(k, i % 3, 1) for i, k in enumerate(pa_keys)], outer=c.x_uses([0, 1, 2]))
        pb_keys = [("e", h, k) for h in range(HP) for k in range(T)] + [("y", t) for t in range(T)]
        uses = [(k, 3 + i % 3, 1) for i, k in enumerate(pb_keys)]
        pb.open(uses[:8] + [(("o", 0), 6, 1), (("o", 1), 7, 1), (("sum", 0), 3, 1), (("sum", 1), 4, 1)] + uses[8:])
        block = ctx.enter_context(nc.Block())

        def flat(ap):
            return ap.rearrange("p a n -> p (a n)")

        def side(buf, turn):
            return flat(buf[:, bass.ds(turn % 2, 1), :])

        def load_proj(sp, g):
            sp.dma_start(raw_x[:, OQ:OKV].rearrange("p (k n) -> p k n", k=KD),
                         d["l1x_wq"].rearrange("(k p) n -> p k n", p=P)[:, :, bass.ds(g * NW, NW)]).then_inc(rawx_in.sem, 16)
            kv = raw_x[:, OKV:].rearrange("p (k a n) -> p k a n", k=KC, a=2)
            for a, nm in ((0, "l1x_wk"), (1, "l1x_wv")):
                sp.dma_start(kv[:, :, a, :],
                             d[nm].rearrange("(k p) n -> p k n", p=P)[:, :, bass.ds(g * NW, NW)]).then_inc(rawx_in.sem, 16)

        def load_out(sp, g):
            sp.dma_start(raw_o[:, :].rearrange("p (h n) -> p h n", h=HP),
                         d["l1x_wo"].rearrange("(h p) n -> p h n", p=P)[:, bass.ds(g * HP, HP), :]).then_inc(rawo_in.sem, 16)

        def turns(eng, start, body, finish):
            start(0)
            body(0, (0, 0), None)
            with eng.Fori(0, B - 1) as b:
                with eng.Fori(0, G - 1) as g:
                    body(b, (b, b * G + (g + 1)), b * G + g)
                start(b + 1)
                body(b, (b + 1, b * G + G), b * G + (G - 1))
                finish(b)
            b = B - 1
            with eng.Fori(0, G - 1) as g:
                body(b, (b, g + (b * G + 1)), g + b * G)
            body(b, None, b * G + (G - 1))
            finish(b)

        @block.sync
        def _(sp):
            sp.dma_start(gains[:, 0, :], d["l1x_gq"].broadcast_to([P, DX])).then_inc(consts, 16)
            sp.dma_start(gains[:, 1, :], d["l1x_gk"].broadcast_to([P, DX])).then_inc(consts, 16)
            load_proj(sp, 0)
            load_out(sp, 0)

            def next_proj(turn, g):
                sp.wait_ge(*wx_lo.after(turn, 1))
                load_proj(sp, g)

            def next_out(turn, g):
                sp.wait_ge(*wo_lo.after(turn, 1))
                load_out(sp, g)

            def load_sequence(b):
                c.sync_load_x(sp, b)
                sp.wait_ge(*ctx_lo.after(b, 0))
                sp.dma_start(cT[:, :, :], d["ctxT"][bass.ds(b, 1)].rearrange("a (k p) s -> p (a k) s", p=P)) \
                  .then_inc(ctx_in.sem, 16)

            load_sequence(0)
            next_proj(0, 1)
            with sp.Fori(0, B - 1) as b:
                load_sequence(b + 1)
                with sp.Fori(0, G - 1) as g:
                    next_out(b * G + g, g + 1)
                    next_proj(b * G + g + 1, (g + 2) % G)
                next_out(b * G + (G - 1), 0)
                next_proj(b * G + G, 1)
            with sp.Fori(0, G - 1) as g:
                next_out(g + (B - 1) * G, g + 1)
                next_proj(g + ((B - 1) * G + 1), (g + 2) % G)
            next_out(B * G - 1, 0)

        @block.gpsimd
        def _(pool):
            def lo(out, raw, hi, hi_ready, done, turn, piece=None):
                pool.wait_ge(*hi_ready.after(turn, 1))
                pool.wait_ge(c.pool_consts, 1)
                pool.tensor_tensor(out, raw, hi.bitcast(F32), ALU.subtract).then_inc(done.sem, 1)

            lo(wx_l[:, 0, :], raw_x[:, :], wx_h[:, 0, :], wx_hi, wx_lo, 0)
            lo(wo_l[:, 0, :], raw_o[:, :], wo_h[:, 0, :], wo_hi, wo_lo, 0)

            def rstd(j, nm, turn):
                pool.wait_ge(*ms_ready[nm].after(turn, 1))
                pool.tensor_tensor(rs[:, j, :, :], ms[:, j, :, :],
                                   c.mhalf[:, 0:T * HP].rearrange("p (t h) -> p t h", h=HP), ALU.pow) \
                    .then_inc(rs_ready[nm].sem, 1)

            def body(b, x, y):
                if y is not None:
                    for h in range(HP):
                        pool.wait_ge(*pb.released(y, ("e", h, T - 1)))
                        pool.tensor_tensor(psum2[:, :, :], probsT[:, h, 0:2, :], probsT[:, h, 2:4, :], ALU.add)
                        pool.drain()
                        pool.tensor_tensor(psum1[:, h, :], psum2[:, 0, :], psum2[:, 1, :], ALU.add).then_inc(p_sum.sem, 1)
                        pool.drain()
                if x is not None:
                    tx = x[1]
                    pool.wait_ge(*pa.released(x, ("q", 1)))
                    q3 = q[:, :, :].rearrange("p t (h n) -> p (t h) n", h=HP)
                    pool.tensor_tensor(q3, q3, gqk[:, :].unsqueeze(1).broadcast_to([P, T * HP, DX]), ALU.mult) \
                        .then_inc(q_gained.sem, 1)
                    rstd(0, "q", tx)
                    rstd(1, "k", tx)
                    lo(side(wx_l, tx + 1), raw_x[:, :], side(wx_h, tx + 1), wx_hi, wx_lo, tx + 1)
                if y is not None:
                    lo(side(wo_l, y + 1), raw_o[:, :], side(wo_h, y + 1), wo_hi, wo_lo, y + 1)

            turns(pool, nothing, body, lambda b: c.pool_rstd(pool, b))

        @block.scalar
        def _(act):
            act.wait_ge(*rawx_in.after(0, 48))
            act.activation(wx_h[:, 0, :], raw_x[:, :], ACT.Copy).then_inc(wx_hi.sem, 1)
            act.wait_ge(*rawo_in.after(0, 16))
            act.activation(wo_h[:, 0, :], raw_o[:, :], ACT.Copy).then_inc(wo_hi.sem, 1)
            act.wait_ge(bound_ready, 1)

            def body(b, x, y):
                def queries(i):
                    act.wait_ge(*pa.full(x, ("q", i)))
                    s = act.activation(flat(sq[:, 2 * i:2 * i + 2, :]), pa.ap(("q", i)), ACT.Square)
                    if i == 1:
                        s.then_inc(squared["q"].sem, 1)
                    act.activation(flat(q[:, 2 * i:2 * i + 2, :]), pa.ap(("q", i)), ACT.Copy) \
                       .then_inc(pa.freed(("q", i)), 1)

                def keys_values(t):
                    act.wait_ge(*pa.full(x, ("kv", t)))
                    if t == 0:
                        act.wait_ge(*ms_ready["q"].after(x[1], 1))
                    s = act.activation(sq[:, t, :], pa.ap(("kv", t))[:, 0:NW], ACT.Square)
                    if t == T - 1:
                        s.then_inc(squared["k"].sem, 1)
                    act.activation(kk[:, t, :], pa.ap(("kv", t))[:, 0:NW], ACT.Copy)
                    act.activation(v[:, t, :], pa.ap(("kv", t))[:, NW:], ACT.Copy).then_inc(pa.freed(("kv", t)), 1)

                def transposed_hi(nm, j):
                    for h in range(HP):
                        act.wait_ge(*pa.full(x, (nm, h)))
                        act.activation(f_h[:, j, h, :], pa.ap((nm, h)), ACT.Copy).then_inc(f_hi[nm].sem, 1)

                if y is not None:
                    for h in range(HP):
                        for k in range(T):
                            act.wait_ge(*pb.full(y, ("e", h, k)))
                            act.activation(probsT[:, h, k, :], pb.ap(("e", h, k)), ACT.Exp, bias=bound[:, 0:1],
                                           scale=DX ** -0.5).then_inc(pb.freed(("e", h, k)), 1)
                if x is not None:
                    queries(0)
                    act.wait_ge(*rawx_in.after(x[1], 96))
                    act.wait_ge(bound_ready, 1)
                    act.activation(side(wx_h, x[1] + 1), raw_x[:, :], ACT.Copy).then_inc(wx_hi.sem, 1)
                    queries(1)

                def outputs_hi(h):
                    act.wait_ge(*inv_ready.after(y, h + 1))
                    act.activation(o_h[:, h, :], inv[:, h, :], ACT.Copy).then_inc(o_hi.sem, 1)

                if y is not None:
                    outputs_hi(0)
                    outputs_hi(1)
                if x is not None:
                    for t in range(T):
                        keys_values(t)
                    transposed_hi("qT", 1)
                if y is not None:
                    act.wait_ge(*rawo_in.after(y, 32))
                    act.wait_ge(bound_ready, 1)
                    act.activation(side(wo_h, y + 1), raw_o[:, :], ACT.Copy).then_inc(wo_hi.sem, 1)
                if x is not None:
                    transposed_hi("kT", 0)

            def start(b):
                c.act_x_hi(act, b, (b, b * G), pa)
                act.wait_ge(*ctx_in.after(b, 16))
                act.activation(c_h[:, :, :], cT[:, :, :], ACT.Copy).then_inc(ctx_hi.sem, 1)

            turns(act, start, body, nothing)

        @block.vector
        def _(dve):
            dve.wait_ge(consts, 32)
            dve.tensor_tensor(gqk[:, :], gains[:, 0, :], gains[:, 1, :], ALU.mult)
            dve.drain()
            dve.tensor_reduce(gmax[:, :], gqk[:, :], AX.X, ALU.max, apply_absolute_value=True)
            dve.drain()
            dve.tensor_scalar(bound[:, :], gmax[:, :], -DX ** 0.5, None, ALU.mult).then_inc(bound_ready, 1)

            def body(b, x, y):
                def mean_squares(j, nm):
                    dve.wait_ge(*squared[nm].after(x[1], 1))
                    dve.tensor_reduce(ms[:, j, :, :], sq[:, :, :].rearrange("p t (h n) -> p t h n", h=HP), AX.X, ALU.add)
                    dve.drain()
                    dve.tensor_scalar(ms[:, j, :, :], ms[:, j, :, :], 1.0 / DX, 1e-5, ALU.mult, ALU.add) \
                       .then_inc(ms_ready[nm].sem, 1)

                def normalise(j, nm, buf, raw_out):
                    dve.wait_ge(*rs_ready[nm].after(x[1], 1))
                    dve.wait_ge(*raw_out)
                    x3 = buf[:, :, :].rearrange("p t (h n) -> p (t h) n", h=HP)
                    dve.tensor_tensor(x3, x3, rs[:, j, :, :].rearrange("p t h -> p (t h)").unsqueeze(2)
                                      .broadcast_to([P, T * HP, DX]), ALU.mult).then_inc(normed[nm].sem, 1)

                def outputs(h):
                    dve.wait_ge(*pb.full(y, ("sum", h)))
                    dve.reciprocal(inv[:, h, :], pb.ap(("sum", h))).then_inc(pb.freed(("sum", h)), 1)
                    dve.wait_ge(*pb.released(y, ("sum", h)))
                    dve.wait_ge(*pb.full(y, ("o", h)))
                    dve.tensor_tensor(inv[:, h, :], pb.ap(("o", h)), inv[:, h, :], ALU.mult).then_inc(inv_ready.sem, 1)

                def outputs_lo(h):
                    dve.wait_ge(*o_hi.after(y, h + 1))
                    dve.tensor_tensor(o_l[:, h, :], inv[:, h, :], o_h[:, h, :].bitcast(F32), ALU.subtract) \
                       .then_inc(pb.freed(("o", h)), 1)

                def transposed_lo(nm, j):
                    for h in range(HP):
                        dve.wait_ge(*f_hi[nm].after(x[1], h + 1))
                        dve.tensor_tensor(f_l[:, j, h, :], pa.ap((nm, h)), f_h[:, j, h, :].bitcast(F32), ALU.subtract) \
                           .then_inc(pa.freed((nm, h)), 1)

                if y is not None:
                    outputs(0)
                    outputs(1)
                if x is not None:
                    mean_squares(0, "q")
                if y is not None:
                    outputs_lo(0)
                    outputs_lo(1)
                if x is not None:
                    normalise(0, "q", q, q_gained.after(x[1], 1))
                    mean_squares(1, "k")
                    transposed_lo("qT", 1)
                    normalise(1, "k", kk, pa.released(x, ("kv", T - 1)))
                def add_out(t):
                    xt = c.x[:, b * T + t, :]
                    dve.wait_ge(*pb.full(y, ("y", t)))
                    dve.tensor_tensor(xt, pb.ap(("y", t)), xt, ALU.add).then_inc(pb.freed(("y", t)), 1)

                if y is not None:
                    for t in range(T - 1):
                        add_out(t)
                if x is not None:
                    transposed_lo("kT", 0)
                if y is not None:
                    add_out(T - 1)

            def start(b):
                c.dve_x_lo(dve, b, (b, b * G), pa)
                dve.wait_ge(*ctx_hi.after(b, 1))
                dve.tensor_tensor(c_l[:, :, :], cT[:, :, :], c_h[:, :, :].bitcast(F32), ALU.subtract).then_inc(ctx_lo.sem, 1)

            def finish(b):
                dve.drain()
                for t in range(T):
                    dve.bn_stats(c.stats[:, t, :], c.x[:, b * T + t, :])
                c.dve_normalize(dve, b)

            turns(dve, start, body, finish)

        @block.tensor
        def _(pe):
            def body(b, x, y):
                def wx(off, n):
                    return tuple(side(a, x[1])[:, off:off + n] for a in (wx_h, wx_l))

                def queries(i):
                    if i == 0:
                        pe.wait_ge(*wx_lo.after(x[1], 1))
                        pe.wait_ge(*ctx_lo.after(x[0], 1))
                    pa.wait_empty(pe, x, ("q", i))
                    for t in (2 * i, 2 * i + 1):
                        for k in range(KD):
                            mm = split3(pe, pa.ap(("q", i))[:, t % 2 * NW:(t % 2 + 1) * NW],
                                        (c.xhi[:, k, t * P:(t + 1) * P], c.xlo[:, k, t * P:(t + 1) * P]),
                                        wx(OQ + k * NW, NW), k == 0, k == KD - 1)
                    mm.then_inc(pa.filled(("q", i)), 1)

                def keys_values(t):
                    pa.wait_empty(pe, x, ("kv", t))
                    for k in range(KC):
                        mm = split3(pe, pa.ap(("kv", t)), (c_h[:, k, t * P:(t + 1) * P], c_l[:, k, t * P:(t + 1) * P]),
                                    wx(OKV + k * 2 * NW, 2 * NW), k == 0, k == KC - 1)
                    mm.then_inc(pa.filled(("kv", t)), 1)

                def transposed(nm, src, done):
                    pe.wait_ge(*done.after(x[1], 1))
                    for h in range(HP):
                        pa.wait_empty(pe, x, (nm, h))
                        for t in range(T):
                            mm = pe.transpose(pa.ap((nm, h))[:, t * P:(t + 1) * P], src[:, t, h * DX:(h + 1) * DX],
                                              c.ident[:, :])
                        mm.then_inc(pa.filled((nm, h)), 1)

                def scores(h):
                    pe.wait_ge(*pa.released((b, y), ("kT", h)))
                    for k in range(T):
                        pb.wait_empty(pe, y, ("e", h, k))
                        split3(pe, pb.ap(("e", h, k)), (f_h[:, 0, h, k * P:(k + 1) * P], f_l[:, 0, h, k * P:(k + 1) * P]),
                               (f_h[:, 1, h, :], f_l[:, 1, h, :]), True, True).then_inc(pb.filled(("e", h, k)), 1)

                def values(h):
                    pb.wait_empty(pe, y, ("o", h))
                    for k in range(T):
                        pe.wait_ge(*pb.released(y, ("e", h, k)))
                        mm = pe.matmul(pb.ap(("o", h)), v[:, k, h * DX:(h + 1) * DX], probsT[:, h, k, :],
                                       start=(k == 0), stop=(k == T - 1))
                    mm.then_inc(pb.filled(("o", h)), 1)

                def sums(h):
                    pb.wait_empty(pe, y, ("sum", h))
                    pe.wait_ge(*p_sum.after(y, h + 1))
                    pe.matmul(pb.ap(("sum", h)), c.ones[:, :], psum1[:, h, :], start=True, stop=True) \
                      .then_inc(pb.filled(("sum", h)), 1)

                def project_out(t):
                    pb.wait_empty(pe, y, ("y", t))
                    for h in range(HP):
                        mm = split3(pe, pb.ap(("y", t)), (o_h[:, h, t * P:(t + 1) * P], o_l[:, h, t * P:(t + 1) * P]),
                                    tuple(side(a, y)[:, h * D:(h + 1) * D] for a in (wo_h, wo_l)), h == 0, h == HP - 1)
                    mm.then_inc(pb.filled(("y", t)), 1)

                if y is not None:
                    scores(0)
                    scores(1)
                    values(0)
                if x is not None:
                    queries(0)
                if y is not None:
                    sums(0)
                    values(1)
                    sums(1)
                if x is not None:
                    queries(1)
                    for t in range(T):
                        keys_values(t)
                    transposed("qT", q, normed["q"])
                if y is not None:
                    pe.wait_ge(*wo_lo.after(y, 1))
                    for h in range(HP):
                        pe.wait_ge(*pb.released(y, ("o", h)))
                    for t in range(T - 1):
                        project_out(t)
                if x is not None:
                    transposed("kT", kk, normed["k"])
                if y is not None:
                    project_out(T - 1)

            def start(b):
                c.pe_turn_x(pe, b, (b, b * G), pa)

            turns(pe, start, body, nothing)

        pa.close(B * G, B)
        pb.close(B * G)
        c.close_common()


def workspace_rounds(c):
    nc, d, ps = c.nc, c.d, c.ps
    g = Buffers()
    with ExitStack() as ctx:
        def sb(nm, shape, dt=F32):
            return ctx.enter_context(nc.sbuf_tensor(f"s6_{nm}", shape, dt))

        g.xw = sb("x_work", [P, B * T, D])
        g.cw = sb("compete", [P, KD, SB])
        g.cw_h = sb("compete_hi", [P, KD, SB], F32R)
        g.cw_l = sb("compete_lo", [P, KD, SB], F32R)
        g.cb = sb("compete_b", [P, 1])
        g.pre = sb("pre_w", [P, KD])
        g.ww, g.wk, g.wv, g.wq, g.wo = (sb(nm, [P, KD, D]) for nm in ("write_w", "wk", "wv", "wq", "wo"))
        g.wb, g.post, g.ob = (sb(nm, [P, D]) for nm in ("write_b", "post_w", "out_b"))
        g.bqkv = sb("b_qkv", [P, 3, NP])
        g.bq_rep = sb("bq_replicated", [P, NP, P])
        g.ssq = sb("sum_sq", [P, T])
        g.ms = sb("mean_sq", [P, T])
        g.rs = sb("row_rstd", [P, T])
        g.lT = sb("slot_logits_T", [P, S])
        g.ltok = sb("slot_logits_by_token", [P, T, B * SB])
        g.lrow = sb("slot_logits", [P, S + 8])
        g.rest = sb("slot_logits_rest", [P, S + 8])
        g.mask = sb("top_mask", [P, S])
        g.top = sb("top8", [P, 8])
        g.nmax = sb("neg_max", [P, 1])
        g.ssum = sb("row_sum", [P, 1])
        g.gw = sb("slot_weights", [P, S])
        g.gt = sb("slot_weights_by_token", [P, T, B * SB])
        g.gx = sb("gathered", [P, D])
        g.gxT = sb("gatheredT", [P, KD, B * SB])
        g.ws = sb("slots", [P, D])
        g.wsn = sb("slots_new", [P, D])
        g.wsT = sb("slotsT", [P, KD, B * SB])
        g.bdk = sb("kkT_by_head", [P, NP, B, SB])
        g.bdv = sb("vvT_by_head", [P, NP, B, SB])
        g.m_h = sb("folded_k_hi", [P, KD, B, P], F32R)
        g.m_l = sb("folded_k_lo", [P, KD, B, P], F32R)
        g.squares = [g.lrow, g.rest, g.mask, g.gw]
        g.mc_h = sb("folded_k_hi_now", [P, KD, P], F32R)
        g.mc_l = sb("folded_k_lo_now", [P, KD, P], F32R)
        g.lTs = g.gx
        g.lb = sb("logit_bias", [P, B, P])
        g.u = sb("folded_v", [P, B, D])
        g.lg = sb("token_logits", [P, T, P])
        g.mx8 = sb("token_max", [P, T * H6])
        g.att = sb("att", [P, T, P])
        g.attT = sb("attT", [P, S])

        def cnt(name, per=1):
            return Count(c.sem("s6_" + name), per)

        weights = c.sem("s6_weights_loaded")
        g.large = c.sem("s6_large_weights_loaded")
        consts = c.sem("s6_constants_set")
        cw_hi_s, cw_lo_s = c.sem("s6_compete_hi_ready"), c.sem("s6_compete_lo_ready")
        g.ssq_ready = c.s6_ssq
        g.ms_ready = c.s6_ms
        g.rs_ready = cnt("x_rstd_ready")
        g.top_found, g.exps, g.weighted = cnt("top_found"), cnt("slot_exps_ready"), cnt("slot_weights_ready")
        g.ws_sum, g.ws_sq, g.ws_ms, g.ws_rs, g.ws_ready = (cnt(x) for x in (
            "slots_added", "slots_squared", "slots_mean_sq_ready", "slots_rstd_ready", "slots_ready"))
        g.m_hi = cnt("folded_k_hi_ready", KD)
        g.shifted, g.att_exps, g.att_ready = cnt("token_logits_shifted"), cnt("token_exps_ready"), cnt("att_ready")
        g.added = cnt("y_added", T)
        g.m_cur = cnt("folded_k_in_place")

        with ExitStack() as blk:
            block = blk.enter_context(nc.Block())

            @block.sync
            def _(sp):
                for dst, nm in ((g.wb, "l1f_wb"), (g.post, "l1f_post"), (g.ob, "l1f_ob")):
                    sp.dma_start(dst[:, :], d[nm].broadcast_to([P, D])).then_inc(weights, 16)
                for j, nm in enumerate(("l1f_bq", "l1f_bk", "l1f_bv")):
                    sp.dma_start(g.bqkv[:, j, :], d[nm]).then_inc(weights, 16)
                sp.dma_start(g.pre[:, :], d["l1f_pre"]).then_inc(weights, 16)
                sp.wait_ge(consts, 2)
                sp.dma_start(g.cw[:, :, 0:NS], d["l1f_cwT"].rearrange("(k p) n -> p k n", p=P)).then_inc(weights, 16)
                for b in range(B):
                    sp.dma_start(g.cb[b * SB:b * SB + NS, :], d["l1f_cb"]).then_inc(weights, 16)
                    sp.dma_start(g.ws[b * SB:b * SB + NS, :], d["l1f_ws"]).then_inc(weights, 16)
                for dst, nm in ((g.ww, "l1f_wwT"), (g.wk, "l1f_wkT"), (g.wv, "l1f_wvT"), (g.wq, "l1f_wq"), (g.wo, "l1f_woT")):
                    sp.dma_start(dst[:, :, :], d[nm].rearrange("(k p) n -> p k n", p=P)).then_inc(g.large, 16)
                sp.wait_ge(weights, 16 * 16)

            @block.gpsimd
            def _(pool):
                for tns in (g.cw[:, :, :], g.cb[:, :], g.ws[:, :], g.lT[:, :]):
                    pool.memset(tns, 0.0)
                    pool.drain()
                pool.memset(g.lrow[:, :], LOWEST).then_inc(consts, 1)

            @block.vector
            def _(dve):
                dve.memset(g.bdk[:, :, :, :], 0.0)
                dve.memset(g.bdv[:, :, :, :], 0.0).then_inc(consts, 1)
                dve.wait_ge(weights, 16 * 16)
                for k in range(KD):
                    dve.tensor_scalar(g.cw[:, k, :], g.cw[:, k, :], g.pre[:, k:k + 1], None, ALU.mult)
                    dve.tensor_scalar(g.bq_rep[:, k, :], c.ones[:, :], g.bqkv[:, 0, k:k + 1], None, ALU.mult)
                dve.drain()
                dve.tensor_copy(g.cw_h[:, :, :], g.cw[:, :, :])
                dve.drain()
                dve.tensor_tensor(g.cw_l[:, :, :], g.cw[:, :, :], g.cw_h[:, :, :].bitcast(F32), ALU.subtract).then_inc(cw_lo_s, 1)
                dve.wait_ge(cw_lo_s, 1)

        for r in range(2):
            g.src = c.x if r == 0 else g.xw
            g.last_round = r == 1
            workspace_collect(c, g)
            workspace_slots(c, g)
            workspace_attend(c, g)




def pow_rstd(c, pool, out, src, n):
    return pool.tensor_tensor(out, src, c.mhalf[:, 0:n], ALU.pow)


def workspace_collect(c, g):
    nc, ps = c.nc, c.ps
    ps.open(c.x_uses([0, 1]) + [(("lT", 0), 3, 1), (("l", 0), 2, 1)])
    with ExitStack() as ctx:
        block = ctx.enter_context(nc.Block())

        @block.sync
        def _(sp):
            with sp.Fori(0, B) as b:
                c.sync_load_x(sp, b, g.src, g.ssq_ready)

        @block.gpsimd
        def _(pool):
            with pool.Fori(0, B) as b:
                pool.wait_ge(*g.ms_ready.after(b, 1))
                pow_rstd(c, pool, g.rs[:, :], g.ms[:, :], T).then_inc(g.rs_ready.sem, 1)

        @block.scalar
        def _(act):
            with act.Fori(0, B) as b:
                c.act_x_hi(act, b)
                act.wait_ge(*g.ms_ready.after(b, 0))
                for t in range(T):
                    s = act.activation(g.squares[t][:, 0:D], c.xcur[:, t, :], ACT.Square, accum_out=g.ssq[:, t:t + 1])
                s.then_inc(g.ssq_ready.sem, 1)
                act.wait_ge(*ps.full(b, ("lT", 0)))
                act.activation(g.lT[0:SB, :], ps.ap(("lT", 0))[0:SB, :], ACT.Copy).then_inc(ps.freed(("lT", 0)), 1)

        @block.vector
        def _(dve):
            with dve.Fori(0, B) as b:
                c.dve_x_lo(dve, b)
                dve.wait_ge(*g.ssq_ready.after(b, 1))
                dve.tensor_scalar(g.ms[:, :], g.ssq[:, :], 1.0 / D, EPS6, ALU.mult, ALU.add).then_inc(g.ms_ready.sem, 1)
                dve.wait_ge(*ps.full(b, ("l", 0)))
                dve.wait_ge(*g.rs_ready.after(b, 1))
                dve.tensor_tensor(g.ltok[:, :, bass.ds(b * SB, SB)],
                                  ps.ap(("l", 0)).rearrange("p (t s) -> p t s", t=T)[:, :, 0:SB],
                                  g.rs[:, :].unsqueeze(2).broadcast_to([P, T, SB]), ALU.mult).then_inc(ps.freed(("l", 0)), 1)

        @block.tensor
        def _(pe):
            with pe.Fori(0, B) as b:
                c.pe_turn_x(pe, b)
                c.wait_xT(pe, b)
                ps.wait_empty(pe, b, ("lT", 0))
                for k in range(KD):
                    mm = split3(pe, ps.ap(("lT", 0))[0:SB, :], (g.cw_h[:, k, :], g.cw_l[:, k, :]),
                                (c.xhi[:, k, :], c.xlo[:, k, :]), k == 0, k == KD - 1)
                mm.then_inc(ps.filled(("lT", 0)), 1)
                ps.wait_empty(pe, b, ("l", 0))
                pe.wait_ge(*ps.released(b, ("lT", 0)))
                for t in range(T):
                    mm = pe.transpose(ps.ap(("l", 0))[:, t * P:(t + 1) * P], g.lT[:, t * P:(t + 1) * P], c.ident[:, :])
                mm.then_inc(ps.filled(("l", 0)), 1)

    ps.close(B)
    for x in (c.cur, c.xT_hi, g.ssq_ready, g.ms_ready, g.rs_ready):
        x.close(B)


def workspace_slots(c, g):
    nc, ps = c.nc, c.ps
    BS = B * SB
    banks = [("L", 0), ("G", 1), ("gx", 2), ("gxT", 3), ("w", 4), ("wsT", 5), ("k", 6), ("v", 7)]
    banks += [(("m", m), m) for m in range(KD)] + [("lb", 4)] + [(("u", b), (5, 6, 7, 0)[b]) for b in range(B)]
    ps.open([(k, bank, 1) for k, bank in banks])

    with ExitStack() as ctx:
        block = ctx.enter_context(nc.Block())

        @block.gpsimd
        def _(pool):
            pool.wait_ge(*g.ws_ms.after(0, 1))
            pow_rstd(c, pool, g.rs[:, 0:1], g.ms[:, 0:1], 1).then_inc(g.ws_rs.sem, 1)

        @block.scalar
        def _(act):
            act.wait_ge(*ps.full(0, "L"))
            act.activation(g.lrow[:, 0:S], ps.ap("L"), ACT.Identity, bias=g.cb[:, 0:1]).then_inc(ps.freed("L"), 1)
            act.wait_ge(*g.top_found.after(0, 1))
            act.activation(g.gw[:, :], g.lrow[:, 0:S], ACT.Exp, bias=g.nmax[:, 0:1]).then_inc(g.exps.sem, 1)
            act.wait_ge(*ps.full(0, "gx"))
            act.activation(g.gx[:, :], ps.ap("gx"), ACT.Copy).then_inc(ps.freed("gx"), 1)
            act.wait_ge(*g.ws_sum.after(0, 1))
            act.activation(g.attT[:, 0:D], g.wsn[:, :], ACT.Square, accum_out=g.ssq[:, 0:1]).then_inc(g.ws_sq.sem, 1)
            act.wait_ge(*ps.full(0, "wsT"))
            act.activation(g.wsT[:, :, :].rearrange("p k n -> p (k n)"), ps.ap("wsT"), ACT.Copy) \
               .then_inc(ps.freed("wsT"), 1)
            for m in range(KD):
                act.wait_ge(*ps.full(0, ("m", m)))
                act.activation(g.m_h[:, m, :, :].rearrange("p b (q n) -> p q b n", q=NP),
                               ps.ap(("m", m)).rearrange("p (q b n) -> p q b n", q=NP, b=B), ACT.Copy) \
                   .then_inc(g.m_hi.sem, 1)
            for b in range(B):
                act.wait_ge(*ps.full(0, ("u", b)))
                act.activation(g.u[:, b, :], ps.ap(("u", b)), ACT.Copy).then_inc(ps.freed(("u", b)), 1)

        @block.vector
        def _(dve):
            dve.wait_ge(*ps.released(0, "L"))
            dve.max(g.top[:, :], g.lrow[:, :])
            dve.drain()
            dve.tensor_scalar(g.nmax[:, :], g.top[:, 0:1], -1.0, None, ALU.mult)
            dve.memset(g.top[:, K6:], LOWEST)
            dve.drain()
            dve.match_replace(g.rest[:, :], g.top[:, :], g.lrow[:, :], LOWEST)
            dve.drain()
            dve.tensor_tensor(g.mask[:, :], g.rest[:, 0:S], g.lrow[:, 0:S], ALU.not_equal).then_inc(g.top_found.sem, 1)
            dve.wait_ge(*g.exps.after(0, 1))
            dve.wait_ge(*g.top_found.after(0, 1))
            dve.tensor_tensor(g.gw[:, :], g.gw[:, :], g.mask[:, :], ALU.mult)
            dve.drain()
            dve.tensor_reduce(g.ssum[:, :], g.gw[:, :], AX.X, ALU.add)
            dve.drain()
            dve.reciprocal(g.ssum[:, :], g.ssum[:, :])
            dve.drain()
            dve.tensor_scalar(g.gw[:, :], g.gw[:, :], g.ssum[:, 0:1], None, ALU.mult).then_inc(g.weighted.sem, 1)
            dve.wait_ge(*ps.full(0, "G"))
            dve.tensor_copy(g.gt[:, :, :].rearrange("p t n -> p (t n)"), ps.ap("G")).then_inc(ps.freed("G"), 1)
            dve.wait_ge(*ps.full(0, "gxT"))
            dve.tensor_copy(g.gxT[:, :, :].rearrange("p t n -> p (t n)"), ps.ap("gxT")).then_inc(ps.freed("gxT"), 1)
            dve.wait_ge(*ps.full(0, "w"))
            dve.tensor_tensor(g.wsn[:, :], ps.ap("w"), g.wb[:, :], ALU.add).then_inc(ps.freed("w"), 1)
            dve.drain()
            dve.tensor_tensor(g.wsn[:, :], g.wsn[:, :], g.ws[:, :], ALU.add).then_inc(g.ws_sum.sem, 1)
            dve.wait_ge(*g.ws_sq.after(0, 1))
            dve.tensor_scalar(g.ms[:, 0:1], g.ssq[:, 0:1], 1.0 / D, EPS6, ALU.mult, ALU.add).then_inc(g.ws_ms.sem, 1)
            dve.wait_ge(*g.ws_rs.after(0, 1))
            dve.tensor_scalar(g.ws[:, :], g.wsn[:, :], g.rs[:, 0:1], None, ALU.mult)
            dve.drain()
            dve.tensor_tensor(g.ws[:, :], g.ws[:, :], g.post[:, :], ALU.mult).then_inc(g.ws_ready.sem, 1)
            for key, dst, j in (("k", g.bdk, 1), ("v", g.bdv, 2)):
                dve.wait_ge(*ps.full(0, key))
                for hh in range(2):
                    rows = slice(hh * W6, (hh + 1) * W6)
                    o = dve.tensor_tensor(dst[rows, :, :, hh * NS:(hh + 1) * NS],
                                          ps.ap(key)[rows, :].rearrange("p (q b n) -> p q b n", q=NP, b=B)[:, :, :, 0:NS],
                                          g.bqkv[rows, j, :].unsqueeze(2).unsqueeze(3).broadcast_to([W6, NP, B, NS]),
                                          ALU.add)
                o.then_inc(ps.freed(key), 1)
            for m in range(KD):
                dve.wait_ge(*g.m_hi.after(0, m + 1))
                dve.tensor_tensor(g.m_l[:, m, :, :].rearrange("p b (q n) -> p q b n", q=NP),
                                  ps.ap(("m", m)).rearrange("p (q b n) -> p q b n", q=NP, b=B),
                                  g.m_h[:, m, :, :].bitcast(F32).rearrange("p b (q n) -> p q b n", q=NP), ALU.subtract) \
                   .then_inc(ps.freed(("m", m)), 1)
            dve.wait_ge(*ps.full(0, "lb"))
            dve.tensor_copy(g.lb[:, :, :].rearrange("p b (q n) -> p q b n", q=NP),
                            ps.ap("lb").rearrange("p (q b n) -> p q b n", q=NP, b=B)).then_inc(ps.freed("lb"), 1)

        @block.tensor
        def _(pe):
            def transposes(key, src_of):
                for t in range(T):
                    mm = pe.transpose(ps.ap(key)[:, t * P:(t + 1) * P], src_of(t), c.ident[:, :])
                mm.then_inc(ps.filled(key), 1)

            pe.wait_ge(g.large, 16 * 5)
            transposes("L", lambda t: g.ltok[:, t, :])
            pe.wait_ge(*g.weighted.after(0, 1))
            transposes("G", lambda t: g.gw[:, t * P:(t + 1) * P])
            pe.wait_ge(*ps.released(0, "G"))
            for t in range(T):
                for b in range(B):
                    mm = pe.matmul(ps.ap("gx")[b * SB:(b + 1) * SB, :], g.gt[:, t, b * SB:(b + 1) * SB],
                                   g.src[:, b * T + t, :], start=(t == 0), stop=(t == T - 1))
            mm.then_inc(ps.filled("gx"), 1)
            pe.wait_ge(*ps.released(0, "gx"))
            transposes("gxT", lambda t: g.gx[:, t * P:(t + 1) * P])
            pe.wait_ge(*ps.released(0, "gxT"))
            for k in range(KD):
                mm = pe.matmul(ps.ap("w"), g.gxT[:, k, :], g.ww[:, k, :], start=(k == 0), stop=(k == KD - 1))
            mm.then_inc(ps.filled("w"), 1)
            pe.wait_ge(*g.ws_ready.after(0, 1))
            transposes("wsT", lambda t: g.ws[:, t * P:(t + 1) * P])
            pe.wait_ge(*ps.released(0, "wsT"))
            for key, w in (("k", g.wk), ("v", g.wv)):
                for p in range(NP):
                    for k in range(KD):
                        mm = pe.matmul(ps.ap(key)[:, p * P:(p + 1) * P], w[:, k, p * P:(p + 1) * P], g.wsT[:, k, :],
                                       start=(k == 0), stop=(k == KD - 1))
                mm.then_inc(ps.filled(key), 1)
            pe.wait_ge(*ps.released(0, "k"))
            for m in range(KD):
                for p in range(NP):
                    mm = pe.matmul(ps.ap(("m", m))[:, p * P:(p + 1) * P], g.wq[:, p, m * P:(m + 1) * P],
                                   g.bdk[:, p, :, :].rearrange("p b n -> p (b n)"), start=True, stop=True)
                mm.then_inc(ps.filled(("m", m)), 1)
            for p in range(NP):
                mm = pe.matmul(ps.ap("lb")[:, p * P:(p + 1) * P], g.bq_rep[:, p, :],
                               g.bdk[:, p, :, :].rearrange("p b n -> p (b n)"), start=True, stop=True)
            mm.then_inc(ps.filled("lb"), 1)
            pe.wait_ge(*ps.released(0, "v"))
            for b in range(B):
                if b == 3:
                    ps.wait_empty(pe, 0, ("u", b))
                for p in range(NP):
                    mm = pe.matmul(ps.ap(("u", b))[p * SB:(p + 1) * SB, :], g.bdv[:, p, b, :], g.wo[:, p, :],
                                   start=True, stop=True)
                mm.then_inc(ps.filled(("u", b)), 1)

    ps.close(1)
    for x in (g.top_found, g.exps, g.weighted, g.ws_sum, g.ws_sq, g.ws_ms, g.ws_rs, g.ws_ready, g.m_hi):
        x.close(1)


def workspace_attend(c, g):
    nc, ps = c.nc, c.ps
    ps.open(c.x_uses([0, 1]) + [(("lT", 0), 2, 1), (("l", 0), 2, 1), (("aT", 0), 3, 1)] + c.y_uses([4, 5, 6, 7]))

    def heads(ap):
        return ap.rearrange("p t (h n) -> p (t h) n", n=NS)

    with ExitStack() as ctx:
        block = ctx.enter_context(nc.Block())

        @block.sync
        def _(sp):
            with sp.Fori(0, B) as b:
                c.sync_load_x(sp, b, g.src)

        @block.gpsimd
        def _(pool):
            with pool.Fori(0, B) as b:
                pool.wait_ge(*g.ms_ready.after(b, 1))
                pow_rstd(c, pool, g.rs[:, :], g.ms[:, :], T).then_inc(g.rs_ready.sem, 1)
                if g.last_round:
                    c.pool_rstd(pool, b)

        @block.scalar
        def _(act):
            def front(b):
                c.act_x_hi(act, b)
                for dst, src in ((g.mc_h, g.m_h), (g.mc_l, g.m_l)):
                    m = act.activation(dst[:, :, :], src[:, :, bass.ds(b, 1), :].rearrange("p k a n -> p (k a) n"),
                                       ACT.Copy)
                m.then_inc(g.m_cur.sem, 1)
                act.wait_ge(*ps.full(b, ("lT", 0)))
                act.activation(g.lTs[:, :], ps.ap(("lT", 0)), ACT.Copy).then_inc(ps.freed(("lT", 0)), 1)

            def back(b, following):
                act.wait_ge(*g.shifted.after(b, 1))
                act.activation(g.att[:, :, :], g.lg[:, :, :], ACT.Exp, scale=W6 ** -0.5).then_inc(g.att_exps.sem, 1)
                act.wait_ge(*ps.full(b, ("aT", 0)))
                act.activation(g.attT[:, :], ps.ap(("aT", 0)), ACT.Copy).then_inc(ps.freed(("aT", 0)), 1)
                act.wait_ge(*g.ms_ready.after(b, 0))
                for t in range(T):
                    act.wait_ge(*g.added.after(b, t + 1))
                    s = act.activation(g.squares[t][:, 0:D], g.xw[:, bass.ds(b * T + t, 1), :].rearrange("p a n -> p (a n)"),
                                       ACT.Square, accum_out=g.ssq[:, t:t + 1])
                s.then_inc(g.ssq_ready.sem, 1)
                if following is not None:
                    following(b + 1)

            pipelined(act, front, back)

        @block.vector
        def _(dve):
            def front(b):
                c.dve_x_lo(dve, b)

            def back(b, following):
                dve.wait_ge(*ps.full(b, ("l", 0)))
                dve.tensor_tensor(g.lg[:, :, :], ps.ap(("l", 0)).rearrange("p (t n) -> p t n", t=T),
                                  g.lb[:, bass.ds(b, 1), :].broadcast_to([P, T, P]), ALU.add).then_inc(ps.freed(("l", 0)), 1)
                dve.drain()
                dve.tensor_reduce(g.mx8[:, :], heads(g.lg[:, :, :]), AX.X, ALU.max)
                dve.drain()
                dve.tensor_tensor(heads(g.lg[:, :, :]), heads(g.lg[:, :, :]),
                                  g.mx8[:, :].unsqueeze(2).broadcast_to([P, T * H6, NS]), ALU.subtract) \
                   .then_inc(g.shifted.sem, 1)
                dve.wait_ge(*g.att_exps.after(b, 1))
                dve.tensor_reduce(g.mx8[:, :], heads(g.att[:, :, :]), AX.X, ALU.add)
                dve.drain()
                dve.reciprocal(g.mx8[:, :], g.mx8[:, :])
                dve.drain()
                dve.tensor_tensor(heads(g.att[:, :, :]), heads(g.att[:, :, :]),
                                  g.mx8[:, :].unsqueeze(2).broadcast_to([P, T * H6, NS]), ALU.mult) \
                   .then_inc(g.att_ready.sem, 1)
                for t in range(T):
                    xt = g.xw[:, b * T + t, :]
                    dve.wait_ge(*ps.full(b, ("y", t)))
                    dve.tensor_tensor(xt, ps.ap(("y", t)), g.src[:, b * T + t, :], ALU.add).then_inc(ps.freed(("y", t)), 1)
                    dve.drain()
                    dve.tensor_tensor(xt, xt, g.ob[:, :], ALU.add).then_inc(g.added.sem, 1)
                if following is not None:
                    following(b + 1)
                dve.wait_ge(*g.ssq_ready.after(b, 1))
                dve.tensor_scalar(g.ms[:, :], g.ssq[:, :], 1.0 / D, EPS6, ALU.mult, ALU.add).then_inc(g.ms_ready.sem, 1)
                dve.wait_ge(*g.rs_ready.after(b, 1))
                for t in range(T):
                    xt = g.xw[:, b * T + t, :]
                    dve.scalar_tensor_tensor(xt, xt, g.rs[:, t:t + 1], g.post[:, :], ALU.mult, ALU.mult)
                if g.last_round:
                    dve.drain()
                    for t in range(T):
                        dve.tensor_tensor(c.x[:, b * T + t, :], c.x[:, b * T + t, :], g.xw[:, b * T + t, :], ALU.add)
                    dve.drain()
                    for t in range(T):
                        dve.bn_stats(c.stats[:, t, :], c.x[:, b * T + t, :])
                    c.dve_normalize(dve, b)

            pipelined(dve, front, back)

        @block.tensor
        def _(pe):
            def front(b):
                c.pe_turn_x(pe, b)
                c.wait_xT(pe, b)
                ps.wait_empty(pe, b, ("lT", 0))
                pe.wait_ge(*g.m_cur.after(b, 1))
                for k in range(KD):
                    mm = split3(pe, ps.ap(("lT", 0)), (g.mc_h[:, k, :], g.mc_l[:, k, :]), (c.xhi[:, k, :], c.xlo[:, k, :]),
                                k == 0, k == KD - 1)
                mm.then_inc(ps.filled(("lT", 0)), 1)
                ps.wait_empty(pe, b, ("l", 0))
                for t in range(T):
                    mm = pe.transpose(ps.ap(("l", 0))[:, t * P:(t + 1) * P], g.lTs[:, t * P:(t + 1) * P], c.ident[:, :])
                mm.then_inc(ps.filled(("l", 0)), 1)

            def back(b, following):
                pe.wait_ge(*g.att_ready.after(b, 1))
                ps.wait_empty(pe, b, ("aT", 0))
                for t in range(T):
                    mm = pe.transpose(ps.ap(("aT", 0))[:, t * P:(t + 1) * P], g.att[:, t, :], c.ident[:, :])
                mm.then_inc(ps.filled(("aT", 0)), 1)
                pe.wait_ge(*ps.released(b, ("aT", 0)))
                for t in range(T):
                    ps.wait_empty(pe, b, ("y", t))
                    pe.matmul(ps.ap(("y", t)), g.attT[:, t * P:(t + 1) * P],
                              g.u[:, bass.ds(b, 1), :].rearrange("p a n -> p (a n)"), start=True, stop=True) \
                      .then_inc(ps.filled(("y", t)), 1)
                if following is not None:
                    following(b + 1)

            pipelined(pe, front, back)

    ps.close(B)
    for x in (c.cur, c.xT_hi, g.ssq_ready, g.ms_ready, g.rs_ready, g.shifted, g.att_exps, g.att_ready, g.added, g.m_cur):
        x.close(B)
    if g.last_round:
        c.var_ready.close(B)
        c.rstd_ready.close(B)


def store_x(c, out):
    with ExitStack() as ctx:
        stored = c.sem("out_stored")
        block = ctx.enter_context(c.nc.Block())

        @block.sync
        def _(sp):
            for b in range(B):
                sp.dma_start(out[b].rearrange("(t p) d -> p t d", p=P), c.x[:, b * T:(b + 1) * T, :]).then_inc(stored, 16)
            sp.wait_ge(stored, 16 * B)


STAGES = [rope_attention, similarity_mixing, lora_experts, window_attention, cross_attention, workspace_rounds]


def build(nc, d, out, stages=STAGES):
    with ExitStack() as ctx:
        c = Core(nc, ctx, d)
        with ExitStack() as s:
            c.start(s)
        for stage in stages:
            stage(c)
        store_x(c, out)


def rope_tables(s, hd, scale):
    half = hd // 2
    freqs = np.float32(1.0) / np.float32(10000.0) ** (np.arange(half, dtype=np.float32) / np.float32(half))
    angles = np.arange(s, dtype=np.float32)[:, None] * freqs[None, :]
    cos, sin = np.cos(angles) * np.float32(scale), np.sin(angles) * np.float32(scale)
    out = np.zeros((s, 2, hd), np.float32)
    out[:, 0, 0::2], out[:, 0, 1::2] = cos, cos
    out[:, 1, 0::2], out[:, 1, 1::2] = -sin, sin
    return out


def window_mask():
    k, q = np.arange(P)[:, None], np.arange(P)[None, :]
    own = np.where((k <= q) & (q - k <= WIN), 0.0, NEG)
    nxt = np.where(q + P - k <= WIN, 0.0, NEG)
    return np.concatenate([own, nxt, own, nxt], 1).astype(np.float32)


def layout(i):
    def f(a):
        return np.ascontiguousarray(a)

    def row(a):
        return f(a.reshape(1, -1))

    def column(a):
        return f(a.reshape(-1, 1))

    def columns(a):
        return f(a.reshape(-1, P).T)

    w, ib = i['L1_ffn_in_proj_w'], i['L1_ffn_in_proj_b']
    return {
        'x': f(i['x']), 'ident': np.eye(P, dtype=np.float32),
        'cos_sin': rope_tables(S, HD, HD ** -0.25), 'cos_sin_plain': rope_tables(S, HD, 1.0),
        'window_mask': window_mask(),
        'l0a_wqkv': f(np.concatenate([i['L0_attn_W_q'], i['L0_attn_W_k'], i['L0_attn_W_v']], 1)),
        'l0a_wo': f(i['L0_attn_W_o']),
        'ctxT': f(i['ctx_1024'].transpose(0, 2, 1)),
        'l0x_wqT': f(i['L0_xattn_Wq'].T), 'l0x_bq': column(i['L0_xattn_bq']),
        'l0x_wkT': f(i['L0_xattn_Wk'].T), 'l0x_bk': column(i['L0_xattn_bk']),
        'l0f_wT': f(i['L0_ffn_weight'].T),
        'l0f_agT': f(np.concatenate([i['L0_ffn_A_w'].reshape(LORA, D), i['L0_ffn_gate_w']], 0).T),
        'l0f_bT': f(i['L0_ffn_B_w'].transpose(0, 2, 1).reshape(LORA, D)),
        'l1a_wqkvT': f(np.concatenate([i['L1_attn_Wq'], i['L1_attn_Wk'], i['L1_attn_Wv']], 0).T),
        'l1a_bqkv': row(np.concatenate([i['L1_attn_bq'], i['L1_attn_bk'], i['L1_attn_bv']])),
        'l1a_woT': f(i['L1_attn_Wo'].T), 'l1a_bo': row(i['L1_attn_bo']),
        'l1a_qn': row(i['L1_attn_qn_w']), 'l1a_kn': row(i['L1_attn_kn_w']),
        'l1a_scale': f(i['L1_attn_scale'].reshape(1, 1)),
        'l1x_wq': f(i['L1_xattn_Wq']), 'l1x_wk': f(i['L1_xattn_Wk']), 'l1x_wv': f(i['L1_xattn_Wv']),
        'l1x_wo': f(i['L1_xattn_Wo']), 'l1x_gq': row(i['L1_xattn_gq']), 'l1x_gk': row(i['L1_xattn_gk']),
        'l1f_ws': f(i['L1_ffn_workspace']), 'l1f_cwT': f(i['L1_ffn_compete_w'].T),
        'l1f_cb': column(i['L1_ffn_compete_b']),
        'l1f_wwT': f(i['L1_ffn_write_w'].T), 'l1f_wb': row(i['L1_ffn_write_b']),
        'l1f_wq': f(w[0:D]), 'l1f_wkT': f(w[D:2 * D].T), 'l1f_wvT': f(w[2 * D:].T),
        'l1f_bq': columns(ib[0:D]), 'l1f_bk': columns(ib[D:2 * D]), 'l1f_bv': columns(ib[2 * D:]),
        'l1f_woT': f(i['L1_ffn_out_proj_w'].T), 'l1f_ob': row(i['L1_ffn_out_proj_b']),
        'l1f_pre': columns(i['L1_ffn_norm_pre_w']), 'l1f_post': row(i['L1_ffn_norm_post_w']),
    }


def kernel(**inputs):
    import concourse.bacc as bacc
    from concourse.bass_utils import run_bass_kernel_spmd

    arrays = layout({name: np.asarray(a) for name, a in inputs.items()})
    nc = bacc.Bacc("TRN2", target_bir_lowering=False, num_devices=1)
    d = {name: nc.dram_tensor(name, a.shape, mybir.dt.from_np(a.dtype), kind="ExternalInput").ap()
         for name, a in arrays.items()}
    out = nc.dram_tensor("out", (B, S, D), F32, kind="ExternalOutput").ap()
    build(nc, d, out)
    return run_bass_kernel_spmd(nc, [arrays], core_ids=[0]).results[0]["out"]
```
